# Optimizing a Trainium2 kernel written in Bass

```python
import numpy as np
import jax
import jax.numpy as jnp

def _softmax(x, axis=-1):
    return jax.nn.softmax(x, axis=axis)

def _gelu(x):
    return jax.nn.gelu(x, approximate=True)

def _silu(x):
    return jax.nn.silu(x)

def _sigmoid(x):
    return jax.nn.sigmoid(x)

def _layernorm(x, axis=-1, eps=1e-05):
    m = jnp.mean(x, axis=axis, keepdims=True)
    v = jnp.var(x, axis=axis, keepdims=True)
    return (x - m) / jnp.sqrt(v + eps)

def _scatter_add(tgt, idx, src, axis=0):
    return tgt.at[idx].add(src)

def _segment_sum(src, seg, n):
    return jax.ops.segment_sum(src, seg, n)
kernel_name = 'mk_sandwich_d2_jaxref_r4_3179f4'

def setup_inputs(seed: int=0):
    np.random.seed(seed)
    _w = jnp.asarray

    def _L0_attn_setup():
        import jax, jax.numpy as jnp
        import numpy as np
        DEPTH, DIM, DFF, VOCAB = (4, 128, 512, 1024)
        EPS = 1e-05

        def layernorm(x, w, b):
            mu = jnp.mean(x, axis=-1, keepdims=True)
            var = jnp.mean((x - mu) ** 2, axis=-1, keepdims=True)
            return (x - mu) * jax.lax.rsqrt(var + EPS) * w + b

        def sconv(x, phazor_c, last_conv_c):
            B, L, D = x.shape
            r = jnp.abs(phazor_c)
            p = jnp.tanh(r) * jnp.exp(1j * jnp.angle(phazor_c))
            prog = p[None, :] ** jnp.arange(L, dtype=jnp.float32)[:, None]
            filt_fft = jnp.fft.fft(prog, n=2 * L, axis=0)
            x_fft = jnp.fft.fft(x.astype(jnp.complex64), n=2 * L, axis=1)
            conv = jnp.fft.ifft(filt_fft[None] * x_fft, axis=1)[:, :L]
            conv = conv + last_conv_c[None, None, :] * prog[None] * p[None, None, :]
            return conv.real.astype(x.dtype)

        def _forward(x, Win, bin, ln1_w, ln1_b, phz_re, phz_im, lc_re, lc_im, sc_lin, ln2_w, ln2_b, W1, b1, W2, b2, lnl_w, lnl_b, Wout, bout):
            h = jnp.einsum('blv,dv->bld', x, Win) + bin

            def body(h, p):
                l1w, l1b, pr, pi, lr, li, scl, l2w, l2b, w1, b1_, w2, b2_ = p
                y = jax.nn.silu(layernorm(h, l1w, l1b))
                y = sconv(y, pr + 1j * pi, lr + 1j * li)
                h = h + y * scl
                y = layernorm(h, l2w, l2b)
                y = jax.nn.silu(jnp.einsum('bld,fd->blf', y, w1) + b1_)
                y = jnp.einsum('blf,df->bld', y, w2) + b2_
                return (h + y, None)
            xs = (ln1_w, ln1_b, phz_re, phz_im, lc_re, lc_im, sc_lin, ln2_w, ln2_b, W1, b1, W2, b2)
            h, _ = jax.lax.scan(body, h, xs)
            h = layernorm(h, lnl_w, lnl_b)
            return jnp.einsum('bld,vd->blv', h, Wout) + bout
        key = jax.random.key(seed)
        ks = jax.random.split(key, 20)
        f32 = jnp.float32
        inp = {}
        inp['x'] = jax.random.normal(ks[0], (2, 1024, VOCAB), dtype=f32)
        inp['Win'] = jax.random.normal(ks[1], (DIM, VOCAB), dtype=f32) * VOCAB ** (-0.5)
        inp['bin'] = jnp.zeros((DIM,), f32)
        inp['ln1_w'] = jnp.ones((DEPTH, DIM), f32)
        inp['ln1_b'] = jnp.zeros((DEPTH, DIM), f32)
        ang = 2 * np.pi * jnp.arange(DIM, dtype=f32) / DIM
        mag = jnp.abs(jax.random.normal(ks[2], (DEPTH, DIM), dtype=f32))
        inp['phz_re'] = mag * jnp.cos(ang)[None]
        inp['phz_im'] = mag * jnp.sin(ang)[None]
        inp['lc_re'] = jax.random.normal(ks[3], (DEPTH, DIM), dtype=f32)
        inp['lc_im'] = jax.random.normal(ks[4], (DEPTH, DIM), dtype=f32)
        inp['sc_lin'] = jnp.ones((DEPTH, DIM), f32)
        inp['ln2_w'] = jnp.ones((DEPTH, DIM), f32)
        inp['ln2_b'] = jnp.zeros((DEPTH, DIM), f32)
        inp['W1'] = jax.random.normal(ks[5], (DEPTH, DFF, DIM), dtype=f32) * DIM ** (-0.5)
        inp['b1'] = jnp.zeros((DEPTH, DFF), f32)
        inp['W2'] = jax.random.normal(ks[6], (DEPTH, DIM, DFF), dtype=f32) * DFF ** (-0.5)
        inp['b2'] = jnp.zeros((DEPTH, DIM), f32)
        inp['lnl_w'] = jnp.ones((DIM,), f32)
        inp['lnl_b'] = jnp.zeros((DIM,), f32)
        inp['Wout'] = jax.random.normal(ks[7], (VOCAB, DIM), dtype=f32) * DIM ** (-0.5)
        inp['bout'] = jnp.zeros((VOCAB,), f32)
        return inp
    _L0_attn_in = _L0_attn_setup()

    def _L0_ffn_setup():
        import jax, jax.numpy as jnp
        import numpy as np
        LORA_SCALING = 1.0 / 2.0

        def _qlora_linear(x, wq, A, B):
            w = jnp.tile(wq, (1, 4))
            base = x @ w.T
            lora = x @ A.T @ B.T
            return base + lora * LORA_SCALING
        key = jax.random.key(seed)
        ks = jax.random.split(key, 10)
        d, h, r = (1024, 2752, 2)
        return {'x': jax.random.normal(ks[0], (16, 1, d), dtype=jnp.float32), 'w1q': jax.random.normal(ks[1], (h, d // 4), dtype=jnp.float32) * 0.02, 'a1': jax.random.normal(ks[2], (r, d), dtype=jnp.float32) * 0.02, 'b1': jax.random.normal(ks[3], (h, r), dtype=jnp.float32) * 0.02, 'w3q': jax.random.normal(ks[4], (h, d // 4), dtype=jnp.float32) * 0.02, 'a3': jax.random.normal(ks[5], (r, d), dtype=jnp.float32) * 0.02, 'b3': jax.random.normal(ks[6], (h, r), dtype=jnp.float32) * 0.02, 'w2q': jax.random.normal(ks[7], (d, h // 4), dtype=jnp.float32) * 0.02, 'a2': jax.random.normal(ks[8], (r, h), dtype=jnp.float32) * 0.02, 'b2': jax.random.normal(ks[9], (d, r), dtype=jnp.float32) * 0.02}
    _L0_ffn_in = _L0_ffn_setup()

    def _L1_attn_setup():
        import jax, jax.numpy as jnp
        import numpy as np
        B, T, D = (1, 512, 1024)
        H, G = (32, 8)
        HD = D // H
        REP = H // G
        KV_DIM = 2 * HD * G
        key = jax.random.key(seed)
        k0, k1, k2, k3 = jax.random.split(key, 4)
        x = jax.random.normal(k0, (B, T, D), dtype=jnp.float32)
        Wq = jax.random.normal(k1, (D, D), dtype=jnp.float32) * 0.02
        Wkv = jax.random.normal(k2, (D, KV_DIM), dtype=jnp.float32) * 0.02
        Wo = jax.random.normal(k3, (D, D), dtype=jnp.float32) * 0.02
        bo = jnp.zeros((D,), dtype=jnp.float32)
        return {'x': x, 'Wq': Wq, 'Wkv': Wkv, 'Wo': Wo, 'bo': bo}
    _L1_attn_in = _L1_attn_setup()

    def _L1_ffn_setup():
        import jax, jax.numpy as jnp
        import numpy as np
        import math
        B, S, IN, OUT = (4, 512, 1024, 1024)
        E, R, K = (8, 64, 128)
        SCALE = 64.0 / 64.0
        MULTIPLIER = 1.0
        key = jax.random.key(seed)
        ks = jax.random.split(key, 6)
        return {'x': jax.random.normal(ks[0], (B, S, IN), jnp.float32), 'W_org': jax.random.normal(ks[1], (OUT, IN), jnp.float32) * 0.02, 'lora_down': jax.random.normal(ks[2], (E, IN, R), jnp.float32) * 0.02, 'lora_up': jax.random.normal(ks[3], (E, R, OUT), jnp.float32) * 0.02, 'lora_keys': jax.random.normal(ks[4], (E, K), jnp.float32), 'Wq': jax.random.normal(ks[5], (K, IN), jnp.float32) * 0.02}
    _L1_ffn_in = _L1_ffn_setup()
    _d = {'L0_attn_x': _L0_attn_in['x'], 'L0_attn_Win': _L0_attn_in['Win'], 'L0_attn_bin': _L0_attn_in['bin'], 'L0_attn_ln1_w': _L0_attn_in['ln1_w'], 'L0_attn_ln1_b': _L0_attn_in['ln1_b'], 'L0_attn_phz_re': _L0_attn_in['phz_re'], 'L0_attn_phz_im': _L0_attn_in['phz_im'], 'L0_attn_lc_re': _L0_attn_in['lc_re'], 'L0_attn_lc_im': _L0_attn_in['lc_im'], 'L0_attn_sc_lin': _L0_attn_in['sc_lin'], 'L0_attn_ln2_w': _L0_attn_in['ln2_w'], 'L0_attn_ln2_b': _L0_attn_in['ln2_b'], 'L0_attn_W1': _L0_attn_in['W1'], 'L0_attn_b1': _L0_attn_in['b1'], 'L0_attn_W2': _L0_attn_in['W2'], 'L0_attn_b2': _L0_attn_in['b2'], 'L0_attn_lnl_w': _L0_attn_in['lnl_w'], 'L0_attn_lnl_b': _L0_attn_in['lnl_b'], 'L0_attn_Wout': _L0_attn_in['Wout'], 'L0_attn_bout': _L0_attn_in['bout'], 'L0_ffn_w1q': _L0_ffn_in['w1q'], 'L0_ffn_a1': _L0_ffn_in['a1'], 'L0_ffn_b1': _L0_ffn_in['b1'], 'L0_ffn_w3q': _L0_ffn_in['w3q'], 'L0_ffn_a3': _L0_ffn_in['a3'], 'L0_ffn_b3': _L0_ffn_in['b3'], 'L0_ffn_w2q': _L0_ffn_in['w2q'], 'L0_ffn_a2': _L0_ffn_in['a2'], 'L0_ffn_b2': _L0_ffn_in['b2'], 'L1_attn_Wq': _L1_attn_in['Wq'], 'L1_attn_Wkv': _L1_attn_in['Wkv'], 'L1_attn_Wo': _L1_attn_in['Wo'], 'L1_attn_bo': _L1_attn_in['bo'], 'L1_ffn_W_org': _L1_ffn_in['W_org'], 'L1_ffn_lora_down': _L1_ffn_in['lora_down'], 'L1_ffn_lora_up': _L1_ffn_in['lora_up'], 'L1_ffn_lora_keys': _L1_ffn_in['lora_keys'], 'L1_ffn_Wq': _L1_ffn_in['Wq']}
    _x0 = _d['L0_attn_x']
    _d['L0_attn_x'] = jax.random.normal(jax.random.fold_in(jax.random.key(seed), 1), (2, 1024, 1024), dtype=_x0.dtype)
    del _x0
    return _d

def reference(L0_attn_x, L0_attn_Win, L0_attn_bin, L0_attn_ln1_w, L0_attn_ln1_b, L0_attn_phz_re, L0_attn_phz_im, L0_attn_lc_re, L0_attn_lc_im, L0_attn_sc_lin, L0_attn_ln2_w, L0_attn_ln2_b, L0_attn_W1, L0_attn_b1, L0_attn_W2, L0_attn_b2, L0_attn_lnl_w, L0_attn_lnl_b, L0_attn_Wout, L0_attn_bout, L0_ffn_w1q, L0_ffn_a1, L0_ffn_b1, L0_ffn_w3q, L0_ffn_a3, L0_ffn_b3, L0_ffn_w2q, L0_ffn_a2, L0_ffn_b2, L1_attn_Wq, L1_attn_Wkv, L1_attn_Wo, L1_attn_bo, L1_ffn_W_org, L1_ffn_lora_down, L1_ffn_lora_up, L1_ffn_lora_keys, L1_ffn_Wq):

    def _L0_attn_ref(x, Win, bin, ln1_w, ln1_b, phz_re, phz_im, lc_re, lc_im, sc_lin, ln2_w, ln2_b, W1, b1, W2, b2, lnl_w, lnl_b, Wout, bout):
        import jax, jax.numpy as jnp
        import numpy as np
        DEPTH, DIM, DFF, VOCAB = (4, 128, 512, 1024)
        EPS = 1e-05

        def layernorm(x, w, b):
            mu = jnp.mean(x, axis=-1, keepdims=True)
            var = jnp.mean((x - mu) ** 2, axis=-1, keepdims=True)
            return (x - mu) * jax.lax.rsqrt(var + EPS) * w + b

        def sconv(x, phazor_c, last_conv_c):
            B, L, D = x.shape
            r = jnp.abs(phazor_c)
            p = jnp.tanh(r) * jnp.exp(1j * jnp.angle(phazor_c))
            prog = p[None, :] ** jnp.arange(L, dtype=jnp.float32)[:, None]
            filt_fft = jnp.fft.fft(prog, n=2 * L, axis=0)
            x_fft = jnp.fft.fft(x.astype(jnp.complex64), n=2 * L, axis=1)
            conv = jnp.fft.ifft(filt_fft[None] * x_fft, axis=1)[:, :L]
            conv = conv + last_conv_c[None, None, :] * prog[None] * p[None, None, :]
            return conv.real.astype(x.dtype)

        def _forward(x, Win, bin, ln1_w, ln1_b, phz_re, phz_im, lc_re, lc_im, sc_lin, ln2_w, ln2_b, W1, b1, W2, b2, lnl_w, lnl_b, Wout, bout):
            h = jnp.einsum('blv,dv->bld', x, Win) + bin

            def body(h, p):
                l1w, l1b, pr, pi, lr, li, scl, l2w, l2b, w1, b1_, w2, b2_ = p
                y = jax.nn.silu(layernorm(h, l1w, l1b))
                y = sconv(y, pr + 1j * pi, lr + 1j * li)
                h = h + y * scl
                y = layernorm(h, l2w, l2b)
                y = jax.nn.silu(jnp.einsum('bld,fd->blf', y, w1) + b1_)
                y = jnp.einsum('blf,df->bld', y, w2) + b2_
                return (h + y, None)
            xs = (ln1_w, ln1_b, phz_re, phz_im, lc_re, lc_im, sc_lin, ln2_w, ln2_b, W1, b1, W2, b2)
            h, _ = jax.lax.scan(body, h, xs)
            h = layernorm(h, lnl_w, lnl_b)
            return jnp.einsum('bld,vd->blv', h, Wout) + bout
        return _forward(x, Win, bin, ln1_w, ln1_b, phz_re, phz_im, lc_re, lc_im, sc_lin, ln2_w, ln2_b, W1, b1, W2, b2, lnl_w, lnl_b, Wout, bout)

    def _L0_ffn_ref(x, w1q, a1, b1, w3q, a3, b3, w2q, a2, b2):
        import jax, jax.numpy as jnp
        import numpy as np
        LORA_SCALING = 1.0 / 2.0

        def _qlora_linear(x, wq, A, B):
            w = jnp.tile(wq, (1, 4))
            base = x @ w.T
            lora = x @ A.T @ B.T
            return base + lora * LORA_SCALING
        gate = jax.nn.silu(_qlora_linear(x, w1q, a1, b1))
        up = _qlora_linear(x, w3q, a3, b3)
        return _qlora_linear(gate * up, w2q, a2, b2)

    def _L1_attn_ref(x, Wq, Wkv, Wo, bo):
        import jax, jax.numpy as jnp
        import numpy as np
        B, T, D = (1, 512, 1024)
        H, G = (32, 8)
        HD = D // H
        REP = H // G
        KV_DIM = 2 * HD * G
        b, t, d = x.shape
        q = jnp.dot(x, Wq).reshape(b, t, H, HD).transpose(0, 2, 1, 3)
        kv = jnp.dot(x, Wkv).reshape(b, t, G, 2, HD).transpose(2, 3, 0, 1, 4)
        k, v = (kv[:, 0], kv[:, 1])
        k = jnp.broadcast_to(k[:, :, None], (G, b, REP, t, HD)).reshape(b, H, t, HD)
        v = jnp.broadcast_to(v[:, :, None], (G, b, REP, t, HD)).reshape(b, H, t, HD)
        scores = jnp.einsum('bhqd,bhkd->bhqk', q, k)
        causal = jnp.triu(jnp.ones((t, t), dtype=bool), 1)
        scores = jnp.where(causal[None, None], -jnp.inf, scores)
        weights = jax.nn.softmax(scores * (1.0 / HD ** 0.5), axis=-1)
        ctx = jnp.einsum('bhqk,bhkd->bhqd', weights, v)
        ctx = ctx.transpose(0, 2, 1, 3).reshape(b, t, d)
        return jnp.dot(ctx, Wo) + bo

    def _L1_ffn_ref(x, W_org, lora_down, lora_up, lora_keys, Wq):
        import jax, jax.numpy as jnp
        import numpy as np
        import math
        B, S, IN, OUT = (4, 512, 1024, 1024)
        E, R, K = (8, 64, 128)
        SCALE = 64.0 / 64.0
        MULTIPLIER = 1.0
        base = jnp.einsum('bsi,oi->bso', x, W_org)
        q = jnp.einsum('bi,ki->bk', x.mean(axis=1), Wq)
        scores = jnp.einsum('bk,ek->be', q, lora_keys) / math.sqrt(K)
        coeffs = jax.nn.softmax(scores, axis=-1)
        h = jnp.einsum('bsi,eir->bser', x, lora_down)
        delta = jnp.einsum('be,bser,ero->bso', coeffs, h, lora_up)
        return base + delta * (SCALE * MULTIPLIER)
    x = L0_attn_x
    x = x + _layernorm(_L0_attn_ref(_layernorm(x, axis=-1), L0_attn_Win, L0_attn_bin, L0_attn_ln1_w, L0_attn_ln1_b, L0_attn_phz_re, L0_attn_phz_im, L0_attn_lc_re, L0_attn_lc_im, L0_attn_sc_lin, L0_attn_ln2_w, L0_attn_ln2_b, L0_attn_W1, L0_attn_b1, L0_attn_W2, L0_attn_b2, L0_attn_lnl_w, L0_attn_lnl_b, L0_attn_Wout, L0_attn_bout), axis=-1)
    x = x + _layernorm(_L0_ffn_ref(_layernorm(x, axis=-1), L0_ffn_w1q, L0_ffn_a1, L0_ffn_b1, L0_ffn_w3q, L0_ffn_a3, L0_ffn_b3, L0_ffn_w2q, L0_ffn_a2, L0_ffn_b2), axis=-1)
    x = x + _layernorm(_L1_attn_ref(_layernorm(x, axis=-1), L1_attn_Wq, L1_attn_Wkv, L1_attn_Wo, L1_attn_bo), axis=-1)
    x = x + _layernorm(_L1_ffn_ref(_layernorm(x, axis=-1), L1_ffn_W_org, L1_ffn_lora_down, L1_ffn_lora_up, L1_ffn_lora_keys, L1_ffn_Wq), axis=-1)
    return x

_drawn_inputs = setup_inputs


def setup_inputs(seed=0):
    import zlib

    import numpy as np

    out = dict(_drawn_inputs(seed))
    spreads = {'L0_attn_bin': (0.0, 0.1),
     'L0_attn_ln1_w': (1.0, 0.2),
     'L0_attn_ln1_b': (0.0, 0.1),
     'L0_attn_sc_lin': (1.0, 0.2),
     'L0_attn_ln2_w': (1.0, 0.2),
     'L0_attn_ln2_b': (0.0, 0.1),
     'L0_attn_b1': (0.0, 0.1),
     'L0_attn_b2': (0.0, 0.1),
     'L0_attn_lnl_w': (1.0, 0.2),
     'L0_attn_lnl_b': (0.0, 0.1),
     'L0_attn_bout': (0.0, 0.1),
     'L1_attn_bo': (0.0, 0.1)}
    factors = {'L0_attn_lc_im': 2.768,
     'L0_ffn_a1': 7.163,
     'L0_ffn_b1': 8.0,
     'L0_ffn_a3': 7.148,
     'L0_ffn_b3': 7.412,
     'L0_ffn_a2': 7.859,
     'L0_ffn_b2': 8.0,
     'L1_ffn_lora_keys': 8.0,
     'L1_ffn_Wq': 8.0}
    for name, (base, spread) in spreads.items():
        noise = np.random.default_rng([zlib.crc32(name.encode()), seed]).standard_normal(out[name].shape)
        drawn = base * np.exp(spread * noise) if base else spread * noise
        out[name] = jnp.asarray(drawn.astype(out[name].dtype))
    for name, factor in factors.items():
        out[name] = (out[name] * factor).astype(out[name].dtype)
    return out
```

```python
from contextlib import ExitStack

import numpy as np
import concourse.bass as bass
from concourse import mybir

F32 = mybir.dt.float32
F32R = mybir.dt.float32r
ACT = mybir.ActivationFunctionType
ALU = mybir.AluOpType
AX = mybir.AxisListType.X

STAGES = "ABCD"
NT = 16
D = 1024
EPS = 1e-5
FH = 2752
VECS = {}
_at = 0
for _n, _w in (("bin", 1), ("ln1w", 4), ("ln1b", 4), ("pre", 4), ("pim", 4), ("lre", 4), ("lim", 4),
               ("scl", 4), ("ln2w", 4), ("ln2b", 4), ("b1", 16), ("b2", 4), ("lnlw", 1), ("lnlb", 1)):
    VECS[_n] = _at
    _at += _w
NVEC = _at


class Prog:

    def __init__(self, nc, ctx):
        self.nc = nc
        self.ctx = ctx
        self.q = {e: [] for e in ("pe", "act", "dve", "pool", "sp")}
        self.sem = {e: ctx.enter_context(nc.semaphore("s_" + e)) for e in ("pe", "act", "dve", "pool")}
        self.n = {e: 0 for e in self.sem}
        self.seen = {e: {} for e in self.q}

    def wait(self, e, waits):
        for w in flat(waits):
            k, v = w
            if self.seen[e].get(k, 0) < v:
                self.seen[e][k] = v
                self.q[e].append(("w", self.sem[k], v))

    def op(self, e, fn, waits=(), inc=True):
        self.wait(e, waits)
        if inc:
            self.n[e] += 1
            self.q[e].append(("i", fn, self.sem[e], 1))
            return (e, self.n[e])
        self.q[e].append(("i", fn, None, 0))
        return None

    def last(self, e):
        return (e, self.n[e])

    def dma(self, ch, out, in_, waits=()):
        k = ch.names[ch.i % len(ch.names)]
        ch.i += 1
        self.wait("sp", [(k, self.n[k])] if self.n[k] else [])
        self.wait("sp", waits)
        self.n[k] += 16
        self.q["sp"].append(("i", lambda: self.nc.sync.dma_start(out, in_), self.sem[k], 16))
        return (k, self.n[k])

    def channel(self, name, n):
        return Channel(self, name, n)

    def barrier(self):
        toks = [(k, v) for k, v in self.n.items() if v]
        for e in self.q:
            self.wait(e, toks)

    def run(self, block):
        def play(eng, items):
            for it in items:
                if it[0] == "w":
                    eng.wait_ge(it[1], it[2])
                else:
                    ins = it[1]()
                    if it[2] is not None:
                        ins.then_inc(it[2], it[3])

        @block.sync
        def _(e):
            play(e, self.q["sp"])

        @block.tensor
        def _(e):
            play(e, self.q["pe"])

        @block.scalar
        def _(e):
            play(e, self.q["act"])

        @block.vector
        def _(e):
            play(e, self.q["dve"])

        @block.gpsimd
        def _(e):
            play(e, self.q["pool"])


class Channel:
    def __init__(self, p, name, n):
        self.names = [f"{name}{i}" for i in range(n)]
        self.i = 0
        for k in self.names:
            p.sem[k] = p.ctx.enter_context(p.nc.semaphore("s_" + k))
            p.n[k] = 0


def flat(w):
    if w is None:
        return
    if isinstance(w, tuple) and len(w) == 2 and isinstance(w[0], str):
        yield w
        return
    for x in w:
        yield from flat(x)


class Ring:

    def __init__(self, bufs):
        self.bufs = bufs
        self.i = 0
        self.busy = [[] for _ in bufs]

    def get(self):
        i = self.i % len(self.bufs)
        assert self.i < len(self.bufs) or self.busy[i], "its readers aren't known yet"
        self.i += 1
        w, self.busy[i] = self.busy[i], []
        return i, self.bufs[i], w

    def free(self, i, toks):
        self.busy[i].append(toks)


class K:
    def __init__(self, nc, ctx, io, out):
        self.nc, self.io, self.out = nc, io, out
        self.p = Prog(nc, ctx)
        self.PS = ctx.enter_context(nc.psum_tensor("PS", [128, 4096], F32))
        self.cst = ctx.enter_context(nc.sbuf_tensor("cst", [128, 256 + 128 + 128 + 8], F32))
        self.ident = self.cst[:, 0:128]
        self.cmat = self.cst[:, 128:256]
        self.mask = self.cst[:, 256:384]
        self.ones = self.cst[:, 384:512]
        self.onediv = self.cst[:, 512:513]
        self.small = ctx.enter_context(nc.sbuf_tensor("small", [128, 8, 24], F32))
        self.mhalf = ctx.enter_context(nc.sbuf_tensor("mhalf", [128, 16], F32))
        self.ld = self.p.channel("ld", 6)
        self.st = self.p.channel("st", 6)
        self.wl = self.p.channel("wl", 6)
        self.t_c = self.p.dma(self.ld, self.cst[:, :], io["cst"])
        self.t_mh = self.dve(lambda: nc.vector.memset(self.mhalf[:, :], -0.5))
        self.smr = Ring(list(range(8)))
        self.scr = [nc.dram_tensor(f"scr{i}", (NT * 128, D), F32, kind="Internal").ap() for i in range(8)]

    def bank(self, b, n=1):
        return self.PS[:, 512 * b:512 * (b + n)]

    def pe(self, fn, w=(), inc=False):
        return self.p.op("pe", fn, w, inc)

    def act(self, fn, w=()):
        return self.p.op("act", fn, w)

    def dve(self, fn, w=()):
        return self.p.op("dve", fn, w)

    def pool(self, fn, w=()):
        return self.p.op("pool", fn, w)

    def mm(self, out, l, r, start, stop, w=(), inc=False, skip=False):
        nc = self.nc
        if skip:
            return self.pe(lambda: nc.tensor.matmul(out, l, r, start=start, stop=stop, skip_group_check=True), w, inc)
        return self.pe(lambda: nc.tensor.matmul(out, l, r, start=start, stop=stop), w, inc)

    def tr(self, out, in_, w=(), inc=False):
        nc = self.nc
        n = in_.shape[0]
        return self.pe(lambda: nc.tensor.transpose(out, in_, self.ident[0:n, 0:n]), [w, self.t_c], inc)

    def af(self, out, in_, func, w=(), scale=None, bias=None):
        nc = self.nc
        kw = {}
        if scale is not None:
            kw["scale"] = scale
        if bias is not None:
            kw["bias"] = bias
        return self.act(lambda: nc.scalar.activation(out, in_, func, **kw), w)

    def tt(self, out, a, b, op, w=(), e="dve"):
        nc = self.nc
        en = nc.vector if e == "dve" else nc.gpsimd
        return self.p.op(e, lambda: en.tensor_tensor(out, a, b, op), w)

    def ts(self, out, a, s1, s2, op0, op1=None, w=()):
        nc = self.nc
        if op1 is None:
            return self.dve(lambda: nc.vector.tensor_scalar(out, a, s1, None, op0), w)
        return self.dve(lambda: nc.vector.tensor_scalar(out, a, s1, s2, op0, op1), w)

    def stt(self, out, a, s, b, op0, op1, w=()):
        nc = self.nc
        return self.dve(lambda: nc.vector.scalar_tensor_tensor(out=out, in0=a, scalar=s, in1=b, op0=op0, op1=op1), w)

    def copy(self, out, in_, w=(), e="dve"):
        nc = self.nc
        if e == "act":
            return self.act(lambda: nc.scalar.copy(out, in_), w)
        en = nc.vector if e == "dve" else nc.gpsimd
        return self.p.op(e, lambda: en.tensor_copy(out, in_), w)

    def split(self, h, l, src, w=(), e="act"):
        a = self.copy(h, src, w, e)
        b = self.tt(l, src, h.bitcast(F32), ALU.subtract, [w, a])
        return [a, b]

    def load_split(self, h, l, dram, ring, w=()):
        i, buf, fr = ring.get()
        n, m = h.shape[0], h.shape[-1]
        s = buf[0:n, 0:m]
        t = self.p.dma(self.wl, s, dram, fr)
        r = self.split(h, l, s, [t, w])
        ring.free(i, r)
        return r

    def stats(self, src, w):
        nc = self.nc
        i, k, fr = self.smr.get()
        s = self.small[:, k, :]
        a = self.dve(lambda: nc.vector.bn_stats(s[:, 0:6], src[:, 0:512]), [w, fr])
        b = self.dve(lambda: nc.vector.bn_stats(s[:, 6:12], src[:, 512:1024]), w)
        c = self.dve(lambda: nc.vector.bn_aggr(s[:, 12:14], s[:, 0:12]), [a, b])
        d = self.ts(s[:, 14:15], s[:, 13:14], EPS, None, ALU.add, w=[c])
        e = self.tt(s[:, 15:16], s[:, 14:15], self.mhalf[:, 0:1], ALU.pow, [d, self.t_mh], e="pool")
        return {"i": i, "s": s, "mean": c, "rs": e, "st": b}

    def normalize(self, out, src, q, w=()):
        s = q["s"]
        n = self.stt(s[:, 16:17], s[:, 12:13], -1.0, s[:, 15:16], ALU.mult, ALU.mult, [q["rs"], q["mean"]])
        t = self.af(out, src, ACT.Identity, [w, n, q["rs"]], scale=s[:, 15:16], bias=s[:, 16:17])
        self.smr.free(q["i"], t)
        return t

    def tail_steps(self, t, y, ytok, free_y, xring, yring, x_src, x_dst, xn_dst, bias=None, btok=None, hook=None,
                   x_tok=None):
        S = {}
        rows = slice(128 * t, 128 * t + 128)

        def s1():
            S["xi"], S["x"], fr = xring.get()
            S["xl"] = self.p.dma(self.ld, S["x"][:, :], x_src[rows, :], [fr, x_tok])
            S["yi"], S["yn"], S["yf"] = yring.get()
            src, w = y, ytok
            if bias is not None:
                b = self.tt(S["yn"][:, :], y, bias, ALU.add, [ytok, btok, S["yf"]])
                free_y([b])
                src, w = S["yn"][:, :], b
            S["src"] = src
            S["q"] = self.stats(src, w)

        def s2():
            a = self.normalize(S["yn"][:, :], S["src"], S["q"], [S["yf"]])
            if bias is None:
                free_y([a, S["q"]["st"]])
            b = self.tt(S["x"][:, :], S["x"][:, :], S["yn"][:, :], ALU.add, [a, S["xl"]])
            S["b"] = b
            S["xs"] = self.p.dma(self.st, x_dst[rows, :], S["x"][:, :], b)
            S["out"] = [S["xs"]]
            if xn_dst is None:
                xring.free(S["xi"], [S["xs"]])
                yring.free(S["yi"], [b])

        def s3():
            S["q"] = self.stats(S["x"][:, :], S["b"])

        def s4():
            a = self.normalize(S["yn"][:, :], S["x"][:, :], S["q"], [S["b"]])
            c = self.p.dma(self.st, xn_dst[rows, :], S["yn"][:, :], a)
            h = hook(t, S["yn"], a) if hook else None
            xring.free(S["xi"], [S["xs"], a, S["q"]["st"]])
            yring.free(S["yi"], [c, h])
            self.done_xn[t] = c
            self.done_x[t] = S["xs"]

        if xn_dst is None:
            return [s1, s2]
        return [s1, s2, s3, s4]


def pipeline(items, lags=None):
    n = len(items)
    k = max(len(x) for x in items)
    for i in range(n + k):
        for s in reversed(range(k)):
            j = i - s
            if 0 <= j < n and s < len(items[j]):
                items[j][s]()


def stage_a(k, x_src, x_dst, xn_dst):
    nc, p, io = k.nc, k.p, k.io
    with ExitStack() as ctx:
        def sb(name, shape, dt=F32):
            return ctx.enter_context(nc.sbuf_tensor("a_" + name, shape, dt))

        win_h, win_l = sb("winh", [128, 8, 128], F32R), sb("winl", [128, 8, 128], F32R)
        h = sb("h", [128, 2048])
        vec = sb("vec", [128, NVEC])
        w1 = sb("w1", [128, 4, 512])
        w2 = sb("w2", [128, 4, 4, 128])
        wout = sb("wout", [128, 1024])
        bout = sb("bout", [128, 1024])
        cosT, sinT = sb("cosT", [128, 4, 1024]), sb("sinT", [128, 4, 1024])
        sm = sb("sm", [128, 20, 4])
        stg = Ring([sb(f"stg{i}", [128, 1024]) for i in range(2)])

        t_vec = p.dma(k.wl, vec[:, :], io["vecs"])
        i, buf, fr = stg.get()
        t = p.dma(k.wl, buf[:, :].rearrange("p (c n) -> p c n", c=8), io["winT"].rearrange("(c p) n -> p c n", p=128))
        t_win = k.split(win_h[:, :, :], win_l[:, :, :], buf[:, :].rearrange("p (c n) -> p c n", c=8), t)

        def V(name, i=0):
            c = VECS[name] + i
            return vec[:, c:c + 1]

        def V4(name):
            return vec[:, VECS[name]:VECS[name] + 4]

        r2, t0, z0, rinv, r, rho, c0, s0, i1, i2, t1, t2 = (sm[:, n, :] for n in range(12))
        M, A_, S_ = ALU.mult, ALU.add, ALU.subtract
        a = k.tt(r2, V4("pre"), V4("pre"), M, t_vec)
        b = k.tt(t0, V4("pim"), V4("pim"), M, t_vec)
        a = k.tt(r2, r2, t0, A_, [a, b])
        z = k.ts(z0, r2, 0.0, None, ALU.is_equal, w=a)
        b = k.ts(t0, r2, 1e-37, None, ALU.max, w=a)
        rv = k.tt(rinv, t0, k.mhalf[:, 0:4], ALU.pow, [b, k.t_mh], e="pool")
        a = k.tt(r, r2, rinv, M, [rv, a])
        t_rho = k.af(rho, r, ACT.Tanh, a)
        a = k.tt(t1, V4("pre"), rinv, M, rv)
        c_ = k.tt(c0, t1, z0, A_, [a, z])
        s_ = k.tt(s0, V4("pim"), rinv, M, rv)
        a = k.tt(t1, c0, V4("lre"), M, [c_])
        b = k.tt(t2, s0, V4("lim"), M, s_)
        t_i1 = k.tt(i1, t1, t2, S_, [a, b])
        a = k.tt(t1, s0, V4("lre"), M, [t_i1])
        b = k.tt(t2, c0, V4("lim"), M, t_i1)
        a = k.tt(t1, t1, t2, A_, [a, b])
        t_i2 = k.ts(i2, t1, -1.0, None, M, w=a)

        tmp = sb("tmp", [128, 2, 512])
        e = [sm[:, 12 + n, :] for n in range(4)]
        first = [k.dve(lambda: nc.vector.memset(cosT[:, :, 0:1], 1.0)), k.dve(lambda: nc.vector.memset(sinT[:, :, 0:1], 0.0))]
        tabs = {}

        def table(level):
            n = 1 << level
            cn, sn = (c0, s0) if level == 0 else (e[0], e[1])
            w = [tabs.get("e"), tabs.get("t"), first, c_, s_]
            last = []
            for l in range(4):
                u = k.af(tmp[:, 0, 0:n], sinT[:, l, 0:n], ACT.Copy, [w, tabs.get("u")], scale=sn[:, l:l + 1])
                v = k.af(tmp[:, 1, 0:n], cosT[:, l, 0:n], ACT.Copy, [w, tabs.get("u")], scale=sn[:, l:l + 1])
                a = k.stt(cosT[:, l, n:2 * n], cosT[:, l, 0:n], cn[:, l:l + 1], tmp[:, 0, 0:n], M, S_, [u, w])
                b = k.stt(sinT[:, l, n:2 * n], sinT[:, l, 0:n], cn[:, l:l + 1], tmp[:, 1, 0:n], M, A_, [v, w])
                tabs["u"] = [a, b]
                last += [a, b]
            tabs["t"] = last
            if level < 9:
                a = k.tt(e[2], cn, cn, M, [w, last])
                b = k.tt(e[3], sn, sn, M, [w, last])
                c = k.tt(t2, cn, sn, M, [w, last, t_i2])
                d = k.tt(e[0], e[2], e[3], S_, [a, b, c])
                f = k.ts(e[1], t2, 2.0, None, M, w=[c, b])
                tabs["e"] = [d, f]

        xin = Ring([sb(f"xin{i}", [128, 1024]) for i in range(3)])
        xT_ring = Ring([(sb(f"xth{i}", [128, 8, 512], F32R), sb(f"xtl{i}", [128, 8, 512], F32R)) for i in range(1)])
        trb = Ring([0, 2])
        hb = Ring([4, 5])
        G = {}
        h_tok = [[], []]

        def a0(t):
            S = {}

            def s0_():
                S["i"], S["x"], fr = xin.get()
                ld = p.dma(k.ld, S["x"][:, :], x_src[128 * t:128 * t + 128, :], fr)
                S["q"] = k.stats(S["x"][:, :], ld)
                if t < 10:
                    table(t)

            def s1_():
                a = k.normalize(S["x"][:, :], S["x"][:, :], S["q"], [S["q"]["st"]])
                bi, b, fr = trb.get()
                for c in range(8):
                    m = k.tr(k.PS[:, 512 * b + 128 * c:512 * b + 128 * c + 128], S["x"][:, 128 * c:128 * c + 128],
                             [a, fr], inc=c % 4 == 3)
                xin.free(S["i"], m)
                if t % 4 == 0:
                    G["i"], G["b"], G["f"] = xT_ring.get()
                    G["w"] = []
                xh, xl = G["b"]
                cols = slice(128 * (t % 4), 128 * (t % 4) + 128)
                w = k.split(xh[:, :, cols], xl[:, :, cols], k.bank(b, 2).rearrange("p (c n) -> p c n", c=8), [m, G["f"]])
                trb.free(bi, w)
                G["w"] = [G["w"], w]

            def s2_():
                if t % 4 != 3:
                    return
                g = t // 4
                xh, xl = G["b"]
                hi, b, fr = hb.get()
                o = k.bank(b)
                for c in range(8):
                    k.mm(o, win_h[:, c, :], xh[:, c, :], c == 0, False, [G["w"], fr, t_win])
                    k.mm(o, win_h[:, c, :], xl[:, c, :], False, False)
                    m = k.mm(o, win_l[:, c, :], xh[:, c, :], False, c == 7, inc=c == 7)
                xT_ring.free(G["i"], m)
                r = k.af(h[:, 512 * g:512 * g + 512], o, ACT.Identity, [m, t_vec], bias=V("bin"))
                hb.free(hi, r)
                h_tok[g // 2].append(r)
            return [s0_, s1_, s2_]

        pipeline_a0 = [a0(t) for t in range(NT)]
        for i in range(NT + 1):
            if i < NT:
                pipeline_a0[i][0]()
            if i >= 1:
                pipeline_a0[i - 1][1]()
                pipeline_a0[i - 1][2]()

        t_w1 = p.dma(k.wl, w1[:, :, :], io["w1T"].rearrange("l p n -> p l n"))
        t_w2 = [p.dma(k.wl, w2[:, l, :, :], io["w2T"][l].rearrange("(c p) n -> p c n", p=128)) for l in range(4)]
        t_wo = p.dma(k.wl, wout[:, :], io["woutT"])
        t_bo = p.dma(k.wl, bout[:, :], io["bout"].partition_broadcast(128))

        W = [{n: sb(f"{n}{b}", [128, 1024]) for n in ("sq", "cs", "y", "a1")} for b in range(2)]
        hid = [sb(f"hid{b}", [128, 4, 1024]) for b in range(2)]
        vs = sb("vs", [128, 2, 16])
        T = [{"h": h_tok[b], "bank": [k.p.last("act"), k.p.last("dve")], "y": None} for b in range(2)]

        def ln_steps(b, wv, bv, func):
            X, w = T[b], W[b]
            B0 = 4 * b
            hc = h[:, 1024 * b:1024 * b + 1024]

            def n0():
                for s in range(2):
                    m = k.mm(k.bank(B0 + s), k.cmat, hc[:, 512 * s:512 * s + 512], True, True,
                             [X["h"], X["bank"], k.t_c], inc=s == 1)
                X["sq"] = k.af(w["sq"][:, :], k.bank(B0, 2), ACT.Square, [m, X.get("sqf")])
                X["cs"] = k.copy(w["cs"][:, :], k.bank(B0, 2), [m, X.get("csf")], e="act")

            def n1():
                for t in range(8):
                    m = k.mm(k.PS[:, 512 * B0 + t:512 * B0 + t + 1], w["sq"][:, 128 * t:128 * t + 128], k.onediv,
                             True, True, [X["sq"], X["cs"]], inc=t == 7)
                X["sqf"] = m
                a = k.ts(vs[:, b, 0:8], k.PS[:, 512 * B0:512 * B0 + 8], EPS, None, ALU.add, w=m)
                X["rs"] = k.tt(vs[:, b, 8:16], vs[:, b, 0:8], k.mhalf[:, 0:8], ALU.pow, [a, k.t_mh, X.get("rsf")], e="pool")

            def n2():
                for t in range(8):
                    o = 512 * (B0 + 2) + 128 * t
                    m = k.mm(k.PS[:, o:o + 128], vs[:, b, 8 + t:9 + t].broadcast_to([128, 128]), k.ident,
                             True, True, [X["rs"]], inc=t == 7)
                X["rsf"] = m
                X["tt"] = k.tt(w["cs"][:, :], w["cs"][:, :], k.bank(B0 + 2, 2), M, [m, X["cs"]])
                X["bank"] = [X["tt"]]

            def n3():
                X["y"] = k.af(w["y"][:, :], w["cs"][:, :], func, [X["tt"], X.get("yf"), t_vec], scale=wv, bias=bv)
                X["csf"] = X["y"]
            return [n0, n1, n2, n3]

        def conv_steps(b, l):
            X, w = T[b], W[b]
            hc = h[:, 1024 * b:1024 * b + 1024]

            def v0():
                rb = rho[:, l:l + 1].broadcast_to([128, 1024])
                u1 = k.tt(w["a1"][:, :], w["y"][:, :], cosT[:, l, :], M, [X["y"], tabs["t"], X.get("a1f")])
                u2 = k.tt(w["cs"][:, :], w["y"][:, :], sinT[:, l, :], M, [X["y"], tabs["t"], X.get("csf")])
                X["yf"] = [u1, u2]
                q1 = k.dve(lambda: nc.vector.tensor_tensor_scan(w["sq"][:, :], rb, w["a1"][:, :], i1[:, l:l + 1], M, A_),
                           [u1, t_i1, t_rho, X["sqf"]])
                q2 = k.dve(lambda: nc.vector.tensor_tensor_scan(w["a1"][:, :], rb, w["cs"][:, :], i2[:, l:l + 1], M, A_),
                           [u2, t_i2, t_rho, q1])
                u1 = k.tt(w["sq"][:, :], w["sq"][:, :], cosT[:, l, :], M, [q1])
                u2 = k.tt(w["a1"][:, :], w["a1"][:, :], sinT[:, l, :], M, [q2])
                u3 = k.tt(w["sq"][:, :], w["sq"][:, :], w["a1"][:, :], A_, [u1, u2])
                X["a1f"] = u3
                X["csf"] = q2
                X["h"] = k.stt(hc, w["sq"][:, :], V("scl", l), hc, M, A_, [u3, X["h"]])
                X["sqf"] = X["h"]
            return [v0]

        def mlp_steps(b, l):
            X, w = T[b], W[b]
            B0 = 4 * b
            hc = h[:, 1024 * b:1024 * b + 1024]
            st = []
            X["hid"] = []

            def up(m):
                def f():
                    bk = B0 + 2 * (m % 2)
                    for s in range(2):
                        q = k.mm(k.bank(bk + s), w1[:, l, 128 * m:128 * m + 128], w["y"][:, 512 * s:512 * s + 512], True, True,
                                 [X["y"], X["bank"] if m < 2 else X["hid"][m - 2], t_w1], inc=s == 1)
                    X["yf"] = q
                    X["hid"].append(k.af(hid[b][:, m, :], k.bank(bk, 2), ACT.Silu, [q, X.get("hf"), t_vec], bias=V("b1", 4 * l + m)))
                return f

            def down():
                for s in range(2):
                    for m in range(4):
                        q = k.mm(k.bank(B0 + s), w2[:, l, m, :], hid[b][:, m, 512 * s:512 * s + 512], m == 0, m == 3,
                                 [X["hid"], t_w2], inc=m == 3 and s == 1)
                X["hf"] = q
                X["h"] = k.stt(hc, k.bank(B0, 2), V("b2", l), hc, A_, A_, [q, X["h"]])
                X["bank"] = [X["h"], X["hid"]]
            return [up(0), up(1), up(2), up(3), down]

        seqs = []
        for b in range(2):
            s = []
            for l in range(4):
                s.append(("ln", V("ln1w", l), V("ln1b", l), ACT.Silu, l))
                s.append(("conv", l))
                s.append(("ln", V("ln2w", l), V("ln2b", l), ACT.Identity, l))
                s.append(("mlp", l))
            s.append(("ln", V("lnlw"), V("lnlb"), ACT.Identity, 9))
            steps = []
            for q in s:
                if q[0] == "ln":
                    steps += ln_steps(b, q[1], q[2], q[3])
                elif q[0] == "conv":
                    steps += conv_steps(b, q[1])
                else:
                    steps.append(("mlp", q[1]))
            seqs.append(steps)

        def runner(b):
            for s in seqs[b]:
                if isinstance(s, tuple):
                    for f in mlp_steps(b, s[1]):
                        yield f
                else:
                    yield s
        r0, r1 = runner(0), runner(1)
        lead = 5
        done0 = done1 = False
        n = 0
        while not (done0 and done1):
            if not done0:
                f = next(r0, None)
                if f is None:
                    done0 = True
                else:
                    f()
            if n >= lead and not done1:
                f = next(r1, None)
                if f is None:
                    done1 = True
                else:
                    f()
            n += 1

        yb = Ring([0, 2, 4, 6])
        for q in range(4):
            yb.free(q, [T[0]["bank"], T[1]["bank"], T[0]["y"], T[1]["y"]])
        xr, yr = xin, Ring([sb(f"yn{i}", [128, 1024]) for i in range(3)])

        def item(t):
            S = {}

            def mmul():
                S["i"], b, fr = yb.get()
                bb, tt_ = t // 8, t % 8
                for s in range(2):
                    m = k.mm(k.bank(b + s), W[bb]["y"][:, 128 * tt_:128 * tt_ + 128], wout[:, 512 * s:512 * s + 512], True, True,
                             [fr, T[bb]["y"], t_wo], inc=s == 1)
                S["steps"] = k.tail_steps(t, k.bank(b, 2), m, lambda toks: yb.free(S["i"], toks), xr, yr, x_src, x_dst, xn_dst,
                                          bias=bout[:, :], btok=t_bo)
            n_ = 4 if xn_dst is not None else 2
            return [mmul] + [(lambda j=j: S["steps"][j]()) for j in range(n_)]
        pipeline([item(t) for t in range(NT)])


def stage_b(k, x_src, xn_src, x_dst, xn_dst):
    nc, p, io = k.nc, k.p, k.io
    with ExitStack() as ctx:
        def sb(name, shape, dt=F32):
            return ctx.enter_context(nc.sbuf_tensor("b_" + name, shape, dt))

        w13h = sb("w13h", [128, 2, 2, FH], F32R)
        w13l = sb("w13l", [128, 2, 2, FH], F32R)
        bx = sb("bx", [96, FH], F32R)
        w2h, w2l = sb("w2h", [128, 6, 1024], F32R), sb("w2l", [128, 6, 1024], F32R)
        a13 = sb("a13", [128, 8, 32])
        a2 = sb("a2", [128, 24, 32])
        sel = sb("sel", [128, 3, 96])
        xnb = [sb(f"xn{i}", [128, 1024]) for i in range(2)]
        xr = Ring([sb(f"x{i}", [128, 1024]) for i in range(2)])
        yr = Ring([sb(f"y{i}", [128, 1024]) for i in range(2)])
        xT = sb("xT", [128, 8, 128])
        xsh, xsl = sb("xsh", [128, 2, 2, 256], F32R), sb("xsl", [128, 2, 2, 256], F32R)
        xs = sb("xs", [128, 2, 128])
        usb = sb("usb", [128, 256])
        ux = sb("ux", [96, 2, 2, 256], F32R)
        ur = sb("ur", [96, 2, 256], F32R)
        gr = Ring([sb(f"g{i}", [128, 2, 256]) for i in range(4)])
        ga = sb("ga", [128, 2, 256])
        gf = sb("gf", [128, 256])
        gfh, gfl = sb("gfh", [128, 6, 256], F32R), sb("gfl", [128, 6, 256], F32R)
        u2 = sb("u2", [128, 256])

        t_a13 = p.dma(k.wl, a13[:, :, :], io["a13T"].rearrange("(c p) n -> p c n", p=128))
        t_sel = p.dma(k.wl, sel[:, :, :], io["sel"])
        t_a2 = []
        for r in range(6):
            n = 128 if r < 5 else 48
            t_a2.append(p.dma(k.wl, a2[0:n, 4 * r:4 * r + 4, :],
                              io["a2T"].rearrange("(j q) n -> q j n", q=688)[128 * r:128 * r + n, :, :]))
        stage = Ring([xr.bufs[0], xr.bufs[1], yr.bufs[0], yr.bufs[1]])
        t_w = {}
        zero = [k.dve(lambda: nc.vector.memset(gfh[:, 5, :].bitcast(F32), 0.0)),
                k.dve(lambda: nc.vector.memset(gfl[:, 5, :].bitcast(F32), 0.0))]
        for c0 in range(0, FH, 688):
            for v in range(2):
                for c in range(2):
                    t_w[v, c, c0] = k.load_split(w13h[:, v, c, c0:c0 + 688], w13l[:, v, c, c0:c0 + 688],
                                                 io["w13T"][v, 128 * c:128 * c + 128, c0:c0 + 688], stage)
            i, buf, fr = stage.get()
            t = p.dma(k.wl, buf[0:96, 0:688], io["bx"][:, c0:c0 + 688], fr)
            a = k.copy(bx[:, c0:c0 + 688], buf[0:96, 0:688], t, e="act")
            b = k.tt(bx[32:64, c0:c0 + 688], buf[32:64, 0:688], bx[32:64, c0:c0 + 688].bitcast(F32), ALU.subtract, [a])
            stage.free(i, [a, b])
            t_w["b", c0] = [a, b]
        t_up = list(t_w.values())
        t_dn = [k.load_split(w2h[:, c, :], w2l[:, c, :], io["w2x"][128 * c:128 * c + 128, :], stage) for c in range(6)]
        fr = [stage.busy[i] for i in range(4)]
        for i in range(2):
            xr.busy[i] = fr[i]
            yr.busy[i] = fr[2 + i]

        NB = 8
        gbanks = Ring([0, 2])
        misc_free = [None]
        y_free = [None]
        XS = {}

        def prep(n):
            steps = []
            S = {"x": [], "w": []}
            par = n % 2

            def load():
                for i in range(2):
                    t = 2 * n + i
                    S["x"].append(p.dma(k.ld, xnb[i][:, :], xn_src[128 * t:128 * t + 128, :], [XS.get(("f", i)), k.done_xn[t]]))
            steps.append(load)

            def trans(i, hf):
                def f():
                    o = k.bank(5)
                    for c in range(4):
                        cc = 4 * hf + c
                        m = k.tr(o[:, 128 * c:128 * c + 128], xnb[i][:, 128 * cc:128 * cc + 128],
                                 [S["x"][i], misc_free[0]], inc=c == 3)
                    if hf == 1:
                        XS["f", i] = m
                    a = k.copy(xT[:, 4 * hf:4 * hf + 4, :], o.rearrange("p (c n) -> p c n", c=4), [m, XS.get("xTf")], e="act")
                    misc_free[0] = a
                    S["xT", hf] = a
                return f

            def fold(i):
                def f():
                    w = [S["xT", 0], S["xT", 1]]
                    o = k.bank(5)
                    for c in range(8):
                        g = c % 4
                        m = k.mm(o[32 * g:32 * g + 32, 0:128], a13[:, c, :], xT[:, c, :],
                                 c < 4, c >= 4, [w, misc_free[0], t_a13], inc=c == 7, skip=True)
                    a = k.copy(usb[:, 128 * i:128 * i + 128], o[:, 0:128], [m, XS.get("uf")], e="act")
                    misc_free[0] = a
                    S["u", i] = a
                    v = xT[:, :, :].rearrange("p (j c) n -> p j c n", c=2)
                    a = k.tt(xs[:, :, :], v[:, 0], v[:, 1], ALU.add, [w, XS.get("xsf")])
                    a = k.tt(xs[:, :, :], xs[:, :, :], v[:, 2], ALU.add, [a])
                    a = k.tt(xs[:, :, :], xs[:, :, :], v[:, 3], ALU.add, [a])
                    XS["xTf"] = [a, m]
                    cols = slice(128 * i, 128 * i + 128)
                    r = k.split(xsh[:, par, :, cols], xsl[:, par, :, cols], xs[:, :, :], [a, XS.get(("xsf", par))])
                    XS["xsf"] = r
                    S["w"].append(r)
                return f

            def low():
                o = k.bank(5)
                for v in range(2):
                    m = k.mm(o[0:96, 256 * v:256 * v + 256], sel[:, v, :], usb[:, :], True, True,
                             [S["u", 0], S["u", 1], misc_free[0], t_sel], inc=v == 1)
                XS["uf"] = m
                o3 = o.rearrange("p (v n) -> p v n", v=2)
                wf = [m, XS.get(("xsf", par))]
                a = k.copy(ux[0:64, par, :, :], o3[0:64], wf, e="act")
                b = k.copy(ur[64:96, :, :], o3[64:96], [m, XS.get("urf")], e="act")
                c = k.tt(ux[64:96, par, :, :], o3[64:96], ur[64:96, :, :].bitcast(F32), ALU.subtract, [b, wf])
                misc_free[0] = [a, b, c]
                XS["urf"] = c
                S["w"].append([a, c])
                XS["w", n] = S["w"]
            steps += [trans(0, 0), trans(0, 1), fold(0), trans(1, 0), trans(1, 1), fold(1), low]
            return steps

        DN = {}

        def updown(n):
            par = n % 2
            steps = []
            S = {"g": [], "last": None}

            def pair(r, jp):
                rows = 128 if r < 5 else 48

                def f():
                    gi, b, fr = gbanks.get()
                    for v in range(2):
                        for jj in range(2):
                            o = k.PS[0:rows, 512 * (b + v) + 256 * jj:512 * (b + v) + 256 * jj + 256]
                            c0 = 688 * (2 * jp + jj) + 128 * r
                            cs = slice(c0, c0 + rows)
                            w = [XS["w", n], fr, t_up if n == 0 else None]
                            for c in range(2):
                                k.mm(o, w13h[:, v, c, cs], xsh[:, par, c, :], c == 0, False, w)
                                k.mm(o, w13h[:, v, c, cs], xsl[:, par, c, :], False, False)
                                k.mm(o, w13l[:, v, c, cs], xsh[:, par, c, :], False, False)
                            m = k.mm(o, bx[:, cs], ux[:, par, v, :], False, True, inc=True)
                    S["m"] = m
                    i, g, gfr = gr.get()
                    gp = g[0:rows, :, :]
                    P2 = lambda q: k.PS[0:rows, 512 * q:512 * q + 512].rearrange("p (a n) -> p a n", a=2)
                    a = k.af(gp, P2(b), ACT.Silu, [m, gfr])
                    c = k.tt(gp, gp, P2(b + 1), ALU.mult, [a])
                    gbanks.free(gi, [a, c])
                    S["g"].append((i, g, c, r, jp))
                return f

            def folded(r):
                rows = 128 if r < 5 else 48

                def f():
                    if 1:
                        i0, g0, c0_ = S["g"][2 * r][:3]
                        _, g1, c = S["g"][2 * r + 1][:3]
                        a = k.tt(ga[0:rows, :, :], g0[0:rows, :, :], g1[0:rows, :, :], ALU.add, [c0_, c, XS.get("gaf")])
                        d = k.tt(gf[0:rows, :], ga[0:rows, 0, :], ga[0:rows, 1, :], ALU.add, [a, XS.get("gff")])
                        XS["gaf"] = d
                        e = k.split(gfh[0:rows, r, :], gfl[0:rows, r, :], gf[0:rows, :], [d, DN.get("free"), zero])
                        XS["gff"] = e
                        S["gs"] = [S.get("gs"), e]
                        S["fa"] = a
                return f

            def lora2(idx):
                def f():
                    i, g, c, r, jp = S["g"][idx]
                    rows = 128 if r < 5 else 48
                    for jj in range(2):
                        j = 2 * jp + jj
                        m = k.mm(k.PS[32 * j:32 * j + 32, 2048:2048 + 256], a2[0:rows, 4 * r + j, :], g[0:rows, jj, :],
                                 r == 0, r == 5, [c, t_a2, DN.get("u2f")], inc=jj == 1, skip=True)
                    S.setdefault("lm", {})[idx] = m
                    if jp == 1:
                        for q in (idx - 1, idx):
                            gr.free(S["g"][q][0], [S["lm"][q], S["fa"]])
                return f

            for r in range(6):
                for jp in range(2):
                    def both(r=r, jp=jp):
                        pair(r, jp)()
                        idx = 2 * r + jp
                        if idx >= 2 and jp == 0:
                            folded(r - 1)()
                        if idx >= 1:
                            lora2(idx - 1)()
                    steps.append(both)

            def end():
                folded(5)()
                lora2(11)()
                XS["xsf", par] = S["m"]
                m = S["lm"][11]
                a = k.copy(u2[:, :], k.PS[:, 2048:2048 + 256], [m, DN.get("u2sb")], e="act")
                DN["u2f"] = a
                o = k.bank(5)[0:96, 0:256]
                m = k.mm(o, sel[:, 2, :], u2[:, :], True, True, [a, misc_free[0]], inc=True)
                DN["u2sb"] = m
                o = k.bank(5)[64:96, 0:256]
                e = k.split(gfh[64:96, 5, :], gfl[64:96, 5, :], o, [m, DN.get("free"), zero])
                misc_free[0] = e
                S["gs"] = [S["gs"], e]
            return steps, end, S

        def down(n, i, S):
            t = 2 * n + i
            cols = slice(128 * i, 128 * i + 128)

            for s in range(2):
                o = k.bank(6 + s)
                for c in range(6):
                    q = slice(0, 128) if c < 5 else slice(0, 96)
                    a, b = gfh[q, c, cols], gfl[q, c, cols]
                    u, v = w2h[q, c, 512 * s:512 * s + 512], w2l[q, c, 512 * s:512 * s + 512]
                    w = [S["gs"], y_free[0], t_dn if n == 0 else None]
                    k.mm(o, a, u, c == 0, False, w)
                    k.mm(o, a, v, False, False)
                    m = k.mm(o, b, u, False, c == 5, inc=c == 5)
            if i == 1:
                DN["free"] = m

            def free_y(toks):
                y_free[0] = toks
            return k.tail_steps(t, k.bank(6, 2), m, free_y, xr, yr, x_src, x_dst, xn_dst, x_tok=k.done_x[t])

        nx = prep(0)
        for f in nx:
            f()
        pend = None
        tails = []

        def tail_some():
            if tails:
                tails.pop(0)()

        for n in range(NB + 1):
            if n < NB:
                steps, end, S = updown(n)
                nx = prep(n + 1) if n + 1 < NB else []
                if nx:
                    nx.pop(0)()
                for q, f in enumerate(steps):
                    f()
                    if q == 0 and pend is not None:
                        tails += down(n - 1, 0, pend)
                    if q == 1 and pend is not None:
                        tail_some()
                        tail_some()
                        tails += down(n - 1, 1, pend)
                    if q >= 2:
                        tail_some()
                    if q >= 4 and nx:
                        nx.pop(0)()
                while nx:
                    nx.pop(0)()
                while tails:
                    tail_some()
                end()
                pend = S
            else:
                a = down(n - 1, 0, pend)
                a[0]()
                a[1]()
                b = down(n - 1, 1, pend)
                for q in range(len(b)):
                    b[q]()
                    if q + 2 < len(a):
                        a[q + 2]()


def proj_pass(k, ctx, pre, tiles, in_src, in_tok, wh, wl, t_w, x_src, x_dst, xn_dst, rings, bias=None, btok=None, hook=None):
    nc, p = k.nc, k.p
    inr, xth, xr, yr = rings
    trb, yb = Ring([0, 2]), Ring([4, 6])
    if "pp" in k.carry:
        trb, yb = k.carry["pp"]
    k.carry["pp"] = (trb, yb)

    def item(t):
        S = {}

        def load():
            S["ii"], S["in"], fr = inr.get()
            S["ld"] = p.dma(k.ld, S["in"][:, :], in_src[128 * t:128 * t + 128, :], [fr, in_tok(t)])

        def trans():
            bi, b, fr = trb.get()
            for c in range(8):
                m = k.tr(k.PS[:, 512 * b + 128 * c:512 * b + 128 * c + 128], S["in"][:, 128 * c:128 * c + 128],
                         [S["ld"], fr], inc=c == 7)
            inr.free(S["ii"], m)
            S["xi"], (S["h"], S["l"]), fr = xth.get()
            S["w"] = k.split(S["h"][:, :, :], S["l"][:, :, :], k.bank(b, 2).rearrange("p (c n) -> p c n", c=8), [m, fr])
            trb.free(bi, S["w"])

        def mmul():
            S["i"], b, fr = yb.get()
            for s in range(2):
                o = k.bank(b + s)
                for c in range(8):
                    u, v = wh[:, c, 512 * s:512 * s + 512], wl[:, c, 512 * s:512 * s + 512]
                    k.mm(o, S["h"][:, c, :], u, c == 0, False, [S["w"], fr, t_w[c]])
                    k.mm(o, S["h"][:, c, :], v, False, False)
                    m = k.mm(o, S["l"][:, c, :], u, False, c == 7, inc=c == 7)
            xth.free(S["xi"], m)
            S["steps"] = k.tail_steps(t, k.bank(b, 2), m, lambda toks: yb.free(S["i"], toks), xr, yr, x_src, x_dst, xn_dst,
                                      bias=bias, btok=btok, hook=hook, x_tok=k.done_x[t])
        n_ = 4 if xn_dst is not None else 2
        return [load, trans, mmul] + [(lambda j=j: S["steps"][j]()) for j in range(n_)]
    pipeline([item(t) for t in tiles])


def stage_c(k, x_src, xn_src, ctx_d, x_dst, xn_dst):
    nc, p, io = k.nc, k.p, k.io
    SC = float(1.0 / 32 ** 0.5)
    with ExitStack() as ctx:
        def sb(name, shape, dt=F32):
            return ctx.enter_context(nc.sbuf_tensor("c_" + name, shape, dt))

        xth, xtl = sb("xth", [128, 8, 1024], F32R), sb("xtl", [128, 8, 1024], F32R)
        K4 = sb("K4", [128, 8, 1024], F32R)
        Q4 = sb("Q4", [128, 8, 1024], F32R)
        V = sb("V", [128, 8, 8, 33])
        qh, ql = sb("qh", [128, 1024], F32R), sb("ql", [128, 1024], F32R)
        wqh, wql = sb("wqh", [128, 8, 128], F32R), sb("wql", [128, 8, 128], F32R)
        mc = sb("mc", [128, 4, 8])
        mT = sb("mT", [32, 128], F32R)
        junk = sb("junk", [128, 128])
        rc = sb("rc", [128, 2, 8])
        cx = sb("cx", [128, 8, 256])
        Pt = Ring([sb(f"P{i}", [128, 1024]) for i in range(3)])
        raw = sb("raw", [128, 1024])
        rawf = [None]
        xin = Ring([Pt.bufs[0], Pt.bufs[1]])

        t_one = [k.dve(lambda: nc.vector.memset(V[:, :, :, 32:33], 1.0)),
                 k.dve(lambda: nc.vector.memset(K4[96:97, :, :].bitcast(F32), -1.0))]
        k4_free, q4_free = [None] * 8, [None] * 8
        stg_free = [None]
        v_free = [None]
        xt_free = [None]
        mT_free = [None]
        wq_free = [None]
        cx_free = [None, None]
        cx_tok = []

        def wload(dst_cols):
            t = p.dma(k.wl, raw[:, :].rearrange("p (c n) -> p c n", c=8), dst_cols.rearrange("(c p) n -> p c n", p=128), rawf[0])
            w = k.split(wqh[:, :, :], wql[:, :, :], raw[:, :].rearrange("p (c n) -> p c n", c=8), [t, wq_free[0]], e="pool")
            rawf[0] = w
            return w

        def load_x(src):
            tb = Ring([0, 2, 4])
            bar = [k.p.last(e) for e in ("pe", "act", "dve", "pool")]
            t_x = []

            def lt(t):
                S = {}

                def f0():
                    S["i"], S["x"], fr = xin.get()
                    S["ld"] = p.dma(k.ld, S["x"][:, :], xn_src[128 * t:128 * t + 128, :], [fr, k.done_xn[t], bar])

                def f1():
                    bi, bk, fr = tb.get()
                    for c in range(8):
                        m = k.tr(k.PS[:, 512 * bk + 128 * c:512 * bk + 128 * c + 128], S["x"][:, 128 * c:128 * c + 128],
                                 [S["ld"], fr, bar], inc=c == 7)
                    xin.free(S["i"], m)
                    cols = slice(128 * (t % 8), 128 * (t % 8) + 128)
                    w = k.split(xth[:, :, cols], xtl[:, :, cols], k.bank(bk, 2).rearrange("p (c n) -> p c n", c=8), [m, xt_free[0]])
                    tb.free(bi, w)
                    t_x.append(w)
                return [f0, f1]
            pipeline([lt(t) for t in range(8 * src, 8 * src + 8)])
            for i in range(3):
                Pt.busy[i] = [xin.busy, k.p.last("pe")]
            xin.busy, xin.i = [[], []], 0
            return t_x

        mb = Ring([6, 7])
        t_k4 = [None] * 8
        t_v = []

        def chunk_T(w, waits, half, bank, fr):
            o = k.bank(bank)
            for c in range(8):
                xc, xd = xth[:, c, 512 * half:512 * half + 512], xtl[:, c, 512 * half:512 * half + 512]
                k.mm(o, wqh[:, c, :], xc, c == 0, False, [w, waits, fr])
                k.mm(o, wqh[:, c, :], xd, False, False)
                m = k.mm(o, wql[:, c, :], xc, False, c == 7, inc=c == 7)
            return m

        def kv(b, src, t_x):
            w = wload(io["wk"][:, 128 * b:128 * b + 128])
            r = []
            for half in range(2):
                i, bk, fr = mb.get()
                m = chunk_T(w, t_x, half, bk, fr)
                cs = slice(512 * half, 512 * half + 512)
                r.append(k.split(qh[:, cs], ql[:, cs], k.bank(bk), [m, stg_free[0]]))
                mb.free(i, r[-1])
            wq_free[0] = m
            ds = []
            for g in range(4):
                j = 2 * g + src
                s = slice(32 * g, 32 * g + 32)
                t_k4[j] = [p.dma(k.ld, K4[0:32, j, :].bitcast(F32), qh[s, :].bitcast(F32), [r, k4_free[j]]),
                           p.dma(k.ld, K4[32:64, j, :].bitcast(F32), qh[s, :].bitcast(F32), [r]),
                           p.dma(k.ld, K4[64:96, j, :].bitcast(F32), ql[s, :].bitcast(F32), [r])]
                ds.append(t_k4[j])
            stg_free[0] = ds
            w = wload(io["wv"][:, 128 * b:128 * b + 128])
            for t4 in range(2):
                i, bk, fr = mb.get()
                for tt_ in range(4):
                    o = k.bank(bk)[:, 128 * tt_:128 * tt_ + 128]
                    tok = slice(128 * (4 * t4 + tt_), 128 * (4 * t4 + tt_) + 128)
                    for c in range(8):
                        k.mm(o, xth[:, c, tok], wqh[:, c, :], c == 0, False, [w, t_x, fr])
                        k.mm(o, xth[:, c, tok], wql[:, c, :], False, False)
                        m = k.mm(o, xtl[:, c, tok], wqh[:, c, :], False, c == 7, inc=c == 7)
                for tt_ in range(4):
                    a = k.copy(V[:, 4 * t4 + tt_, src:8:2, 0:32],
                               k.bank(bk)[:, 128 * tt_:128 * tt_ + 128].rearrange("p (g d) -> p g d", g=4),
                               [m, v_free[0], t_one], e="act")
                    t_v.append(a)
                mb.free(i, a)
            wq_free[0] = m
            xt_free[0] = m

        t_x = None
        for b in range(2):
            if b == 0:
                t_x = load_x(1)
            mb.i, mb.busy = 0, [[k.p.last("dve"), k.p.last("act")] for _ in range(2)]
            kv(b, 1 - b, t_x)
            t_x = load_x(b)
            kv(b, b, t_x)
            v_tok = t_v

            sr = Ring([0, 2, 4])
            for i in range(3):
                sr.free(i, [t_x])
            ctxf = [k.p.last("act")]
            mf = [mb.busy]
            mb.busy = [[], []]
            t_q4 = {}
            t_m = {}

            qS = {}

            def qproj(j, part):
                if part == 0:
                    qS["r"] = []
                    qS["w"] = wload(io["wq"][:, 128 * j:128 * j + 128])
                m = chunk_T(qS["w"], t_x, part, 7, mf[0])
                cs = slice(512 * part, 512 * part + 512)
                e = k.split(qh[:, cs], ql[:, cs], k.bank(7), [m, stg_free[0] if part == 0 else None])
                mf[0] = [e]
                qS["r"].append(e)
                if part == 1:
                    wq_free[0] = m
                    if j == 7:
                        xt_free[0] = m
                    ds = []
                    for g in range(4):
                        s = slice(32 * g, 32 * g + 32)
                        q = (4 * j + g) % 8
                        d = [p.dma(k.ld, Q4[0:32, q, :].bitcast(F32), qh[s, :].bitcast(F32), [qS["r"], q4_free[q]]),
                             p.dma(k.ld, Q4[32:64, q, :].bitcast(F32), ql[s, :].bitcast(F32), [qS["r"]]),
                             p.dma(k.ld, Q4[64:96, q, :].bitcast(F32), qh[s, :].bitcast(F32), [qS["r"]])]
                        t_q4[4 * j + g] = d
                        ds.append(d)
                    stg_free[0] = ds

            def amax(h, t):
                g, q, n = h // 4, h % 8, 128 * (t + 1)
                i, bk, fr = sr.get()
                for s in range(0, n, 512):
                    e = min(n, s + 512)
                    m = k.mm(k.PS[:, 512 * bk + s:512 * bk + e], Q4[0:96, q, 128 * t:128 * t + 128], K4[0:96, g, s:e],
                             True, True, [t_q4[h], t_k4[g], fr], inc=True)
                o = mc[:, h % 4, t:t + 1]
                base = 512 * bk
                w = [m, mT_free[0]]
                if t:
                    a = k.dve(lambda: nc.vector.tensor_reduce(o, k.PS[:, base:base + n - 128], AX, ALU.max), w)
                    init = o
                else:
                    a, init = None, -3.0e38
                b_ = k.dve(lambda: nc.vector.tensor_tensor_reduce(
                    out=junk[:, :], in0=k.PS[:, base + n - 128:base + n], in1=k.mask, scale=1.0, scalar=init,
                    op0=ALU.add, op1=ALU.max, accum_out=o), [w, a, k.t_c, jk[0]])
                jk[0] = b_
                sr.free(i, [b_])
                t_m.setdefault(h, []).append(b_)

            jk = [None]

            def mrow(j):
                m = k.tr(k.bank(7)[0:32, 0:128], mc[:, :, :].rearrange("p a b -> p (a b)"), [[t_m[4 * j + g] for g in range(4)], mf[0]],
                         inc=True)
                a = k.copy(mT[:, :], k.bank(7)[0:32, 0:128], [m, mrow_d[0]], e="act")
                mf[0] = [a]
                mT_free[0] = m
                ds = []
                for g in range(4):
                    h = 4 * j + g
                    d = p.dma(k.ld, Q4[96:97, h % 8, :].bitcast(F32).rearrange("a (t n) -> a t n", t=8), mT[8 * g:8 * g + 8, :].bitcast(F32), [a, q4_free[h % 8]])
                    ds.append(d)
                    t_q4[h] = [t_q4[h], d]
                mrow_d[0] = ds

            mrow_d = [None]
            pend = []

            def score(h, kt):
                g, q, n = h // 4, h % 8, 1024 - 128 * kt
                i, bk, fr = sr.get()
                for s in range(0, n, 512):
                    e = min(n, s + 512)
                    m = k.mm(k.PS[:, 512 * bk + s:512 * bk + e], K4[0:97, g, 128 * kt:128 * kt + 128],
                             Q4[0:97, q, 128 * kt + s:128 * kt + e], True, True, [t_q4[h], t_k4[g], fr, t_one], inc=True)
                pi, P, pf = Pt.get()
                a = k.af(P[:, 0:n], k.PS[:, 512 * bk:512 * bk + n], ACT.Exp, [m, pf], scale=SC)
                sr.free(i, [a])
                c = k.pool(lambda: nc.gpsimd.affine_select(out=P[:, 0:128], in_=P[:, 0:128], compare_op=ALU.is_ge, fill=0.0,
                                                           base=0, pattern=[[1, 128]], channel_multiplier=-1), [a])
                if kt == 7:
                    q4_free[q] = m
                    if h % 4 == 3:
                        k4_free[g] = m
                return (h, kt, pi, P, a, c)

            def pv(h, kt, pi, P, a, c):
                g = h // 4
                for t in [*range(kt + 1, 8), kt]:
                    o = k.bank(6)[:, 33 * t:33 * t + 33]
                    m = k.mm(o, P[:, 128 * (t - kt):128 * (t - kt) + 128], V[:, kt, g, :], kt == 0 and t == 1, kt == t,
                             [a, c if t == kt else None, ctxf, v_tok], inc=t == kt, skip=True)
                Pt.free(pi, m)
                if kt == 7:
                    v = k.bank(6)[:, 0:264].rearrange("p (t n) -> p t n", n=33)
                    hb = (h // 4) % 2
                    r = k.dve(lambda: nc.vector.reciprocal(rc[:, h % 2, :], v[:, :, 32]), [m])
                    dst = cx[:, :, 128 * hb + 32 * (h % 4):128 * hb + 32 * (h % 4) + 32]
                    e = k.tt(dst, v[:, :, 0:32], rc[:, h % 2, :].unsqueeze(2).broadcast_to([128, 8, 32]), ALU.mult, [r, cx_free[hb]])
                    ctxf[0] = e
                    if h == 31:
                        v_free[0] = m
                    if h % 4 == 3:
                        d = p.dma(k.st, ctx_d[1024 * b:1024 * b + 1024, 128 * g:128 * g + 128].rearrange("(t p) n -> p t n", p=128),
                                  cx[:, :, 128 * hb:128 * hb + 128], e)
                        cx_free[hb] = d
                        cx_tok.append(d)

            qproj(0, 0)
            qproj(0, 1)
            for g in range(4):
                for t in range(8):
                    amax(g, t)
            mrow(0)
            qproj(1, 0)
            qproj(1, 1)
            for j in range(8):
                for g in range(4):
                    h = 4 * j + g
                    for n in range(8):
                        s = score(h, n)
                        if j < 7:
                            amax(h + 4, 7 - n)
                        pend.append(s)
                        if len(pend) > 1:
                            pv(*pend.pop(0))
                if j < 7:
                    while pend:
                        pv(*pend.pop(0))
                    mrow(j + 1)
                    if j + 2 < 8:
                        qproj(j + 2, 0)
                        qproj(j + 2, 1)
            while pend:
                pv(*pend.pop(0))
    p.barrier()
    with ExitStack() as ctx:
        def sb(name, shape, dt=F32):
            return ctx.enter_context(nc.sbuf_tensor("c2_" + name, shape, dt))
        wh, wl = sb("wh", [128, 8, 1024], F32R), sb("wl", [128, 8, 1024], F32R)
        bo = sb("bo", [128, 1024])
        stg = Ring([sb(f"stg{i}", [128, 1024]) for i in range(2)])
        rings = (Ring([sb(f"in{i}", [128, 1024]) for i in range(3)]),
                 Ring([(sb(f"h{i}", [128, 8, 128], F32R), sb(f"l{i}", [128, 8, 128], F32R)) for i in range(2)]),
                 Ring([sb(f"x{i}", [128, 1024]) for i in range(4)]), Ring([sb(f"y{i}", [128, 1024]) for i in range(4)]))
        t_bo = p.dma(k.wl, bo[:, :], io["bo"].partition_broadcast(128))
        t_w = [k.load_split(wh[:, c, :], wl[:, c, :], io["wo"][128 * c:128 * c + 128, :], stg) for c in range(8)]
        k.carry.pop("pp", None)
        proj_pass(k, ctx, "c", range(NT), ctx_d, lambda t: None, wh, wl, t_w, x_src, x_dst, xn_dst, rings,
                  bias=bo[:, :], btok=t_bo)


def stage_d(k, x_src, xn_src, x_dst):
    nc, p, io = k.nc, k.p, k.io
    with ExitStack() as ctx:
        def sb(name, shape, dt=F32):
            return ctx.enter_context(nc.sbuf_tensor("d_" + name, shape, dt))
        wh, wl = sb("wh", [128, 8, 1024], F32R), sb("wl", [128, 8, 1024], F32R)
        dn = sb("dn", [128, 4, 1024])
        up = sb("up", [128, 4, 1024])
        upc = sb("upc", [128, 4, 1024])
        wqT = sb("wqT", [128, 8, 128])
        keyT = sb("keyT", [128, 8])
        sm = sb("sm", [128, 64])
        wor = Ring([sb(f"wo{i}", [128, 1024]) for i in range(2)])
        rings = (Ring([sb(f"in{i}", [128, 1024]) for i in range(3)]),
                 Ring([(sb(f"h{i}", [128, 8, 128], F32R), sb(f"l{i}", [128, 8, 128], F32R)) for i in range(1)]),
                 Ring([sb(f"x{i}", [128, 1024]) for i in range(2)]), Ring([sb(f"y{i}", [128, 1024]) for i in range(2)]))
        t_dn = p.dma(k.wl, dn[:, :, :], io["dnT"].rearrange("(c p) n -> p c n", p=128))
        t_up = p.dma(k.wl, up[:, :, :], io["up"].rearrange("(c p) n -> p c n", p=128))
        t_wq = p.dma(k.wl, wqT[:, :, :], io["lwqT"].rearrange("(c p) n -> p c n", p=128))
        t_ky = p.dma(k.wl, keyT[:, :], io["keyT"])
        xin = rings[0]
        wh_free = [None]
        upc_free = [None]
        smf = [None]
        for b in range(2):
            bar = [k.p.last(e) for e in ("act", "dve", "pe")]
            o = k.PS[:, 0:8]
            for t in range(8 * b, 8 * b + 8):
                i, x, fr = xin.get()
                ld = p.dma(k.ld, x[:, :], xn_src[128 * t:128 * t + 128, :], [fr, k.done_xn[t]])
                for c in range(8):
                    m = k.mm(o[:, c:c + 1], x[:, 128 * c:128 * c + 128], k.ones[:, 0:1], t == 8 * b and c == 0, t == 8 * b + 7,
                             [ld, k.t_c, bar], inc=c == 7, skip=True)
                xin.free(i, m)
            mean = sm[:, 0:8]
            a = k.ts(mean, o, 1.0 / 1024, None, ALU.mult, w=[m, smf[0]])
            for c in range(8):
                m = k.mm(k.PS[:, 512:513], wqT[:, c, :], sm[:, c:c + 1], c == 0, c == 7, [a, t_wq], inc=c == 7)
            a = k.copy(sm[:, 8:9], k.PS[:, 512:513], m)
            m = k.mm(k.PS[0:1, 1024:1032], sm[:, 8:9], keyT[:, :], True, True, [a, t_ky], inc=True)
            s = sm[0:1, 16:24]
            a = k.copy(s, k.PS[0:1, 1024:1032], m)
            a2 = k.dve(lambda: nc.vector.tensor_reduce(sm[0:1, 24:25], s, AX, ALU.max), [a])
            isq = float(1.0 / np.sqrt(128.0))
            a2 = k.ts(sm[0:1, 25:26], sm[0:1, 24:25], -isq, None, ALU.mult, w=a2)
            a = k.af(sm[0:1, 32:40], s, ACT.Exp, [a, a2], scale=isq, bias=sm[0:1, 25:26])
            a2 = k.dve(lambda: nc.vector.tensor_reduce(sm[0:1, 26:27], sm[0:1, 32:40], AX, ALU.add), [a])
            a2 = k.dve(lambda: nc.vector.reciprocal(sm[0:1, 27:28], sm[0:1, 26:27]), [a2])
            a = k.ts(sm[0:1, 40:48], sm[0:1, 32:40], sm[0:1, 27:28], None, ALU.mult, w=[a, a2])
            m = k.mm(k.PS[:, 1536:1544], k.ones[0:1, :], sm[0:1, 40:48], True, True, [a], inc=True)
            ce = k.PS[:, 1536:1544].rearrange("p (c e) -> p c e", e=2)
            a = k.copy(sm[0:64, 48:52], ce[0:64, :, 0], m)
            a2 = k.copy(sm[64:128, 48:52], ce[64:128, :, 1], m)
            u = [k.ts(upc[:, c, :], up[:, c, :], sm[:, 48 + c:49 + c], None, ALU.mult, w=[a, a2, t_up, upc_free[0]]) for c in range(4)]
            smf[0] = u
            wb = Ring([4, 6])
            for q in range(2):
                wb.free(q, bar)
            t_w = []
            for i8 in range(8):
                wi, wo, fr = wor.get()
                tw = p.dma(k.wl, wo[:, :], io["worgT"][128 * i8:128 * i8 + 128, :], fr)
                bi, bk, bf = wb.get()
                for s_ in range(2):
                    for c in range(4):
                        m = k.mm(k.bank(bk + s_), dn[:, c, 128 * i8:128 * i8 + 128], upc[:, c, 512 * s_:512 * s_ + 512],
                                 c == 0, c == 3, [u, t_dn, bf], inc=c == 3)
                a = k.tt(wo[:, :], wo[:, :], k.bank(bk, 2), ALU.add, [tw, m])
                wb.free(bi, a)
                r = k.split(wh[:, i8, :], wl[:, i8, :], wo[:, :], [a, wh_free[0]])
                wor.free(wi, r)
                t_w.append(r)
            upc_free[0] = m
            k.carry.pop("pp", None)
            trb, yb = Ring([0, 2]), Ring([4, 6])
            for q in range(2):
                yb.free(q, a)
                trb.free(q, u)
            k.carry["pp"] = (trb, yb)
            proj_pass(k, ctx, f"d{b}", range(8 * b, 8 * b + 8), xn_src, lambda t: k.done_xn[t], wh, wl, t_w,
                      x_src, x_dst, None, rings)
            wh_free[0] = k.p.last("pe")


def program(nc, io, out):
    with ExitStack() as ctx:
        k = K(nc, ctx, io, out)
        k.carry = {}
        k.done_x, k.done_xn = {}, {}
        x, xn = io["x"], None
        n = 0
        for s in STAGES:
            last = s == STAGES[-1]
            nx = out if last else k.scr[n]
            nn = None if last else k.scr[n + 1]
            n += 2
            old_x, old_xn = dict(k.done_x), dict(k.done_xn)
            for t in range(NT):
                k.done_x.setdefault(t, None)
                k.done_xn.setdefault(t, None)
            if s == "A":
                stage_a(k, x, nx, nn)
            elif s == "B":
                stage_b(k, x, xn, nx, nn)
            elif s == "C":
                stage_c(k, x, xn, k.scr[7], nx, nn)
            elif s == "D":
                stage_d(k, x, xn, nx)
            elif s == "L":
                prelude(k, x, nn)
                nx = x
            x, xn = nx, nn
            k.p.barrier()
        k.p.run(ctx.enter_context(nc.Block()))


def lay_out(i):
    f = np.float32
    g = {n: np.asarray(a) for n, a in i.items()}
    d = {}
    d["x"] = g["L0_attn_x"].reshape(2048, D)
    cst = np.zeros((128, 520), f)
    cst[:, 0:128] = np.eye(128)
    cst[:, 128:256] = np.eye(128) - 1.0 / 128
    cst[:, 256:384] = np.where(np.arange(128)[None, :] > np.arange(128)[:, None], -1.0e38, 0.0)
    cst[:, 384:512] = 1.0
    cst[:, 512] = 1.0 / 128
    d["cst"] = cst
    cols = [g["L0_attn_bin"][None]] + [g["L0_attn_" + n] for n in ("ln1_w", "ln1_b", "phz_re", "phz_im", "lc_re", "lc_im", "sc_lin", "ln2_w", "ln2_b")]
    cols += [g["L0_attn_b1"].reshape(16, 128), g["L0_attn_b2"], g["L0_attn_lnl_w"][None], g["L0_attn_lnl_b"][None]]
    d["vecs"] = np.concatenate(cols, 0).T
    d["winT"] = g["L0_attn_Win"].T
    d["w1T"] = g["L0_attn_W1"].transpose(0, 2, 1)
    d["w2T"] = g["L0_attn_W2"].transpose(0, 2, 1)
    d["woutT"] = g["L0_attn_Wout"].T
    d["bout"] = g["L0_attn_bout"]
    d["w13T"] = np.stack([g["L0_ffn_w1q"].T, g["L0_ffn_w3q"].T])
    bx = np.zeros((96, FH), f)
    for q in range(3):
        bx[32 * q:32 * q + 2] = g["L0_ffn_b1"].T
        bx[32 * q + 2:32 * q + 4] = g["L0_ffn_b3"].T
    d["bx"] = bx
    a13 = np.zeros((D, 32), f)
    a13[:, 0:2] = g["L0_ffn_a1"].T
    a13[:, 2:4] = g["L0_ffn_a3"].T
    d["a13T"] = a13
    a2 = np.zeros((FH, 32), f)
    a2[:, 0:2] = g["L0_ffn_a2"].T
    d["a2T"] = a2
    w2x = np.zeros((768, D), f)
    w2x[0:688] = g["L0_ffn_w2q"].T
    w2x[704:706] = g["L0_ffn_b2"].T
    d["w2x"] = w2x
    sel = np.zeros((128, 3, 96), f)
    for c in range(4):
        for q in range(3):
            for r in range(2):
                sel[32 * c + r, 0, 32 * q + r] = 0.5
                sel[32 * c + 2 + r, 1, 32 * q + 2 + r] = 0.5
        for r in range(2):
            sel[32 * c + r, 2, 64 + r] = 0.5
    d["sel"] = sel
    d["wq"] = g["L1_attn_Wq"]
    kv = g["L1_attn_Wkv"].reshape(D, 8, 2, 32)
    d["wk"] = kv[:, :, 0].reshape(D, 256)
    d["wv"] = kv[:, :, 1].reshape(D, 256)
    d["wo"] = g["L1_attn_Wo"]
    d["bo"] = g["L1_attn_bo"]
    d["worgT"] = g["L1_ffn_W_org"].T
    d["dnT"] = g["L1_ffn_lora_down"].transpose(0, 2, 1).reshape(512, D)
    d["up"] = g["L1_ffn_lora_up"].reshape(512, D)
    d["keyT"] = g["L1_ffn_lora_keys"].T
    d["lwqT"] = g["L1_ffn_Wq"].T
    return {n: np.ascontiguousarray(a) for n, a in d.items()}


def kernel(**inputs):
    import concourse.bacc as bacc
    from concourse.bass_utils import run_bass_kernel_spmd as run

    nc = bacc.Bacc("TRN2", target_bir_lowering=False, num_devices=1, dynamic_dma_scratch_size=1024)
    arrays = lay_out(inputs)
    io = {n: nc.dram_tensor("in_" + n, a.shape, mybir.dt.from_np(a.dtype), kind="ExternalInput").ap()
          for n, a in arrays.items()}
    out = nc.dram_tensor("out_0", (2048, D), F32, kind="ExternalOutput").ap()
    program(nc, io, out)
    r = run(nc, [{"in_" + n: a for n, a in arrays.items()}], core_ids=[0])
    return r.results[0]["out_0"].reshape(2, 1024, D)
```

```python
from contextlib import ExitStack

import numpy as np
import concourse.bass as bass
from concourse import mybir

F32 = mybir.dt.float32
F32R = mybir.dt.float32r
ACT = mybir.ActivationFunctionType
ALU = mybir.AluOpType
AX = mybir.AxisListType.X

STAGES = "ABCD"
NT = 16
D = 1024
EPS = 1e-5
FH = 2752
VECS = {}
_at = 0
for _n, _w in (("bin", 1), ("ln1w", 4), ("ln1b", 4), ("pre", 4), ("pim", 4), ("lre", 4), ("lim", 4),
               ("scl", 4), ("ln2w", 4), ("ln2b", 4), ("b1", 16), ("b2", 4), ("lnlw", 1), ("lnlb", 1)):
    VECS[_n] = _at
    _at += _w
NVEC = _at


class Prog:

    def __init__(self, nc, ctx):
        self.nc = nc
        self.ctx = ctx
        self.q = {e: [] for e in ("pe", "act", "dve", "pool", "sp")}
        self.sem = {e: ctx.enter_context(nc.semaphore("s_" + e)) for e in ("pe", "act", "dve", "pool")}
        self.n = {e: 0 for e in self.sem}
        self.seen = {e: {} for e in self.q}

    def wait(self, e, waits):
        for w in flat(waits):
            k, v = w
            if self.seen[e].get(k, 0) < v:
                self.seen[e][k] = v
                self.q[e].append(("w", self.sem[k], v))

    def op(self, e, fn, waits=(), inc=True):
        self.wait(e, waits)
        if inc:
            self.n[e] += 1
            self.q[e].append(("i", fn, self.sem[e], 1))
            return (e, self.n[e])
        self.q[e].append(("i", fn, None, 0))
        return None

    def last(self, e):
        return (e, self.n[e])

    def dma(self, ch, out, in_, waits=()):
        k = ch.names[ch.i % len(ch.names)]
        ch.i += 1
        self.wait("sp", [(k, self.n[k])] if self.n[k] else [])
        self.wait("sp", waits)
        self.n[k] += 16
        self.q["sp"].append(("i", lambda: self.nc.sync.dma_start(out, in_), self.sem[k], 16))
        return (k, self.n[k])

    def channel(self, name, n):
        return Channel(self, name, n)

    def barrier(self):
        toks = [(k, v) for k, v in self.n.items() if v]
        for e in self.q:
            self.wait(e, toks)

    def run(self, block):
        def play(eng, items):
            for it in items:
                if it[0] == "w":
                    eng.wait_ge(it[1], it[2])
                else:
                    ins = it[1]()
                    if it[2] is not None:
                        ins.then_inc(it[2], it[3])

        @block.sync
        def _(e):
            play(e, self.q["sp"])

        @block.tensor
        def _(e):
            play(e, self.q["pe"])

        @block.scalar
        def _(e):
            play(e, self.q["act"])

        @block.vector
        def _(e):
            play(e, self.q["dve"])

        @block.gpsimd
        def _(e):
            play(e, self.q["pool"])


class Channel:
    def __init__(self, p, name, n):
        self.names = [f"{name}{i}" for i in range(n)]
        self.i = 0
        for k in self.names:
            p.sem[k] = p.ctx.enter_context(p.nc.semaphore("s_" + k))
            p.n[k] = 0


def flat(w):
    if w is None:
        return
    if isinstance(w, tuple) and len(w) == 2 and isinstance(w[0], str):
        yield w
        return
    for x in w:
        yield from flat(x)


class Ring:

    def __init__(self, bufs):
        self.bufs = bufs
        self.i = 0
        self.busy = [[] for _ in bufs]

    def get(self):
        i = self.i % len(self.bufs)
        assert self.i < len(self.bufs) or self.busy[i], "its readers aren't known yet"
        self.i += 1
        w, self.busy[i] = self.busy[i], []
        return i, self.bufs[i], w

    def free(self, i, toks):
        self.busy[i].append(toks)


class Banks:

    def __init__(self, first, n):
        self.first, self.n, self.at = first, n, 0
        self.busy = [[] for _ in range(n)]

    def get(self, k):
        if self.at + k > self.n:
            self.at = 0
        i = self.at
        self.at = (i + k) % self.n
        w = [self.busy[q] for q in range(i, i + k)]
        assert None not in w, "its readers aren't known yet"
        for q in range(i, i + k):
            self.busy[q] = None
        return (i, k), self.first + i, w

    def can(self, k):
        i = 0 if self.at + k > self.n else self.at
        return None not in self.busy[i:i + k]

    def free(self, run, toks):
        for q in range(run[0], run[0] + run[1]):
            self.busy[q] = [toks]


class K:
    def __init__(self, nc, ctx, io, out):
        self.nc, self.io, self.out = nc, io, out
        self.p = Prog(nc, ctx)
        self.PS = ctx.enter_context(nc.psum_tensor("PS", [128, 4096], F32))
        self.cst = ctx.enter_context(nc.sbuf_tensor("cst", [128, 256 + 128 + 128 + 8], F32))
        self.ident = self.cst[:, 0:128]
        self.cmat = self.cst[:, 128:256]
        self.mask = self.cst[:, 256:384]
        self.ones = self.cst[:, 384:512]
        self.onediv = self.cst[:, 512:513]
        self.small = ctx.enter_context(nc.sbuf_tensor("small", [128, 8, 24], F32))
        self.mhalf = ctx.enter_context(nc.sbuf_tensor("mhalf", [128, 16], F32))
        self.ld = self.p.channel("ld", 6)
        self.st = self.p.channel("st", 6)
        self.wl = self.p.channel("wl", 6)
        self.t_c = self.p.dma(self.ld, self.cst[:, :], io["cst"])
        self.t_mh = self.dve(lambda: nc.vector.memset(self.mhalf[:, :], -0.5))
        self.smr = Ring(list(range(8)))
        self.scr = [nc.dram_tensor(f"scr{i}", (NT * 128, D), F32, kind="Internal").ap() for i in range(7)]
        self.sum_d = nc.dram_tensor("sum_d", (64, 1024), F32, kind="Internal").ap()
        self.rec_d = nc.dram_tensor("rec_d", (64, 1024), F32, kind="Internal").ap()
        self.ctxT = nc.dram_tensor("ctxT", (D, NT * 128), F32, kind="Internal").ap()

    def bank(self, b, n=1):
        return self.PS[:, 512 * b:512 * (b + n)]

    def pe(self, fn, w=(), inc=False):
        return self.p.op("pe", fn, w, inc)

    def act(self, fn, w=()):
        return self.p.op("act", fn, w)

    def dve(self, fn, w=()):
        return self.p.op("dve", fn, w)

    def pool(self, fn, w=()):
        return self.p.op("pool", fn, w)

    def mm(self, out, l, r, start, stop, w=(), inc=False, skip=False):
        nc = self.nc
        if skip:
            return self.pe(lambda: nc.tensor.matmul(out, l, r, start=start, stop=stop, skip_group_check=True), w, inc)
        return self.pe(lambda: nc.tensor.matmul(out, l, r, start=start, stop=stop), w, inc)

    def tr(self, out, in_, w=(), inc=False):
        nc = self.nc
        n = in_.shape[0]
        return self.pe(lambda: nc.tensor.transpose(out, in_, self.ident[0:n, 0:n]), [w, self.t_c], inc)

    def af(self, out, in_, func, w=(), scale=None, bias=None):
        nc = self.nc
        kw = {}
        if scale is not None:
            kw["scale"] = scale
        if bias is not None:
            kw["bias"] = bias
        return self.act(lambda: nc.scalar.activation(out, in_, func, **kw), w)

    def tt(self, out, a, b, op, w=(), e="dve"):
        nc = self.nc
        en = nc.vector if e == "dve" else nc.gpsimd
        return self.p.op(e, lambda: en.tensor_tensor(out, a, b, op), w)

    def ts(self, out, a, s1, s2, op0, op1=None, w=()):
        nc = self.nc
        if op1 is None:
            return self.dve(lambda: nc.vector.tensor_scalar(out, a, s1, None, op0), w)
        return self.dve(lambda: nc.vector.tensor_scalar(out, a, s1, s2, op0, op1), w)

    def stt(self, out, a, s, b, op0, op1, w=()):
        nc = self.nc
        return self.dve(lambda: nc.vector.scalar_tensor_tensor(out=out, in0=a, scalar=s, in1=b, op0=op0, op1=op1), w)

    def copy(self, out, in_, w=(), e="dve"):
        nc = self.nc
        if e == "act":
            return self.act(lambda: nc.scalar.copy(out, in_), w)
        en = nc.vector if e == "dve" else nc.gpsimd
        return self.p.op(e, lambda: en.tensor_copy(out, in_), w)

    def split(self, h, l, src, w=(), e="act"):
        a = self.copy(h, src, w, e)
        b = self.tt(l, src, h.bitcast(F32), ALU.subtract, [w, a])
        return [a, b]

    def load_split(self, h, l, dram, ring, w=()):
        i, buf, fr = ring.get()
        n, m = h.shape[0], h.shape[-1]
        s = buf[0:n, 0:m]
        t = self.p.dma(self.wl, s, dram, fr)
        r = self.split(h, l, s, [t, w])
        ring.free(i, r)
        return r

    def stats(self, src, w):
        nc = self.nc
        i, k, fr = self.smr.get()
        s = self.small[:, k, :]
        a = self.dve(lambda: nc.vector.bn_stats(s[:, 0:6], src[:, 0:512]), [w, fr])
        b = self.dve(lambda: nc.vector.bn_stats(s[:, 6:12], src[:, 512:1024]), w)
        c = self.dve(lambda: nc.vector.bn_aggr(s[:, 12:14], s[:, 0:12]), [a, b])
        d = self.ts(s[:, 14:15], s[:, 13:14], EPS, None, ALU.add, w=[c])
        e = self.tt(s[:, 15:16], s[:, 14:15], self.mhalf[:, 0:1], ALU.pow, [d, self.t_mh], e="pool")
        return {"i": i, "s": s, "mean": c, "rs": e, "st": b}

    def normalize(self, out, src, q, w=()):
        s = q["s"]
        n = self.stt(s[:, 16:17], s[:, 12:13], -1.0, s[:, 15:16], ALU.mult, ALU.mult, [q["rs"], q["mean"]])
        t = self.af(out, src, ACT.Identity, [w, n, q["rs"]], scale=s[:, 15:16], bias=s[:, 16:17])
        self.smr.free(q["i"], t)
        return t

    def load_bias(self, bias, ones, buf, dram, w=()):
        nc = self.nc
        t = self.p.dma(self.wl, buf, dram.partition_broadcast(64), w)
        z = self.dve(lambda: nc.vector.memset(bias[:, :].bitcast(F32), 0.0))
        o = self.dve(lambda: nc.vector.memset(ones[:, :].bitcast(F32), 1.0))
        a = self.copy(bias[0:1, :], buf[0:1, :], [t, z])
        b = self.copy(bias[32:33, :], buf[32:33, :], [t, z])
        c = self.tt(bias[32:33, :], buf[32:33, :], bias[32:33, :].bitcast(F32), ALU.subtract, [b])
        return [a, c, o]

    def tail_steps(self, t, y, ytok, free_y, xring, yring, x_src, x_dst, xn_dst, hook=None, x_tok=None,
                   adder="dve"):
        S = {}
        rows = slice(128 * t, 128 * t + 128)

        def s1():
            S["xi"], S["x"], fr = xring.get()
            S["xl"] = self.p.dma(self.ld, S["x"][:, :], x_src[rows, :], [fr, x_tok])
            S["yi"], S["yn"], S["yf"] = yring.get()
            S["q"] = self.stats(y, ytok)

        def s2():
            a = self.normalize(S["yn"][:, :], y, S["q"], [S["yf"]])
            free_y([a, S["q"]["st"]])
            b = self.tt(S["x"][:, :], S["x"][:, :], S["yn"][:, :], ALU.add, [a, S["xl"]], e=adder)
            S["b"] = b
            S["xs"] = self.p.dma(self.st, x_dst[rows, :], S["x"][:, :], b)
            if xn_dst is None:
                xring.free(S["xi"], [S["xs"]])
                yring.free(S["yi"], [b])

        def s3():
            S["q"] = self.stats(S["x"][:, :], S["b"])

        def s4():
            a = self.normalize(S["yn"][:, :], S["x"][:, :], S["q"], [S["b"]])
            c = self.p.dma(self.st, xn_dst[rows, :], S["yn"][:, :], a)
            h = hook(t, S["yn"], a) if hook else None
            xring.free(S["xi"], [S["xs"], a, S["q"]["st"]])
            yring.free(S["yi"], [c, h])
            self.done_xn[t] = c
            self.done_x[t] = S["xs"]

        if xn_dst is None:
            return [s1, s2]
        return [s1, s2, s3, s4]


def pipeline(items, lags=None):
    n = len(items)
    k = max(len(x) for x in items)
    for i in range(n + k):
        for s in reversed(range(k)):
            j = i - s
            if 0 <= j < n and s < len(items[j]):
                items[j][s]()


def stage_a(k, x_src, x_dst, xn_dst):
    nc, p, io = k.nc, k.p, k.io
    with ExitStack() as ctx:
        def sb(name, shape, dt=F32):
            return ctx.enter_context(nc.sbuf_tensor("a_" + name, shape, dt))

        win_h, win_l = sb("winh", [128, 8, 128], F32R), sb("winl", [128, 8, 128], F32R)
        h = sb("h", [128, 2048])
        vec = sb("vec", [128, NVEC])
        w1 = sb("w1", [128, 4, 512])
        w2 = sb("w2", [128, 4, 4, 128])
        wout = sb("wout", [128, 1024])
        bout, one = sb("bout", [64, 1024], F32R), sb("one", [64, 128], F32R)
        cosT, sinT = sb("cosT", [128, 4, 1024]), sb("sinT", [128, 4, 1024])
        sm = sb("sm", [128, 20, 4])
        xin = Ring([sb(f"xin{i}", [128, 1024]) for i in range(4)])

        t_vec = p.dma(k.wl, vec[:, :], io["vecs"])
        buf = xin.bufs[3]
        t = p.dma(k.wl, buf[:, :].rearrange("p (c n) -> p c n", c=8), io["winT"].rearrange("(c p) n -> p c n", p=128))
        t_win = k.split(win_h[:, :, :], win_l[:, :, :], buf[:, :].rearrange("p (c n) -> p c n", c=8), t)
        xin.busy[3] = [t_win]

        def V(name, i=0):
            c = VECS[name] + i
            return vec[:, c:c + 1]

        def V4(name):
            return vec[:, VECS[name]:VECS[name] + 4]

        r2, t0, z0, rinv, r, rho, c0, s0, i1, i2, t1, t2 = (sm[:, n, :] for n in range(12))
        M, A_, S_ = ALU.mult, ALU.add, ALU.subtract
        a = k.tt(r2, V4("pre"), V4("pre"), M, t_vec)
        b = k.tt(t0, V4("pim"), V4("pim"), M, t_vec)
        a = k.tt(r2, r2, t0, A_, [a, b])
        z = k.ts(z0, r2, 0.0, None, ALU.is_equal, w=a)
        b = k.ts(t0, r2, 1e-37, None, ALU.max, w=a)
        rv = k.tt(rinv, t0, k.mhalf[:, 0:4], ALU.pow, [b, k.t_mh], e="pool")
        a = k.tt(r, r2, rinv, M, [rv, a])
        t_rho = k.af(rho, r, ACT.Tanh, a)
        a = k.tt(t1, V4("pre"), rinv, M, rv)
        c_ = k.tt(c0, t1, z0, A_, [a, z])
        s_ = k.tt(s0, V4("pim"), rinv, M, rv)
        a = k.tt(t1, c0, V4("lre"), M, [c_])
        b = k.tt(t2, s0, V4("lim"), M, s_)
        t_i1 = k.tt(i1, t1, t2, S_, [a, b])
        a = k.tt(t1, s0, V4("lre"), M, [t_i1])
        b = k.tt(t2, c0, V4("lim"), M, t_i1)
        a = k.tt(t1, t1, t2, A_, [a, b])
        t_i2 = k.ts(i2, t1, -1.0, None, M, w=a)

        tmp = sb("tmp", [128, 2, 2, 512])
        e = [sm[:, 12 + n, :] for n in range(4)]
        first = [k.dve(lambda: nc.vector.memset(cosT[:, :, 0:1], 1.0)), k.dve(lambda: nc.vector.memset(sinT[:, :, 0:1], 0.0))]
        tabs = {}

        def table(level):
            n = 1 << level
            cn, sn = (c0, s0) if level == 0 else (e[0], e[1])
            w = [tabs.get("e"), tabs.get("t"), first, c_, s_]
            last = []
            for l0 in (0, 2):
                uv = []
                for l in (l0, l0 + 1):
                    f = tabs.get(("u", l % 2))
                    uv.append((k.ts(tmp[:, l % 2, 0, 0:n], sinT[:, l, 0:n], sn[:, l:l + 1], None, M, w=[w, f]),
                               k.ts(tmp[:, l % 2, 1, 0:n], cosT[:, l, 0:n], sn[:, l:l + 1], None, M, w=[w, f])))
                for l in (l0, l0 + 1):
                    u, v = uv[l % 2]
                    a = k.stt(cosT[:, l, n:2 * n], cosT[:, l, 0:n], cn[:, l:l + 1], tmp[:, l % 2, 0, 0:n], M, S_, [u, w])
                    b = k.stt(sinT[:, l, n:2 * n], sinT[:, l, 0:n], cn[:, l:l + 1], tmp[:, l % 2, 1, 0:n], M, A_, [v, w])
                    tabs["u", l % 2] = [a, b]
                    last += [a, b]
            tabs["t"] = last
            if level < 9:
                a = k.tt(e[2], cn, cn, M, [w, last])
                b = k.tt(e[3], sn, sn, M, [w, last])
                c = k.tt(t2, cn, sn, M, [w, last, t_i2])
                d = k.tt(e[0], e[2], e[3], S_, [a, b, c])
                f = k.ts(e[1], t2, 2.0, None, M, w=[c, b])
                tabs["e"] = [d, f]

        xT_ring = Ring([(sb(f"xth{i}", [128, 8, 512], F32R), sb(f"xtl{i}", [128, 8, 512], F32R)) for i in range(1)])
        trb = Ring([0, 2])
        hb = Ring([4, 5])
        G = {}
        h_tok = []

        def a0(t):
            S = {}

            def s0_():
                S["i"], S["x"], fr = xin.get()
                ld = p.dma(k.ld, S["x"][:, :], x_src[128 * t:128 * t + 128, :], fr)
                S["q"] = k.stats(S["x"][:, :], ld)
                if t < 10:
                    table(t)

            def s1n():
                S["a"] = k.normalize(S["x"][:, :], S["x"][:, :], S["q"], [S["q"]["st"]])

            def s1_():
                a = S["a"]
                bi, b, fr = trb.get()
                for c in range(8):
                    m = k.tr(k.PS[:, 512 * b + 128 * c:512 * b + 128 * c + 128], S["x"][:, 128 * c:128 * c + 128],
                             [a, fr], inc=c % 4 == 3)
                xin.free(S["i"], m)
                if t % 4 == 0:
                    G["i"], G["b"], G["f"] = xT_ring.get()
                    G["w"] = []
                xh, xl = G["b"]
                cols = slice(128 * (t % 4), 128 * (t % 4) + 128)
                w = k.split(xh[:, :, cols], xl[:, :, cols], k.bank(b, 2).rearrange("p (c n) -> p c n", c=8), [m, G["f"]])
                trb.free(bi, w)
                G["w"] = [G["w"], w]

            def s2_():
                if t % 4 != 3:
                    return
                g = t // 4
                xh, xl = G["b"]
                hi, b, fr = hb.get()
                o = k.bank(b)
                for c in range(8):
                    k.mm(o, win_h[:, c, :], xh[:, c, :], c == 0, False, [G["w"], fr, t_win])
                    k.mm(o, win_h[:, c, :], xl[:, c, :], False, False)
                    m = k.mm(o, win_l[:, c, :], xh[:, c, :], False, c == 7, inc=c == 7)
                xT_ring.free(G["i"], m)
                r = k.af(h[:, 512 * g:512 * g + 512], o, ACT.Identity, [m, t_vec], bias=V("bin"))
                hb.free(hi, r)
                h_tok.append(r)
            return [s0_, s1n, s1_, s2_]

        pipeline_a0 = [a0(t) for t in range(NT)]
        for i in range(NT + 2):
            if i < NT:
                pipeline_a0[i][0]()
            if 1 <= i <= NT:
                pipeline_a0[i - 1][1]()
            if i >= 2:
                pipeline_a0[i - 2][2]()
                pipeline_a0[i - 2][3]()

        t_w1 = p.dma(k.wl, w1[:, :, :], io["w1T"].rearrange("l p n -> p l n"))
        t_w2 = [p.dma(k.wl, w2[:, l, :, :], io["w2T"][l].rearrange("(c p) n -> p c n", p=128)) for l in range(4)]
        t_wo = p.dma(k.wl, wout[:, :], io["woutT"])
        ST = range(4)
        W = [{n: sb(f"{n}{q}", [128, 512]) for n in ("sq", "cs", "y", "a1", "SA", "SB")} for q in ST]
        hid = [sb(f"hid{q}", [128, 4, 512]) for q in ST]
        vs = sb("vs", [128, 4, 8])
        boot = [k.p.last("act"), k.p.last("dve"), k.p.last("pe")]
        T = [{"h": h_tok[q], "b0": boot, "b1": boot} for q in ST]
        carry = {}

        def ln_steps(q, wv, bv, func):
            X, w = T[q], W[q]
            B0 = 2 * q
            hc = h[:, 512 * q:512 * q + 512]

            def center():
                X["m"] = k.mm(k.bank(B0), k.cmat, hc, True, True, [X["h"], X["b0"], k.t_c], inc=True)

            def square():
                X["sq"] = k.af(w["sq"][:, :], k.bank(B0), ACT.Square, [X["m"], X.get("sqf")])

            def keep():
                X["cs"] = k.copy(w["cs"][:, :], k.bank(B0), [X["m"], X.get("csf")], e="act")

            def var():
                for t in range(4):
                    m = k.mm(k.PS[:, 512 * B0 + t:512 * B0 + t + 1], w["sq"][:, 128 * t:128 * t + 128], k.onediv,
                             True, True, [X["sq"], X["cs"]], inc=t == 3)
                X["m"] = X["sqf"] = m

            def eps():
                X["v"] = X["b0"] = k.ts(vs[:, q, 0:4], k.PS[:, 512 * B0:512 * B0 + 4], EPS, None, ALU.add, w=[X["m"], X.get("rs")])

            def power():
                X["rs"] = k.tt(vs[:, q, 4:8], vs[:, q, 0:4], k.mhalf[:, 0:4], ALU.pow, [X["v"], k.t_mh, X.get("rsf")], e="pool")

            def spread():
                for t in range(4):
                    o = 512 * (B0 + 1) + 128 * t
                    m = k.mm(k.PS[:, o:o + 128], vs[:, q, 4 + t:5 + t].broadcast_to([128, 128]), k.ident,
                             True, True, [X["rs"], X["b1"]], inc=t == 3)
                X["m"] = X["rsf"] = m

            def scale():
                X["tt"] = X["b1"] = k.tt(w["cs"][:, :], w["cs"][:, :], k.bank(B0 + 1), M, [X["m"], X["cs"]])

            def affine():
                X["y"] = X["csf"] = k.af(w["y"][:, :], w["cs"][:, :], func, [X["tt"], X.get("yf"), t_vec], scale=wv, bias=bv)
            return [("pe", .85, center), ("act", .6, square), ("act", .6, keep), ("pe", .85, var), ("dve", .15, eps),
                    ("pool", .9, power), ("pe", .85, spread), ("dve", .6, scale), ("act", .65, affine)]

        def conv_steps(q, l):
            X, w = T[q], W[q]
            b, half = q // 2, q % 2
            hc = h[:, 512 * q:512 * q + 512]
            ts = slice(512 * half, 512 * half + 512)

            def inputs():
                X["u1"] = k.tt(w["a1"][:, :], w["y"][:, :], cosT[:, l, ts], M, [X["y"], tabs["t"], X.get("a1f")])
                X["u2"] = k.tt(w["cs"][:, :], w["y"][:, :], sinT[:, l, ts], M, [X["y"], tabs["t"], X.get("csf")])
                X["yf"] = [X["u1"], X["u2"]]

            def scans():
                rb = rho[:, l:l + 1].broadcast_to([128, 512])
                if half == 0:
                    n1, n2, t1_, t2_ = i1[:, l:l + 1], i2[:, l:l + 1], t_i1, [t_i2, carry.get(("done", q + 1))]
                else:
                    P = W[q - 1]
                    n1, n2 = P["SA"][:, 511:512], P["SB"][:, 511:512]
                    t1_, t2_ = carry["s", q - 1]
                q1 = k.dve(lambda: nc.vector.tensor_tensor_scan(w["SA"][:, :], rb, w["a1"][:, :], n1, M, A_),
                           [X["u1"], t1_, t2_, t_rho, X.get("Sf")])
                q2 = k.dve(lambda: nc.vector.tensor_tensor_scan(w["SB"][:, :], rb, w["cs"][:, :], n2, M, A_),
                           [X["u2"], t1_, t2_, t_rho, X.get("Sf")])
                carry["s", q] = (q1, q2)
                carry["done", q] = [q1, q2]
                X["csf"] = q2
                X["q"] = (q1, q2)

            def outputs():
                q1, q2 = X["q"]
                u1 = k.tt(w["sq"][:, :], w["SA"][:, :], cosT[:, l, ts], M, [q1, X["sqf"]])
                u2 = k.tt(w["a1"][:, :], w["SB"][:, :], sinT[:, l, ts], M, [q2])
                u3 = k.tt(w["sq"][:, :], w["sq"][:, :], w["a1"][:, :], A_, [u1, u2])
                X["Sf"] = [u1, u2]
                X["a1f"] = u3
                X["h"] = X["sqf"] = k.stt(hc, w["sq"][:, :], V("scl", l), hc, M, A_, [u3, X["h"]])
            need = ("conv", q - 1, l) if half else ("conv", q + 1, l - 1)
            return [("dve", 1.3, inputs), ("dve", 1.4, scans, need, ("conv", q, l)), ("dve", 2.5, outputs)]

        def mlp_steps(q, l):
            X, w = T[q], W[q]
            B0 = 2 * q
            hc = h[:, 512 * q:512 * q + 512]

            def up(m):
                def f():
                    X["m", m] = X["yf"] = k.mm(k.bank(B0 + m % 2), w1[:, l, 128 * m:128 * m + 128], w["y"][:, :], True, True,
                                               [X["y"], X["b%d" % (m % 2)], t_w1], inc=True)
                return f

            def act(m):
                def f():
                    X["b%d" % (m % 2)] = X["g", m] = k.af(hid[q][:, m, :], k.bank(B0 + m % 2), ACT.Silu,
                                                         [X["m", m], X.get("hf"), t_vec], bias=V("b1", 4 * l + m))
                return f

            def down():
                for m in range(4):
                    r = k.mm(k.bank(B0), w2[:, l, m, :], hid[q][:, m, :], m == 0, m == 3,
                             [X["g", m], X["b0"], t_w2], inc=m == 3)
                X["hf"] = r

            def add():
                X["h"] = X["b0"] = k.stt(hc, k.bank(B0), V("b2", l), hc, A_, A_, [X["hf"], X["h"]])
            r = [("pe", .85, up(0)), ("pe", .85, up(1))]
            for m in range(4):
                r.append(("act", .65, act(m)))
                if m < 2:
                    r.append(("pe", .85, up(m + 2)))
            return r + [("pe", 3.4, down), ("dve", .6, add)]

        streams = []
        for q in ST:
            s = []
            for l in range(4):
                s += ln_steps(q, V("ln1w", l), V("ln1b", l), ACT.Silu)
                s += conv_steps(q, l)
                s += ln_steps(q, V("ln2w", l), V("ln2b", l), ACT.Identity)
                s += mlp_steps(q, l)
            s += ln_steps(q, V("lnlw"), V("lnlb"), ACT.Identity)
            streams.append(s)
        ready, at, free = [0.0] * 4, [0] * 4, {}
        emitted = {("conv", q, -1) for q in range(4)}
        while any(at[q] < len(streams[q]) for q in ST):
            best = None
            for q in ST:
                if at[q] < len(streams[q]):
                    st = streams[q][at[q]]
                    if len(st) > 3 and st[3] not in emitted:
                        continue
                    start = max(ready[q], free.get(st[0], 0.0))
                    if best is None or (start, -at[q]) < best[:2]:
                        best = (start, -at[q], q, st)
            start, _, q, st = best
            st[2]()
            free[st[0]] = start + st[1]
            ready[q] = start + st[1] + 0.3
            if len(st) > 4:
                emitted.add(st[4])
            at[q] += 1

        yb = Ring([0, 2, 4, 6])
        for q in ST:
            yb.free(q, [T[q]["b0"], T[q]["b1"]])
        xr = xin
        yr = Ring([hid[q][:, 0:2, :].rearrange("p a n -> p (a n)") for q in range(3)])
        for q in range(3):
            yr.free(q, T[q]["hf"])
        t_bo = k.load_bias(bout, one, hid[3][0:64, 0:2, :].rearrange("p a n -> p (a n)"), io["bout"], T[3]["hf"])

        def item(t):
            S = {}

            def mmul():
                S["i"], b, fr = yb.get()
                q, c = t // 4, 128 * (t % 4)
                for s in range(2):
                    cs = slice(512 * s, 512 * s + 512)
                    k.mm(k.bank(b + s), one[:, :], bout[:, cs], True, False, [fr, t_bo])
                    m = k.mm(k.bank(b + s), W[q]["y"][:, c:c + 128], wout[:, cs], False, True,
                             [T[q]["y"], t_wo], inc=s == 1)
                S["steps"] = k.tail_steps(t, k.bank(b, 2), m, lambda toks: yb.free(S["i"], toks), xr, yr, x_src, x_dst, xn_dst,
                                          adder="pool")
            n_ = 4 if xn_dst is not None else 2
            return [mmul] + [(lambda j=j: S["steps"][j]()) for j in range(n_)]
        pipeline([item(t) for t in range(NT)])


def stage_b(k, x_src, xn_src, x_dst, xn_dst):
    nc, p, io = k.nc, k.p, k.io
    with ExitStack() as ctx:
        def sb(name, shape, dt=F32):
            return ctx.enter_context(nc.sbuf_tensor("b_" + name, shape, dt))

        w13h = sb("w13h", [128, 2, 2, FH], F32R)
        w13l = sb("w13l", [128, 2, 2, FH], F32R)
        bx = sb("bx", [96, FH], F32R)
        w2h, w2l = sb("w2h", [128, 6, 1024], F32R), sb("w2l", [128, 6, 1024], F32R)
        a13 = sb("a13", [128, 8, 32])
        a2 = sb("a2", [128, 24, 32])
        sel = sb("sel", [128, 3, 96])
        xnb = [sb(f"xn{i}", [128, 1024]) for i in range(2)]
        xr = Ring([sb(f"x{i}", [128, 1024]) for i in range(2)])
        yr = Ring([sb(f"y{i}", [128, 1024]) for i in range(2)])
        xT = sb("xT", [128, 8, 128])
        xsh, xsl = sb("xsh", [128, 2, 2, 256], F32R), sb("xsl", [128, 2, 2, 256], F32R)
        xs = sb("xs", [128, 2, 128])
        usb = sb("usb", [128, 256])
        ux = sb("ux", [96, 2, 2, 256], F32R)
        ur = sb("ur", [96, 2, 256], F32R)
        gr = Ring([sb(f"g{i}", [128, 2, 256]) for i in range(4)])
        ga = sb("ga", [128, 2, 256])
        gf = sb("gf", [128, 256])
        gfh, gfl = sb("gfh", [128, 6, 256], F32R), sb("gfl", [128, 6, 256], F32R)
        u2 = sb("u2", [128, 256])

        t_a13 = p.dma(k.wl, a13[:, :, :], io["a13T"].rearrange("(c p) n -> p c n", p=128))
        t_sel = p.dma(k.wl, sel[:, :, :], io["sel"])
        t_a2 = []
        for r in range(6):
            n = 128 if r < 5 else 48
            t_a2.append(p.dma(k.wl, a2[0:n, 4 * r:4 * r + 4, :],
                              io["a2T"].rearrange("(j q) n -> q j n", q=688)[128 * r:128 * r + n, :, :]))
        stage = Ring([xr.bufs[0], xr.bufs[1], yr.bufs[0], yr.bufs[1]])
        t_w = {}
        zero = [k.dve(lambda: nc.vector.memset(gfh[:, 5, :].bitcast(F32), 0.0)),
                k.dve(lambda: nc.vector.memset(gfl[:, 5, :].bitcast(F32), 0.0))]
        V4 = lambda a: a.rearrange("p c (j q) -> p c j q", q=688)

        def w13_piece(r, v):
            n = 128 if r < 5 else 48
            i, buf, fr = stage.get()
            b4 = buf[:, 0:8 * n].rearrange("p (c j q) -> p c j q", c=2, j=4)
            t = [p.dma(k.wl, b4[:, c, :, :],
                       io["w13T"][v, 128 * c:128 * c + 128, :].rearrange("p (j q) -> p j q", q=688)[:, :, 128 * r:128 * r + n],
                       fr) for c in range(2)]
            a = k.split(V4(w13h[:, v, :, :])[:, :, :, 128 * r:128 * r + n], V4(w13l[:, v, :, :])[:, :, :, 128 * r:128 * r + n], b4, t)
            stage.free(i, a)
            t_w.setdefault(r, []).append(a)

        def bx_piece(r):
            n = 128 if r < 5 else 48
            i, buf, fr = stage.get()
            view = lambda a: a.rearrange("p (j q) -> p j q", q=688)[:, :, 128 * r:128 * r + n]
            b3 = buf[0:96, 0:4 * n].rearrange("p (j q) -> p j q", j=4)
            t = p.dma(k.wl, b3, view(io["bx"]), fr)
            bx3 = view(bx[:, :])
            a = k.copy(bx3, b3, t, e="act")
            b = k.tt(bx3[32:64], b3[32:64], bx3[32:64].bitcast(F32), ALU.subtract, [a])
            stage.free(i, [a, b])
            t_w.setdefault(r, []).append([a, b])

        t_dn = []
        wpieces = []
        for r in range(6):
            wpieces += [lambda r=r: w13_piece(r, 0), lambda r=r: w13_piece(r, 1), lambda r=r: bx_piece(r)]
        for c in range(6):
            wpieces.append(lambda c=c: t_dn.append(k.load_split(w2h[:, c, :], w2l[:, c, :],
                                                                io["w2x"][128 * c:128 * c + 128, :], stage)))

        def wnext(n):
            for _ in range(min(n, len(wpieces))):
                wpieces.pop(0)()
                if not wpieces:
                    for i in range(2):
                        xr.busy[i], yr.busy[i] = stage.busy[i], stage.busy[2 + i]

        NB = 8
        gbanks = Ring([0, 2])
        misc_free = [None]
        y_free = [None]
        XS = {}

        def prep(n):
            steps = []
            S = {"x": [], "w": []}
            par = n % 2

            def load():
                for i in range(2):
                    t = 2 * n + i
                    S["x"].append(p.dma(k.ld, xnb[i][:, :], xn_src[128 * t:128 * t + 128, :], [XS.get(("f", i)), k.done_xn[t]]))
            steps.append(load)

            def trans(i, hf):
                def f():
                    o = k.bank(5)
                    for c in range(4):
                        cc = 4 * hf + c
                        m = k.tr(o[:, 128 * c:128 * c + 128], xnb[i][:, 128 * cc:128 * cc + 128],
                                 [S["x"][i], misc_free[0]], inc=c == 3)
                    if hf == 1:
                        XS["f", i] = m
                    a = k.copy(xT[:, 4 * hf:4 * hf + 4, :], o.rearrange("p (c n) -> p c n", c=4), [m, XS.get("xTf")], e="act")
                    misc_free[0] = a
                    S["xT", hf] = a
                return f

            def fold(i):
                def f():
                    w = [S["xT", 0], S["xT", 1]]
                    o = k.bank(5)
                    for c in range(8):
                        g = c % 4
                        m = k.mm(o[32 * g:32 * g + 32, 0:128], a13[:, c, :], xT[:, c, :],
                                 c < 4, c >= 4, [w, misc_free[0], t_a13], inc=c == 7, skip=True)
                    a = k.copy(usb[:, 128 * i:128 * i + 128], o[:, 0:128], [m, XS.get("uf")], e="act")
                    misc_free[0] = a
                    S["u", i] = a
                    v = xT[:, :, :].rearrange("p (j c) n -> p j c n", c=2)
                    a = k.tt(xs[:, :, :], v[:, 0], v[:, 1], ALU.add, [w, XS.get("xsf")])
                    a = k.tt(xs[:, :, :], xs[:, :, :], v[:, 2], ALU.add, [a])
                    a = k.tt(xs[:, :, :], xs[:, :, :], v[:, 3], ALU.add, [a])
                    XS["xTf"] = [a, m]
                    cols = slice(128 * i, 128 * i + 128)
                    r = k.split(xsh[:, par, :, cols], xsl[:, par, :, cols], xs[:, :, :], [a, XS.get(("xsf", par))])
                    XS["xsf"] = r
                    S["w"].append(r)
                return f

            def low():
                o = k.bank(5)
                for v in range(2):
                    m = k.mm(o[0:96, 256 * v:256 * v + 256], sel[:, v, :], usb[:, :], True, True,
                             [S["u", 0], S["u", 1], misc_free[0], t_sel], inc=v == 1)
                XS["uf"] = m
                o3 = o.rearrange("p (v n) -> p v n", v=2)
                wf = [m, XS.get(("xsf", par))]
                a = k.copy(ux[0:64, par, :, :], o3[0:64], wf, e="act")
                b = k.copy(ur[64:96, :, :], o3[64:96], [m, XS.get("urf")], e="act")
                c = k.tt(ux[64:96, par, :, :], o3[64:96], ur[64:96, :, :].bitcast(F32), ALU.subtract, [b, wf])
                misc_free[0] = [a, b, c]
                XS["urf"] = c
                S["w"].append([a, c])
                XS["w", n] = S["w"]
            steps += [trans(0, 0), trans(0, 1), fold(0), trans(1, 0), trans(1, 1), fold(1), low]
            return steps

        DN = {}

        def updown(n):
            par = n % 2
            steps = []
            S = {"g": [], "last": None}

            def pair(r, jp):
                rows = 128 if r < 5 else 48

                def f():
                    if n == 0:
                        wnext(2)
                    gi, b, fr = gbanks.get()
                    for v in range(2):
                        for jj in range(2):
                            o = k.PS[0:rows, 512 * (b + v) + 256 * jj:512 * (b + v) + 256 * jj + 256]
                            c0 = 688 * (2 * jp + jj) + 128 * r
                            cs = slice(c0, c0 + rows)
                            w = [XS["w", n], fr, t_w[r] if n == 0 else None]
                            for c in range(2):
                                k.mm(o, w13h[:, v, c, cs], xsh[:, par, c, :], c == 0, False, w)
                                k.mm(o, w13h[:, v, c, cs], xsl[:, par, c, :], False, False)
                                k.mm(o, w13l[:, v, c, cs], xsh[:, par, c, :], False, False)
                            m = k.mm(o, bx[:, cs], ux[:, par, v, :], False, True, inc=True)
                    S["m"] = m
                    i, g, gfr = gr.get()
                    gp = g[0:rows, :, :]
                    P2 = lambda q: k.PS[0:rows, 512 * q:512 * q + 512].rearrange("p (a n) -> p a n", a=2)
                    a = k.af(gp, P2(b), ACT.Silu, [m, gfr])
                    c = k.tt(gp, gp, P2(b + 1), ALU.mult, [a])
                    gbanks.free(gi, [a, c])
                    S["g"].append((i, g, c, r, jp))
                return f

            def folded(r):
                rows = 128 if r < 5 else 48

                def f():
                    if 1:
                        i0, g0, c0_ = S["g"][2 * r][:3]
                        _, g1, c = S["g"][2 * r + 1][:3]
                        a = k.tt(ga[0:rows, :, :], g0[0:rows, :, :], g1[0:rows, :, :], ALU.add, [c0_, c, XS.get("gaf")])
                        d = k.tt(gf[0:rows, :], ga[0:rows, 0, :], ga[0:rows, 1, :], ALU.add, [a, XS.get("gff")])
                        XS["gaf"] = d
                        e = k.split(gfh[0:rows, r, :], gfl[0:rows, r, :], gf[0:rows, :], [d, DN.get("free"), zero])
                        XS["gff"] = e
                        S["gs"] = [S.get("gs"), e]
                        S["fa"] = a
                return f

            def lora2(idx):
                def f():
                    i, g, c, r, jp = S["g"][idx]
                    rows = 128 if r < 5 else 48
                    for jj in range(2):
                        j = 2 * jp + jj
                        m = k.mm(k.PS[32 * j:32 * j + 32, 2048:2048 + 256], a2[0:rows, 4 * r + j, :], g[0:rows, jj, :],
                                 r == 0, r == 5, [c, t_a2, DN.get("u2f")], inc=jj == 1, skip=True)
                    S.setdefault("lm", {})[idx] = m
                    if jp == 1:
                        for q in (idx - 1, idx):
                            gr.free(S["g"][q][0], [S["lm"][q], S["fa"]])
                return f

            for r in range(6):
                for jp in range(2):
                    def both(r=r, jp=jp):
                        pair(r, jp)()
                        idx = 2 * r + jp
                        if idx >= 2 and jp == 0:
                            folded(r - 1)()
                        if idx >= 1:
                            lora2(idx - 1)()
                    steps.append(both)

            def end():
                folded(5)()
                lora2(11)()
                XS["xsf", par] = S["m"]
                m = S["lm"][11]
                a = k.copy(u2[:, :], k.PS[:, 2048:2048 + 256], [m, DN.get("u2sb")], e="act")
                DN["u2f"] = a
                o = k.bank(5)[0:96, 0:256]
                m = k.mm(o, sel[:, 2, :], u2[:, :], True, True, [a, misc_free[0]], inc=True)
                DN["u2sb"] = m
                o = k.bank(5)[64:96, 0:256]
                e = k.split(gfh[64:96, 5, :], gfl[64:96, 5, :], o, [m, DN.get("free"), zero])
                misc_free[0] = e
                S["gs"] = [S["gs"], e]
            return steps, end, S

        def down(n, i, S):
            t = 2 * n + i
            cols = slice(128 * i, 128 * i + 128)

            for s in range(2):
                o = k.bank(6 + s)
                for c in range(6):
                    q = slice(0, 128) if c < 5 else slice(0, 96)
                    a, b = gfh[q, c, cols], gfl[q, c, cols]
                    u, v = w2h[q, c, 512 * s:512 * s + 512], w2l[q, c, 512 * s:512 * s + 512]
                    w = [S["gs"], y_free[0], t_dn if n == 0 else None]
                    k.mm(o, a, u, c == 0, False, w)
                    k.mm(o, a, v, False, False)
                    m = k.mm(o, b, u, False, c == 5, inc=c == 5)
            if i == 1:
                DN["free"] = m

            def free_y(toks):
                y_free[0] = toks
            return k.tail_steps(t, k.bank(6, 2), m, free_y, xr, yr, x_src, x_dst, xn_dst, x_tok=k.done_x[t])

        wnext(3)
        nx = prep(0)
        for f in nx:
            f()
        wnext(3)
        pend = None
        tails = []

        def tail_some():
            if tails:
                tails.pop(0)()

        for n in range(NB + 1):
            if n < NB:
                steps, end, S = updown(n)
                nx = prep(n + 1) if n + 1 < NB else []
                if nx:
                    nx.pop(0)()
                for q, f in enumerate(steps):
                    f()
                    if q == 0 and pend is not None:
                        tails += down(n - 1, 0, pend)
                    if q == 1 and pend is not None:
                        tail_some()
                        tail_some()
                        tails += down(n - 1, 1, pend)
                    if q >= 2:
                        tail_some()
                    if q >= 4 and nx:
                        nx.pop(0)()
                while nx:
                    nx.pop(0)()
                while tails:
                    tail_some()
                end()
                pend = S
            else:
                a = down(n - 1, 0, pend)
                a[0]()
                a[1]()
                b = down(n - 1, 1, pend)
                for q in range(len(b)):
                    b[q]()
                    if q + 2 < len(a):
                        a[q + 2]()


def proj_pass(k, ctx, pre, tiles, in_src, in_tok, wh, wl, t_w, x_src, x_dst, xn_dst, rings, bias=None, hook=None,
              transposed=False):
    nc, p = k.nc, k.p
    inr, xth, xr, yr = rings
    trb, yb = Ring([0, 2]), Ring([4, 6])
    if "pp" in k.carry:
        trb, yb = k.carry["pp"]
    k.carry["pp"] = (trb, yb)

    def item(t):
        S = {}

        def load():
            S["ii"], S["in"], fr = inr.get()
            if transposed:
                S["ld"] = p.dma(k.ld, S["in"][:, :].rearrange("p (c n) -> p c n", c=8),
                                in_src.rearrange("(c p) n -> p c n", p=128)[:, :, 128 * t:128 * t + 128], [fr, in_tok(t)])
            else:
                S["ld"] = p.dma(k.ld, S["in"][:, :], in_src[128 * t:128 * t + 128, :], [fr, in_tok(t)])

        def trans():
            if transposed:
                S["xi"], (S["h"], S["l"]), fr = xth.get()
                S["w"] = k.split(S["h"][:, :, :], S["l"][:, :, :], S["in"][:, :].rearrange("p (c n) -> p c n", c=8), [S["ld"], fr])
                inr.free(S["ii"], S["w"])
                return
            bi, b, fr = trb.get()
            for c in range(8):
                m = k.tr(k.PS[:, 512 * b + 128 * c:512 * b + 128 * c + 128], S["in"][:, 128 * c:128 * c + 128],
                         [S["ld"], fr], inc=c == 7)
            inr.free(S["ii"], m)
            S["xi"], (S["h"], S["l"]), fr = xth.get()
            S["w"] = k.split(S["h"][:, :, :], S["l"][:, :, :], k.bank(b, 2).rearrange("p (c n) -> p c n", c=8), [m, fr])
            trb.free(bi, S["w"])

        def mmul():
            S["i"], b, fr = yb.get()
            for s in range(2):
                o = k.bank(b + s)
                if bias:
                    k.mm(o, bias[1][:, :], bias[0][:, 512 * s:512 * s + 512], True, False, [fr, bias[2]])
                for c in range(8):
                    u, v = wh[:, c, 512 * s:512 * s + 512], wl[:, c, 512 * s:512 * s + 512]
                    k.mm(o, S["h"][:, c, :], u, c == 0 and not bias, False, [S["w"], fr, t_w[c]])
                    k.mm(o, S["h"][:, c, :], v, False, False)
                    m = k.mm(o, S["l"][:, c, :], u, False, c == 7, inc=c == 7)
            xth.free(S["xi"], m)
            S["steps"] = k.tail_steps(t, k.bank(b, 2), m, lambda toks: yb.free(S["i"], toks), xr, yr, x_src, x_dst, xn_dst,
                                      hook=hook, x_tok=k.done_x[t])
        n_ = 4 if xn_dst is not None else 2
        return [load, trans, mmul] + [(lambda j=j: S["steps"][j]()) for j in range(n_)]
    pipeline([item(t) for t in tiles])


def stage_c(k, x_src, xn_src, ctx_d, x_dst, xn_dst):
    nc, p, io = k.nc, k.p, k.io
    SC = float(1.0 / 32 ** 0.5)
    LOOK = 2
    NDVE = 3
    with ExitStack() as ctx:
        def sb(name, shape, dt=F32):
            return ctx.enter_context(nc.sbuf_tensor("c_" + name, shape, dt))

        xth, xtl = sb("xth", [128, 8, 1024], F32R), sb("xtl", [128, 8, 1024], F32R)
        K4 = sb("K4", [128, 8, 1024], F32R)
        Q4 = sb("Q4", [128, 8, 1024], F32R)
        V = sb("V", [128, 8, 8, 65], F32R)
        qh, ql = sb("qh", [128, 1024], F32R), sb("ql", [128, 1024], F32R)
        wqr = Ring([(sb(f"wqh{i}", [128, 8, 128], F32R), sb(f"wql{i}", [128, 8, 128], F32R)) for i in range(2)])
        mc = sb("mc", [128, 4, 8])
        mTr = Ring([sb(f"mT{i}", [8, 128], F32R) for i in range(2)])
        maskw = sb("maskw", [128, 512])
        t_mask = [k.dve(lambda: nc.vector.memset(maskw[:, 0:384], 0.0)),
                  k.copy(maskw[:, 384:512], k.mask, k.t_c)]
        cE = sb("cE", [65, 1024])
        cH, cL, cS = sb("cH", [128, 1024]), sb("cL", [128, 1024]), sb("cS", [128, 1024])
        PU, PE_ = 19, 16
        P0 = sb("P0", [128, 128 * PE_])
        Ph, Pl = sb("Ph", [128, 128 * PU], F32R), sb("Pl", [128, 128 * PU], F32R)
        Pt, Pe = Banks(0, PU), Banks(0, PE_)
        raws = Ring([sb(f"raw{i}", [128, 1024]) for i in range(1)])
        xin = Ring([P0[:, 0:1024], cH[:, :]])

        t_one = [k.dve(lambda: nc.vector.memset(V[:, :, :, 64:65].bitcast(F32), 1.0)),
                 k.dve(lambda: nc.vector.memset(K4[96:97, :, :].bitcast(F32), -1.0))]
        k4_free, q4_free = [None] * 8, [None] * 8
        stg_free = [None]
        v_free = [None]
        xt_free = [None]
        mc_free = [None] * 4
        cE_free, cH_free, rs_free, cS_free = [None], [None], [None], [None]
        rs = sb("rs", [128, 32])

        pieces = []
        for b in range(2):
            for _ in range(2):
                pieces += [io["wk"][:, 128 * b:128 * b + 128], io["wv"][:, 128 * b:128 * b + 128]]
            pieces += [io["wq"][:, 128 * j:128 * j + 128] for j in range(8)]
        ahead = []

        def wprep():
            if pieces:
                src = pieces.pop(0)
                ri, raw, rf = raws.get()
                i, (wh, wl), fr = wqr.get()
                t = p.dma(k.wl, raw[:, :].rearrange("p (c n) -> p c n", c=8), src.rearrange("(c p) n -> p c n", p=128), rf)
                w = k.split(wh[:, :, :], wl[:, :, :], raw[:, :].rearrange("p (c n) -> p c n", c=8), [t, fr])
                raws.free(ri, w)
                ahead.append((i, wh, wl, w))

        def wdone(w, m):
            wqr.free(w[0], m)
            wprep()

        def load_x(src):
            tb = Ring([0, 2, 4])
            bar = [k.p.last(e) for e in ("pe", "act", "dve", "pool")]
            t_x = []

            def lt(t):
                S = {}

                def f0():
                    S["i"], S["x"], fr = xin.get()
                    S["ld"] = p.dma(k.ld, S["x"], xn_src[128 * t:128 * t + 128, :], [fr, k.done_xn[t], bar, cH_free[0]])

                def f1():
                    bi, bk, fr = tb.get()
                    for c in range(8):
                        m = k.tr(k.PS[:, 512 * bk + 128 * c:512 * bk + 128 * c + 128], S["x"][:, 128 * c:128 * c + 128],
                                 [S["ld"], fr, bar], inc=c == 7)
                    xin.free(S["i"], m)
                    cols = slice(128 * (t % 8), 128 * (t % 8) + 128)
                    w = k.split(xth[:, :, cols], xtl[:, :, cols], k.bank(bk, 2).rearrange("p (c n) -> p c n", c=8), [m, xt_free[0]])
                    tb.free(bi, w)
                    t_x.append(w)
                return [f0, f1]
            pipeline([lt(t) for t in range(8 * src, 8 * src + 8)])
            Pe.busy = [[k.p.last("pe")] for _ in range(PE_)]
            cH_free[0] = k.p.last("pe")
            xin.busy, xin.i = [[], []], 0
            return t_x

        mb = Ring([6, 7])
        t_k4 = [None] * 8
        t_v = []

        def chunk_T(w, waits, half, bank, fr):
            o = k.bank(bank)
            for c in range(8):
                xc, xd = xth[:, c, 512 * half:512 * half + 512], xtl[:, c, 512 * half:512 * half + 512]
                k.mm(o, w[1][:, c, :], xc, c == 0, False, [w[3], waits, fr])
                k.mm(o, w[1][:, c, :], xd, False, False)
                m = k.mm(o, w[2][:, c, :], xc, False, c == 7, inc=c == 7)
            return m

        def kv(b, src, t_x):
            w = ahead.pop(0)
            r = []
            for half in range(2):
                i, bk, fr = mb.get()
                m = chunk_T(w, t_x, half, bk, fr)
                cs = slice(512 * half, 512 * half + 512)
                r.append(k.split(qh[:, cs], ql[:, cs], k.bank(bk), [m, stg_free[0]]))
                mb.free(i, r[-1])
            wdone(w, m)
            ds = []
            for g in range(4):
                j = 2 * g + src
                s = slice(32 * g, 32 * g + 32)
                t_k4[j] = [p.dma(k.ld, K4[0:32, j, :].bitcast(F32), qh[s, :].bitcast(F32), [r, k4_free[j]]),
                           p.dma(k.ld, K4[32:64, j, :].bitcast(F32), qh[s, :].bitcast(F32), [r]),
                           p.dma(k.ld, K4[64:96, j, :].bitcast(F32), ql[s, :].bitcast(F32), [r])]
                ds.append(t_k4[j])
            stg_free[0] = ds
            w = ahead.pop(0)
            for t4 in range(2):
                i, bk, fr = mb.get()
                for tt_ in range(4):
                    o = k.bank(bk)[:, 128 * tt_:128 * tt_ + 128]
                    tok = slice(128 * (4 * t4 + tt_), 128 * (4 * t4 + tt_) + 128)
                    for c in range(8):
                        k.mm(o, xth[:, c, tok], w[1][:, c, :], c == 0, False, [w[3], t_x, fr])
                        k.mm(o, xth[:, c, tok], w[2][:, c, :], False, False)
                        m = k.mm(o, xtl[:, c, tok], w[1][:, c, :], False, c == 7, inc=c == 7)
                hi = []
                src4 = [k.bank(bk)[:, 128 * q:128 * q + 128].rearrange("p (g d) -> p g d", g=4) for q in range(4)]
                vs = [V[:, 4 * t4 + q, src:8:2, :] for q in range(4)]
                for q in range(4):
                    hi.append(k.copy(vs[q][:, :, 0:32], src4[q], [m, v_free[0], t_one], e="act"))
                for q in range(4):
                    a = k.tt(vs[q][:, :, 32:64], src4[q], vs[q][:, :, 0:32].bitcast(F32), ALU.subtract, hi)
                t_v.append([hi, a])
                mb.free(i, a)
            wdone(w, m)
            xt_free[0] = m

        wprep()
        wprep()
        t_x = None
        for b in range(2):
            if b == 0:
                t_x = load_x(1)
            mb.i, mb.busy = 0, [[k.p.last("dve"), k.p.last("act")] for _ in range(2)]
            kv(b, 1 - b, t_x)
            t_x = load_x(b)
            kv(b, b, t_x)

            sr = Banks(0, 5)
            sr.busy = [[t_x] for _ in range(5)]
            ctxf = [[mb.busy, t_x], [mb.busy, t_x]]
            qf = [mb.busy]
            t_q4 = {}
            t_m = {}

            def qproj_steps(j):
                S = {}

                def step(part, c):
                    def f():
                        if part == 0 and c == 0:
                            S["w"] = ahead.pop(0)
                        w = S["w"]
                        o = k.bank(7)
                        xc, xd = xth[:, c, 512 * part:512 * part + 512], xtl[:, c, 512 * part:512 * part + 512]
                        k.mm(o, w[1][:, c, :], xc, c == 0, False, [w[3], t_x, qf[0]])
                        k.mm(o, w[1][:, c, :], xd, False, False)
                        m = k.mm(o, w[2][:, c, :], xc, False, c == 7, inc=c == 7)
                        if c == 7:
                            cs = slice(512 * part, 512 * part + 512)
                            e = k.split(qh[:, cs], ql[:, cs], o, [m, stg_free[0] if part == 0 else None])
                            qf[0] = e
                            S["r"] = [S.get("r"), e]
                            if part == 1:
                                wdone(w, m)
                                stg_free[0] = []
                                if j == 7:
                                    xt_free[0] = m
                    return f

                def place(g):
                    s = slice(32 * g, 32 * g + 32)
                    q = (4 * j + g) % 8
                    d = [p.dma(k.ld, Q4[0:32, q, :].bitcast(F32), qh[s, :].bitcast(F32), [S["r"], q4_free[q]]),
                         p.dma(k.ld, Q4[32:64, q, :].bitcast(F32), ql[s, :].bitcast(F32), [S["r"]]),
                         p.dma(k.ld, Q4[64:96, q, :].bitcast(F32), qh[s, :].bitcast(F32), [S["r"]])]
                    t_q4[4 * j + g] = d
                    stg_free[0].append(d)
                return [step(part, c) for part in range(2) for c in range(8)], place

            def amax(h, t):
                g, q, n = h // 4, h % 8, 128 * (t + 1)
                o = mc[:, h % 4, t:t + 1]
                a = None
                for s in range(0, n, 512):
                    e = min(n, s + 512)
                    i, bk, fr = sr.get(1)
                    r = k.bank(bk)[:, 0:e - s]
                    m = k.mm(r, Q4[0:96, q, 128 * t:128 * t + 128], K4[0:96, g, s:e],
                             True, True, [t_q4[h], t_k4[g], fr], inc=True)
                    w = [m, mc_free[h % 4]]
                    if e < n:
                        a = b_ = k.dve(lambda r=r: nc.vector.tensor_reduce(o, r, AX, ALU.max), w)
                    else:
                        b_ = k.dve(lambda r=r, init=o if a else -3.0e38, c0=512 - (e - s): nc.vector.tensor_tensor_reduce(
                            out=r, in0=r, in1=maskw[:, c0:512], scale=1.0, scalar=init,
                            op0=ALU.add, op1=ALU.max, accum_out=o), [w, a, t_mask])
                    sr.free(i, [b_])
                t_m.setdefault(h, []).append(b_)

            def mrow(h):
                si, bk, sf = sr.get(1)
                o = k.bank(bk)[0:8, 0:128]
                m = k.tr(o, mc[:, h % 4, :], [t_m[h], sf], inc=True)
                mc_free[h % 4] = m
                i, mT, fr = mTr.get()
                a = k.copy(mT[:, :], o, [m, fr], e="act")
                sr.free(si, a)
                d = p.dma(k.ld, Q4[96:97, h % 8, :].bitcast(F32).rearrange("a (t n) -> a t n", t=8), mT[:, :].bitcast(F32), [a, q4_free[h % 8]])
                mTr.free(i, d)
                t_q4[h] = [t_q4[h], d]

            pend = []

            def score(h, kt):
                g, q, n = h // 4, h % 8, 1024 - 128 * kt
                i, bk, fr = sr.get(1 if n <= 512 else 2)
                for s in range(0, n, 512):
                    e = min(n, s + 512)
                    m = k.mm(k.PS[:, 512 * bk + s:512 * bk + e], K4[0:97, g, 128 * kt:128 * kt + 128],
                             Q4[0:97, q, 128 * kt + s:128 * kt + e], True, True, [t_q4[h], t_k4[g], fr, t_one], inc=True)
                v0, P, ef = Pe.get(8 - kt)
                P = P0[:, 128 * P:128 * P + n]
                a = k.af(P, k.PS[:, 512 * bk:512 * bk + n], ACT.Exp, [m, ef], scale=SC)
                sr.free(i, [a])
                c = k.pool(lambda: nc.gpsimd.affine_select(out=P[:, 0:128], in_=P[:, 0:128], compare_op=ALU.is_ge, fill=0.0,
                                                           base=0, pattern=[[1, 128]], channel_multiplier=-1), [a])
                late.append((h, kt, v0, P, [a, c]))
                if kt == 7:
                    q4_free[q] = m
                    if h % 4 == 3:
                        k4_free[g] = m

            finish = []

            def finish_steps(g, w):
                S = {}
                r0 = 32 * b + 4 * g
                rows = lambda d_: d_[r0:r0 + 4, :].rearrange("a (x y) -> (a x) y", y=32)

                def load():
                    S["l"] = p.dma(k.st, rs[:, :], rows(k.sum_d), [w, rs_free[0]])

                def recip():
                    S["r"] = k.dve(lambda: nc.vector.reciprocal(rs[:, :], rs[:, :]), [S["l"]])

                def store():
                    S["s"] = rs_free[0] = p.dma(k.st, rows(k.rec_d), rs[:, :], S["r"])

                def spread():
                    S["c"] = [p.dma(k.st, cS[32 * q:32 * q + 32, :], k.rec_d[r0 + q, :].partition_broadcast(32),
                                    [S["s"], cS_free[0]]) for q in range(4)]

                def end():
                    a = k.tt(cH[:, :], cH[:, :], cL[:, :], ALU.add, w)
                    a = k.tt(cH[:, :], cH[:, :], cS[:, :], ALU.mult, [a, S["c"]])
                    cS_free[0] = a
                    cH_free[0] = p.dma(k.st, ctx_d[128 * g:128 * g + 128, 1024 * b:1024 * b + 1024], cH[:, :], a)
                return [load, recip, store, spread, lambda: None, end]

            late = []

            def halves():
                h, kt, v0, P, w = late.pop(0)
                while not Pt.can(8 - kt):
                    pv(*pend.pop(0))
                u0, at, pf = Pt.get(8 - kt)
                w = [w, pf]
                n = 1024 - 128 * kt
                H, L = Ph[:, 128 * at:128 * at + n], Pl[:, 128 * at:128 * at + n]
                d = k.copy(H, P, w, e="act")
                e = k.tt(L, P, H.bitcast(F32), ALU.subtract, [d, w], e="dve" if kt < NDVE else "pool")
                Pe.free(v0, [d, e])
                pend.append((h, kt, u0, H, L, d, e))

            def evac(h, half, m):
                a = k.copy(cE[:, 512 * half:512 * half + 512], k.bank(5 + half)[0:65, :], [m, cE_free[0]], e="act")
                ctxf[half] = [a]
                return a

            E = {}

            def pv(h, kt, u0, H, P, th, tl):
                g, c0 = h // 4, 128 * kt
                for X, tok in ((H, th), (P, tl)):
                    for half in range(2):
                        lo, hi = max(c0, 512 * half), 512 * half + 512
                        if lo >= hi:
                            continue
                        m = k.mm(k.bank(5 + half)[0:65, lo - 512 * half:512], V[:, kt, g, :], X[:, lo - c0:hi - c0],
                                 kt == 0 and X is H, kt == 4 * half + 3 and X is P,
                                 [tok, ctxf[half], t_v, t_one], inc=True, skip=True)
                        E[half] = m
                Pt.free(u0, m)
                if kt == 3:
                    E["a"] = evac(h, 0, E[0])
                if kt == 7:
                    b_ = evac(h, 1, E[1])
                    w = [E["a"], b_]
                    s = slice(32 * (h % 4), 32 * (h % 4) + 32)
                    d = [p.dma(k.st, cH[s, :], cE[0:32, :], [w, cH_free[0]]),
                         p.dma(k.st, cL[s, :], cE[32:64, :], [w, cH_free[0]]),
                         p.dma(k.st, k.sum_d[32 * b + h:32 * b + h + 1, :], cE[64:65, :], w)]
                    cE_free[0] = d[:]
                    E["d"] = [E.get("d"), d] if h % 4 else [d]
                    if h == 31:
                        v_free[0] = m
                    if h % 4 == 3:
                        finish.extend(finish_steps(g, E["d"]))

            for j in range(2):
                steps, place = qproj_steps(j)
                for f in steps:
                    f()
                for g in range(4):
                    place(g)
                if j == 0:
                    for g in range(4):
                        for t in range(8):
                            amax(g, t)
                        mrow(g)
            for j in range(8):
                steps, place = qproj_steps(j + 2) if j + 2 < 8 else ([], None)
                for g in range(4):
                    h = 4 * j + g
                    for n in range(8):
                        while not Pe.can(8 - n):
                            halves()
                        if finish:
                            finish.pop(0)()
                        if n == 2 and 1 <= h < 29:
                            mrow(h + 3)
                        score(h, n)
                        if j < 7:
                            amax(h + 4, n)
                        while len(late) > 1:
                            halves()
                        if len(pend) > LOOK:
                            pv(*pend.pop(0))
                        if steps and n % 4 != 3:
                            steps.pop(0)()
                    if place and g == 2:
                        assert not steps
                        for q in range(3):
                            place(q)
                    if place and g == 3:
                        place(3)
            while late:
                halves()
            while pend:
                pv(*pend.pop(0))
            while finish:
                finish.pop(0)()
    p.barrier()
    with ExitStack() as ctx:
        def sb(name, shape, dt=F32):
            return ctx.enter_context(nc.sbuf_tensor("c2_" + name, shape, dt))
        wh, wl = sb("wh", [128, 8, 1024], F32R), sb("wl", [128, 8, 1024], F32R)
        bo, one = sb("bo", [64, 1024], F32R), sb("one", [64, 128], F32R)
        stg = Ring([sb(f"stg{i}", [128, 1024]) for i in range(2)])
        rings = (Ring([sb(f"in{i}", [128, 1024]) for i in range(3)]),
                 Ring([(sb(f"h{i}", [128, 8, 128], F32R), sb(f"l{i}", [128, 8, 128], F32R)) for i in range(2)]),
                 Ring([sb(f"x{i}", [128, 1024]) for i in range(4)]), Ring([sb(f"y{i}", [128, 1024]) for i in range(4)]))
        t_bo = k.load_bias(bo, one, rings[0].bufs[0][0:64, :], io["bo"])
        rings[0].busy[0] = [t_bo]
        t_w = [k.load_split(wh[:, c, :], wl[:, c, :], io["wo"][128 * c:128 * c + 128, :], stg) for c in range(8)]
        k.carry.pop("pp", None)
        proj_pass(k, ctx, "c", range(NT), ctx_d, lambda t: None, wh, wl, t_w, x_src, x_dst, xn_dst, rings,
                  bias=(bo, one, t_bo), transposed=True)


def stage_d(k, x_src, xn_src, x_dst):
    nc, p, io = k.nc, k.p, k.io
    with ExitStack() as ctx:
        def sb(name, shape, dt=F32):
            return ctx.enter_context(nc.sbuf_tensor("d_" + name, shape, dt))
        wh, wl = sb("wh", [128, 8, 1024], F32R), sb("wl", [128, 8, 1024], F32R)
        dn = sb("dn", [128, 4, 1024])
        up = sb("up", [128, 4, 1024])
        upc = sb("upc", [128, 4, 1024])
        wqT = sb("wqT", [128, 8, 128])
        keyT = sb("keyT", [128, 8])
        sm = sb("sm", [128, 64])
        wor = Ring([sb(f"wo{i}", [128, 1024]) for i in range(2)])
        rings = (Ring([sb(f"in{i}", [128, 1024]) for i in range(3)]),
                 Ring([(sb(f"h{i}", [128, 8, 128], F32R), sb(f"l{i}", [128, 8, 128], F32R)) for i in range(1)]),
                 Ring([sb(f"x{i}", [128, 1024]) for i in range(2)]), Ring([sb(f"y{i}", [128, 1024]) for i in range(2)]))
        t_dn = p.dma(k.wl, dn[:, :, :], io["dnT"].rearrange("(c p) n -> p c n", p=128))
        t_up = p.dma(k.wl, up[:, :, :], io["up"].rearrange("(c p) n -> p c n", p=128))
        t_wq = p.dma(k.wl, wqT[:, :, :], io["lwqT"].rearrange("(c p) n -> p c n", p=128))
        t_ky = p.dma(k.wl, keyT[:, :], io["keyT"])
        xin = rings[0]
        wh_free = [None]
        upc_free = [None]
        smf = [None]
        for b in range(2):
            bar = [k.p.last(e) for e in ("act", "dve", "pe")]
            o = k.PS[:, 0:8]
            for t in range(8 * b, 8 * b + 8):
                i, x, fr = xin.get()
                ld = p.dma(k.ld, x[:, :], xn_src[128 * t:128 * t + 128, :], [fr, k.done_xn[t]])
                for c in range(8):
                    m = k.mm(o[:, c:c + 1], x[:, 128 * c:128 * c + 128], k.ones[:, 0:1], t == 8 * b and c == 0, t == 8 * b + 7,
                             [ld, k.t_c, bar], inc=c == 7, skip=True)
                xin.free(i, m)
            mean = sm[:, 0:8]
            a = k.ts(mean, o, 1.0 / 1024, None, ALU.mult, w=[m, smf[0]])
            for c in range(8):
                m = k.mm(k.PS[:, 512:513], wqT[:, c, :], sm[:, c:c + 1], c == 0, c == 7, [a, t_wq], inc=c == 7)
            a = k.copy(sm[:, 8:9], k.PS[:, 512:513], m)
            m = k.mm(k.PS[0:1, 1024:1032], sm[:, 8:9], keyT[:, :], True, True, [a, t_ky], inc=True)
            s = sm[0:1, 16:24]
            a = k.copy(s, k.PS[0:1, 1024:1032], m)
            a2 = k.dve(lambda: nc.vector.tensor_reduce(sm[0:1, 24:25], s, AX, ALU.max), [a])
            isq = float(1.0 / np.sqrt(128.0))
            a2 = k.ts(sm[0:1, 25:26], sm[0:1, 24:25], -isq, None, ALU.mult, w=a2)
            a = k.af(sm[0:1, 32:40], s, ACT.Exp, [a, a2], scale=isq, bias=sm[0:1, 25:26])
            a2 = k.dve(lambda: nc.vector.tensor_reduce(sm[0:1, 26:27], sm[0:1, 32:40], AX, ALU.add), [a])
            a2 = k.dve(lambda: nc.vector.reciprocal(sm[0:1, 27:28], sm[0:1, 26:27]), [a2])
            a = k.ts(sm[0:1, 40:48], sm[0:1, 32:40], sm[0:1, 27:28], None, ALU.mult, w=[a, a2])
            m = k.mm(k.PS[:, 1536:1544], k.ones[0:1, :], sm[0:1, 40:48], True, True, [a], inc=True)
            ce = k.PS[:, 1536:1544].rearrange("p (c e) -> p c e", e=2)
            a = k.copy(sm[0:64, 48:52], ce[0:64, :, 0], m)
            a2 = k.copy(sm[64:128, 48:52], ce[64:128, :, 1], m)
            u = [k.ts(upc[:, c, :], up[:, c, :], sm[:, 48 + c:49 + c], None, ALU.mult, w=[a, a2, t_up, upc_free[0]]) for c in range(4)]
            smf[0] = u
            wb = Ring([4, 6])
            for q in range(2):
                wb.free(q, bar)
            t_w = []
            for i8 in range(8):
                wi, wo, fr = wor.get()
                tw = p.dma(k.wl, wo[:, :], io["worgT"][128 * i8:128 * i8 + 128, :], fr)
                bi, bk, bf = wb.get()
                for s_ in range(2):
                    for c in range(4):
                        m = k.mm(k.bank(bk + s_), dn[:, c, 128 * i8:128 * i8 + 128], upc[:, c, 512 * s_:512 * s_ + 512],
                                 c == 0, c == 3, [u, t_dn, bf], inc=c == 3)
                a = k.tt(wo[:, :], wo[:, :], k.bank(bk, 2), ALU.add, [tw, m])
                wb.free(bi, a)
                r = k.split(wh[:, i8, :], wl[:, i8, :], wo[:, :], [a, wh_free[0]])
                wor.free(wi, r)
                t_w.append(r)
            upc_free[0] = m
            k.carry.pop("pp", None)
            trb, yb = Ring([0, 2]), Ring([4, 6])
            for q in range(2):
                yb.free(q, a)
                trb.free(q, u)
            k.carry["pp"] = (trb, yb)
            proj_pass(k, ctx, f"d{b}", range(8 * b, 8 * b + 8), xn_src, lambda t: k.done_xn[t], wh, wl, t_w,
                      x_src, x_dst, None, rings)
            wh_free[0] = k.p.last("pe")


def program(nc, io, out):
    with ExitStack() as ctx:
        k = K(nc, ctx, io, out)
        k.carry = {}
        k.done_x, k.done_xn = {}, {}
        x, xn = io["x"], None
        n = 0
        for s in STAGES:
            last = s == STAGES[-1]
            nx = out if last else k.scr[n]
            nn = None if last else k.scr[n + 1]
            n += 2
            old_x, old_xn = dict(k.done_x), dict(k.done_xn)
            for t in range(NT):
                k.done_x.setdefault(t, None)
                k.done_xn.setdefault(t, None)
            if s == "A":
                stage_a(k, x, nx, nn)
            elif s == "B":
                stage_b(k, x, xn, nx, nn)
            elif s == "C":
                stage_c(k, x, xn, k.ctxT, nx, nn)
            elif s == "D":
                stage_d(k, x, xn, nx)
            elif s == "L":
                prelude(k, x, nn)
                nx = x
            x, xn = nx, nn
            k.p.barrier()
        k.p.run(ctx.enter_context(nc.Block()))


def lay_out(i):
    f = np.float32
    g = {n: np.asarray(a) for n, a in i.items()}
    d = {}
    d["x"] = g["L0_attn_x"].reshape(2048, D)
    cst = np.zeros((128, 520), f)
    cst[:, 0:128] = np.eye(128)
    cst[:, 128:256] = np.eye(128) - 1.0 / 128
    cst[:, 256:384] = np.where(np.arange(128)[None, :] > np.arange(128)[:, None], -1.0e38, 0.0)
    cst[:, 384:512] = 1.0
    cst[:, 512] = 1.0 / 128
    d["cst"] = cst
    cols = [g["L0_attn_bin"][None]] + [g["L0_attn_" + n] for n in ("ln1_w", "ln1_b", "phz_re", "phz_im", "lc_re", "lc_im", "sc_lin", "ln2_w", "ln2_b")]
    cols += [g["L0_attn_b1"].reshape(16, 128), g["L0_attn_b2"], g["L0_attn_lnl_w"][None], g["L0_attn_lnl_b"][None]]
    d["vecs"] = np.concatenate(cols, 0).T
    d["winT"] = g["L0_attn_Win"].T
    d["w1T"] = g["L0_attn_W1"].transpose(0, 2, 1)
    d["w2T"] = g["L0_attn_W2"].transpose(0, 2, 1)
    d["woutT"] = g["L0_attn_Wout"].T
    d["bout"] = g["L0_attn_bout"]
    d["w13T"] = np.stack([g["L0_ffn_w1q"].T, g["L0_ffn_w3q"].T])
    bx = np.zeros((96, FH), f)
    for q in range(3):
        bx[32 * q:32 * q + 2] = g["L0_ffn_b1"].T
        bx[32 * q + 2:32 * q + 4] = g["L0_ffn_b3"].T
    d["bx"] = bx
    a13 = np.zeros((D, 32), f)
    a13[:, 0:2] = g["L0_ffn_a1"].T
    a13[:, 2:4] = g["L0_ffn_a3"].T
    d["a13T"] = a13
    a2 = np.zeros((FH, 32), f)
    a2[:, 0:2] = g["L0_ffn_a2"].T
    d["a2T"] = a2
    w2x = np.zeros((768, D), f)
    w2x[0:688] = g["L0_ffn_w2q"].T
    w2x[704:706] = g["L0_ffn_b2"].T
    d["w2x"] = w2x
    sel = np.zeros((128, 3, 96), f)
    for c in range(4):
        for q in range(3):
            for r in range(2):
                sel[32 * c + r, 0, 32 * q + r] = 0.5
                sel[32 * c + 2 + r, 1, 32 * q + 2 + r] = 0.5
        for r in range(2):
            sel[32 * c + r, 2, 64 + r] = 0.5
    d["sel"] = sel
    d["wq"] = g["L1_attn_Wq"]
    kv = g["L1_attn_Wkv"].reshape(D, 8, 2, 32)
    d["wk"] = kv[:, :, 0].reshape(D, 256)
    d["wv"] = kv[:, :, 1].reshape(D, 256)
    d["wo"] = g["L1_attn_Wo"]
    d["bo"] = g["L1_attn_bo"]
    d["worgT"] = g["L1_ffn_W_org"].T
    d["dnT"] = g["L1_ffn_lora_down"].transpose(0, 2, 1).reshape(512, D)
    d["up"] = g["L1_ffn_lora_up"].reshape(512, D)
    d["keyT"] = g["L1_ffn_lora_keys"].T
    d["lwqT"] = g["L1_ffn_Wq"].T
    return {n: np.ascontiguousarray(a) for n, a in d.items()}


def kernel(**inputs):
    import concourse.bacc as bacc
    from concourse.bass_utils import run_bass_kernel_spmd as run

    nc = bacc.Bacc("TRN2", target_bir_lowering=False, num_devices=1, dynamic_dma_scratch_size=1024)
    arrays = lay_out(inputs)
    io = {n: nc.dram_tensor("in_" + n, a.shape, mybir.dt.from_np(a.dtype), kind="ExternalInput").ap()
          for n, a in arrays.items()}
    out = nc.dram_tensor("out_0", (2048, D), F32, kind="ExternalOutput").ap()
    program(nc, io, out)
    r = run(nc, [{"in_" + n: a for n, a in arrays.items()}], core_ids=[0])
    return r.results[0]["out_0"].reshape(2, 1024, D)
```

```python
from contextlib import ExitStack

import numpy as np
import concourse.bass as bass
from concourse import mybir

F32 = mybir.dt.float32
F32R = mybir.dt.float32r
ACT = mybir.ActivationFunctionType
ALU = mybir.AluOpType
AX = mybir.AxisListType.X

STAGES = "ABCD"
NT = 16
D = 1024
EPS = 1e-5
FH = 2752
VECS = {}
_at = 0
for _n, _w in (("bin", 1), ("ln1w", 4), ("ln1b", 4), ("pre", 4), ("pim", 4), ("lre", 4), ("lim", 4),
               ("scl", 4), ("ln2w", 4), ("ln2b", 4), ("b1", 16), ("b2", 4), ("lnlw", 1), ("lnlb", 1)):
    VECS[_n] = _at
    _at += _w
NVEC = _at


class Prog:

    def __init__(self, nc, ctx):
        self.nc = nc
        self.ctx = ctx
        self.q = {e: [] for e in ("pe", "act", "dve", "pool", "sp")}
        self.sem = {e: ctx.enter_context(nc.semaphore("s_" + e)) for e in ("pe", "act", "dve", "pool")}
        self.n = {e: 0 for e in self.sem}
        self.seen = {e: {} for e in self.q}

    def wait(self, e, waits):
        for w in flat(waits):
            k, v = w
            if self.seen[e].get(k, 0) < v:
                self.seen[e][k] = v
                self.q[e].append(("w", self.sem[k], v))

    def op(self, e, fn, waits=(), inc=True):
        self.wait(e, waits)
        if inc:
            self.n[e] += 1
            self.q[e].append(("i", fn, self.sem[e], 1))
            return (e, self.n[e])
        self.q[e].append(("i", fn, None, 0))
        return None

    def last(self, e):
        return (e, self.n[e])

    def dma(self, ch, out, in_, waits=()):
        k = ch.names[ch.i % len(ch.names)]
        ch.i += 1
        self.wait("sp", [(k, self.n[k])] if self.n[k] else [])
        self.wait("sp", waits)
        self.n[k] += 16
        self.q["sp"].append(("i", lambda: self.nc.sync.dma_start(out, in_), self.sem[k], 16))
        return (k, self.n[k])

    def channel(self, name, n):
        return Channel(self, name, n)

    def barrier(self):
        toks = [(k, v) for k, v in self.n.items() if v]
        for e in self.q:
            self.wait(e, toks)

    def run(self, block):
        def play(eng, items):
            for it in items:
                if it[0] == "w":
                    eng.wait_ge(it[1], it[2])
                else:
                    ins = it[1]()
                    if it[2] is not None:
                        ins.then_inc(it[2], it[3])

        @block.sync
        def _(e):
            play(e, self.q["sp"])

        @block.tensor
        def _(e):
            play(e, self.q["pe"])

        @block.scalar
        def _(e):
            play(e, self.q["act"])

        @block.vector
        def _(e):
            play(e, self.q["dve"])

        @block.gpsimd
        def _(e):
            play(e, self.q["pool"])


class Channel:
    def __init__(self, p, name, n):
        self.names = [f"{name}{i}" for i in range(n)]
        self.i = 0
        for k in self.names:
            p.sem[k] = p.ctx.enter_context(p.nc.semaphore("s_" + k))
            p.n[k] = 0


def flat(w):
    if w is None:
        return
    if isinstance(w, tuple) and len(w) == 2 and isinstance(w[0], str):
        yield w
        return
    for x in w:
        yield from flat(x)


class Ring:

    def __init__(self, bufs):
        self.bufs = bufs
        self.i = 0
        self.busy = [[] for _ in bufs]

    def get(self):
        i = self.i % len(self.bufs)
        assert self.i < len(self.bufs) or self.busy[i], "its readers aren't known yet"
        self.i += 1
        w, self.busy[i] = self.busy[i], []
        return i, self.bufs[i], w

    def free(self, i, toks):
        self.busy[i].append(toks)


class Banks:

    def __init__(self, first, n):
        self.first, self.n, self.at = first, n, 0
        self.busy = [[] for _ in range(n)]

    def get(self, k):
        if self.at + k > self.n:
            self.at = 0
        i = self.at
        self.at = (i + k) % self.n
        w = [self.busy[q] for q in range(i, i + k)]
        assert None not in w, "its readers aren't known yet"
        for q in range(i, i + k):
            self.busy[q] = None
        return (i, k), self.first + i, w

    def can(self, k):
        i = 0 if self.at + k > self.n else self.at
        return None not in self.busy[i:i + k]

    def free(self, run, toks):
        for q in range(run[0], run[0] + run[1]):
            self.busy[q] = [toks]


class K:
    def __init__(self, nc, ctx, io, out):
        self.nc, self.io, self.out = nc, io, out
        self.p = Prog(nc, ctx)
        self.PS = ctx.enter_context(nc.psum_tensor("PS", [128, 4096], F32))
        self.cst = ctx.enter_context(nc.sbuf_tensor("cst", [128, 256 + 128 + 128 + 8], F32))
        self.ident = self.cst[:, 0:128]
        self.cmat = self.cst[:, 128:256]
        self.mask = self.cst[:, 256:384]
        self.ones = self.cst[:, 384:512]
        self.onediv = self.cst[:, 512:513]
        self.small = ctx.enter_context(nc.sbuf_tensor("small", [128, 8, 24], F32))
        self.mhalf = ctx.enter_context(nc.sbuf_tensor("mhalf", [128, 16], F32))
        self.ld = self.p.channel("ld", 6)
        self.st = self.p.channel("st", 6)
        self.wl = self.p.channel("wl", 6)
        self.t_c = self.p.dma(self.ld, self.cst[:, :], io["cst"])
        self.t_mh = self.dve(lambda: nc.vector.memset(self.mhalf[:, :], -0.5))
        self.smr = Ring(list(range(8)))
        self.scr = [nc.dram_tensor(f"scr{i}", (NT * 128, D), F32, kind="Internal").ap() for i in range(7)]
        self.sum_d = nc.dram_tensor("sum_d", (64, 1024), F32, kind="Internal").ap()
        self.rec_d = nc.dram_tensor("rec_d", (64, 1024), F32, kind="Internal").ap()
        self.ctxT = nc.dram_tensor("ctxT", (D, NT * 128), F32, kind="Internal").ap()

    def bank(self, b, n=1):
        return self.PS[:, 512 * b:512 * (b + n)]

    def pe(self, fn, w=(), inc=False):
        return self.p.op("pe", fn, w, inc)

    def act(self, fn, w=()):
        return self.p.op("act", fn, w)

    def dve(self, fn, w=()):
        return self.p.op("dve", fn, w)

    def pool(self, fn, w=()):
        return self.p.op("pool", fn, w)

    def mm(self, out, l, r, start, stop, w=(), inc=False, skip=False):
        nc = self.nc
        if skip:
            return self.pe(lambda: nc.tensor.matmul(out, l, r, start=start, stop=stop, skip_group_check=True), w, inc)
        return self.pe(lambda: nc.tensor.matmul(out, l, r, start=start, stop=stop), w, inc)

    def tr(self, out, in_, w=(), inc=False):
        nc = self.nc
        n = in_.shape[0]
        return self.pe(lambda: nc.tensor.transpose(out, in_, self.ident[0:n, 0:n]), [w, self.t_c], inc)

    def af(self, out, in_, func, w=(), scale=None, bias=None):
        nc = self.nc
        kw = {}
        if scale is not None:
            kw["scale"] = scale
        if bias is not None:
            kw["bias"] = bias
        return self.act(lambda: nc.scalar.activation(out, in_, func, **kw), w)

    def tt(self, out, a, b, op, w=(), e="dve"):
        nc = self.nc
        en = nc.vector if e == "dve" else nc.gpsimd
        return self.p.op(e, lambda: en.tensor_tensor(out, a, b, op), w)

    def ts(self, out, a, s1, s2, op0, op1=None, w=()):
        nc = self.nc
        if op1 is None:
            return self.dve(lambda: nc.vector.tensor_scalar(out, a, s1, None, op0), w)
        return self.dve(lambda: nc.vector.tensor_scalar(out, a, s1, s2, op0, op1), w)

    def stt(self, out, a, s, b, op0, op1, w=()):
        nc = self.nc
        return self.dve(lambda: nc.vector.scalar_tensor_tensor(out=out, in0=a, scalar=s, in1=b, op0=op0, op1=op1), w)

    def copy(self, out, in_, w=(), e="dve"):
        nc = self.nc
        if e == "act":
            return self.act(lambda: nc.scalar.copy(out, in_), w)
        en = nc.vector if e == "dve" else nc.gpsimd
        return self.p.op(e, lambda: en.tensor_copy(out, in_), w)

    def split(self, h, l, src, w=(), e="act"):
        a = self.copy(h, src, w, e)
        b = self.tt(l, src, h.bitcast(F32), ALU.subtract, [w, a])
        return [a, b]

    def load_split(self, h, l, dram, ring, w=()):
        i, buf, fr = ring.get()
        n, m = h.shape[0], h.shape[-1]
        s = buf[0:n, 0:m]
        t = self.p.dma(self.wl, s, dram, fr)
        r = self.split(h, l, s, [t, w])
        ring.free(i, r)
        return r

    def stats(self, src, w):
        nc = self.nc
        i, k, fr = self.smr.get()
        s = self.small[:, k, :]
        a = self.dve(lambda: nc.vector.bn_stats(s[:, 0:6], src[:, 0:512]), [w, fr])
        b = self.dve(lambda: nc.vector.bn_stats(s[:, 6:12], src[:, 512:1024]), w)
        c = self.dve(lambda: nc.vector.bn_aggr(s[:, 12:14], s[:, 0:12]), [a, b])
        d = self.ts(s[:, 14:15], s[:, 13:14], EPS, None, ALU.add, w=[c])
        e = self.tt(s[:, 15:16], s[:, 14:15], self.mhalf[:, 0:1], ALU.pow, [d, self.t_mh], e="pool")
        return {"i": i, "s": s, "mean": c, "rs": e, "st": b}

    def normalize(self, out, src, q, w=()):
        s = q["s"]
        n = self.stt(s[:, 16:17], s[:, 12:13], -1.0, s[:, 15:16], ALU.mult, ALU.mult, [q["rs"], q["mean"]])
        t = self.af(out, src, ACT.Identity, [w, n, q["rs"]], scale=s[:, 15:16], bias=s[:, 16:17])
        self.smr.free(q["i"], t)
        return t

    def load_bias(self, bias, ones, buf, dram, w=()):
        nc = self.nc
        t = self.p.dma(self.wl, buf, dram.partition_broadcast(64), w)
        z = self.dve(lambda: nc.vector.memset(bias[:, :].bitcast(F32), 0.0))
        o = self.dve(lambda: nc.vector.memset(ones[:, :].bitcast(F32), 1.0))
        a = self.copy(bias[0:1, :], buf[0:1, :], [t, z])
        b = self.copy(bias[32:33, :], buf[32:33, :], [t, z])
        c = self.tt(bias[32:33, :], buf[32:33, :], bias[32:33, :].bitcast(F32), ALU.subtract, [b])
        return [a, c, o]

    def tail_steps(self, t, y, ytok, free_y, xring, yring, x_src, x_dst, xn_dst, hook=None, x_tok=None,
                   adder="dve", early=True):
        S = {}
        rows = slice(128 * t, 128 * t + 128)

        def load():
            S["xi"], S["x"], fr = xring.get()
            S["xl"] = self.p.dma(self.ld, S["x"][:, :], x_src[rows, :], [fr, x_tok])
        if early:
            load()

        def s1():
            if not early:
                load()
            S["yi"], S["yn"], S["yf"] = yring.get()
            S["q"] = self.stats(y, ytok)

        def s2():
            a = self.normalize(S["yn"][:, :], y, S["q"], [S["yf"]])
            free_y([a, S["q"]["st"]])
            b = self.tt(S["x"][:, :], S["x"][:, :], S["yn"][:, :], ALU.add, [a, S["xl"]], e=adder)
            S["b"] = b
            S["xs"] = self.p.dma(self.st, x_dst[rows, :], S["x"][:, :], b)
            if xn_dst is None:
                xring.free(S["xi"], [S["xs"]])
                yring.free(S["yi"], [b])

        def s3():
            S["q"] = self.stats(S["x"][:, :], S["b"])

        def s4():
            a = self.normalize(S["yn"][:, :], S["x"][:, :], S["q"], [S["b"]])
            c = self.p.dma(self.st, xn_dst[rows, :], S["yn"][:, :], a)
            xring.free(S["xi"], [S["xs"], a, S["q"]["st"]])
            self.done_xn[t] = c
            self.done_x[t] = S["xs"]
            S["c"] = [a, c]
            if hook is None:
                yring.free(S["yi"], c)

        def s5():
            yring.free(S["yi"], [S["c"], hook(t, S["yn"], S["c"][0])])

        if xn_dst is None:
            return [s1, s2]
        return [s1, s2, s3, s4] + ([s5] if hook else [])


def pipeline(items, lags=None):
    n = len(items)
    k = max(len(x) for x in items)
    for i in range(n + k):
        for s in reversed(range(k)):
            j = i - s
            if 0 <= j < n and s < len(items[j]):
                items[j][s]()


def stage_a(k, x_src, x_dst, xn_dst):
    nc, p, io = k.nc, k.p, k.io
    with ExitStack() as ctx:
        def sb(name, shape, dt=F32):
            return ctx.enter_context(nc.sbuf_tensor("a_" + name, shape, dt))

        win_h, win_l = sb("winh", [128, 8, 128], F32R), sb("winl", [128, 8, 128], F32R)
        h = sb("h", [128, 2048])
        vec = sb("vec", [128, NVEC])
        w1 = sb("w1", [128, 4, 512])
        w2 = sb("w2", [128, 4, 4, 128])
        wout = sb("wout", [128, 1024])
        bout, one = sb("bout", [64, 1024], F32R), sb("one", [64, 128], F32R)
        cosT, sinT = sb("cosT", [128, 4, 1024]), sb("sinT", [128, 4, 1024])
        sm = sb("sm", [128, 20, 4])
        xin = Ring([sb(f"xin{i}", [128, 1024]) for i in range(4)])

        t_vec = p.dma(k.wl, vec[:, :], io["vecs"])
        buf = xin.bufs[3]
        t = p.dma(k.wl, buf[:, :].rearrange("p (c n) -> p c n", c=8), io["winT"].rearrange("(c p) n -> p c n", p=128))
        t_win = k.split(win_h[:, :, :], win_l[:, :, :], buf[:, :].rearrange("p (c n) -> p c n", c=8), t)
        xin.busy[3] = [t_win]

        def V(name, i=0):
            c = VECS[name] + i
            return vec[:, c:c + 1]

        def V4(name):
            return vec[:, VECS[name]:VECS[name] + 4]

        r2, t0, z0, rinv, r, rho, c0, s0, i1, i2, t1, t2 = (sm[:, n, :] for n in range(12))
        M, A_, S_ = ALU.mult, ALU.add, ALU.subtract
        a = k.tt(r2, V4("pre"), V4("pre"), M, t_vec)
        b = k.tt(t0, V4("pim"), V4("pim"), M, t_vec)
        a = k.tt(r2, r2, t0, A_, [a, b])
        z = k.ts(z0, r2, 0.0, None, ALU.is_equal, w=a)
        b = k.ts(t0, r2, 1e-37, None, ALU.max, w=a)
        rv = k.tt(rinv, t0, k.mhalf[:, 0:4], ALU.pow, [b, k.t_mh], e="pool")
        a = k.tt(r, r2, rinv, M, [rv, a])
        t_rho = k.af(rho, r, ACT.Tanh, a)
        a = k.tt(t1, V4("pre"), rinv, M, rv)
        c_ = k.tt(c0, t1, z0, A_, [a, z])
        s_ = k.tt(s0, V4("pim"), rinv, M, rv)
        a = k.tt(t1, c0, V4("lre"), M, [c_])
        b = k.tt(t2, s0, V4("lim"), M, s_)
        t_i1 = k.tt(i1, t1, t2, S_, [a, b])
        a = k.tt(t1, s0, V4("lre"), M, [t_i1])
        b = k.tt(t2, c0, V4("lim"), M, t_i1)
        a = k.tt(t1, t1, t2, A_, [a, b])
        t_i2 = k.ts(i2, t1, -1.0, None, M, w=a)

        tmp = sb("tmp", [128, 2, 2, 512])
        e = [sm[:, 12 + n, :] for n in range(4)]
        first = [k.dve(lambda: nc.vector.memset(cosT[:, :, 0:1], 1.0)), k.dve(lambda: nc.vector.memset(sinT[:, :, 0:1], 0.0))]
        tabs = {}

        def table(level, layers=range(4), e_=None):
            n = 1 << level
            cn, sn = (c0, s0) if level == 0 else (e[0], e[1])
            w = [tabs.get("e"), tabs.get("t"), first, c_, s_]

            def times(out, a, l, w):
                if level >= 7:
                    return k.af(out, a, ACT.Copy, w, scale=sn[:, l:l + 1])
                return k.ts(out, a, sn[:, l:l + 1], None, M, w=w)
            for l0 in layers[::2]:
                pair = [l for l in layers if l0 <= l < l0 + 2]
                uv = {}
                for l in pair:
                    f = tabs.get(("u", l % 2))
                    uv[l] = (times(tmp[:, l % 2, 0, 0:n], sinT[:, l, 0:n], l, [w, f]),
                             times(tmp[:, l % 2, 1, 0:n], cosT[:, l, 0:n], l, [w, f]))
                for l in pair:
                    u, v = uv[l]
                    a = k.stt(cosT[:, l, n:2 * n], cosT[:, l, 0:n], cn[:, l:l + 1], tmp[:, l % 2, 0, 0:n], M, S_, [u, w])
                    b = k.stt(sinT[:, l, n:2 * n], sinT[:, l, 0:n], cn[:, l:l + 1], tmp[:, l % 2, 1, 0:n], M, A_, [v, w])
                    tabs["u", l % 2] = [a, b]
                    tabs["new"] = tabs.get("new", []) + [a, b]
            if layers[-1] == 3 and level < 9:
                last = tabs["t"] = tabs.pop("new")
                a = k.tt(e[2], cn, cn, M, [w, last])
                b = k.tt(e[3], sn, sn, M, [w, last])
                c = k.tt(t2, cn, sn, M, [w, last, t_i2])
                d = k.tt(e[0], e[2], e[3], S_, [a, b, c])
                f = k.ts(e[1], t2, 2.0, None, M, w=[c, b])
                tabs["e"] = [d, f]
            if level == 9:
                tabs["half", layers[0]] = tabs.pop("new")

        xT_ring = Ring([(sb(f"xth{i}", [128, 8, 256], F32R), sb(f"xtl{i}", [128, 8, 256], F32R)) for i in range(2)])
        trb = Ring([0, 2])
        hb = Ring([4, 5])
        G = {}
        h_tok = []

        def a0(t):
            S = {}

            def s0_():
                S["i"], S["x"], fr = xin.get()
                ld = p.dma(k.ld, S["x"][:, :], x_src[128 * t:128 * t + 128, :], fr)
                S["q"] = k.stats(S["x"][:, :], ld)
                if t < 8:
                    table(t)
                elif t < 10:
                    table(8, range(2 * t - 16, 2 * t - 14))
                elif t == 10:
                    table(9, range(1))

            def s1n():
                S["a"] = k.normalize(S["x"][:, :], S["x"][:, :], S["q"], [S["q"]["st"]])

            def s1_():
                a = S["a"]
                bi, b, fr = trb.get()
                for c in range(8):
                    m = k.tr(k.PS[:, 512 * b + 128 * c:512 * b + 128 * c + 128], S["x"][:, 128 * c:128 * c + 128],
                             [a, fr], inc=c % 4 == 3)
                xin.free(S["i"], m)
                if t % 2 == 0:
                    G["i"], G["b"], G["f"] = xT_ring.get()
                    G["w"] = []
                xh, xl = G["b"]
                cols = slice(128 * (t % 2), 128 * (t % 2) + 128)
                w = k.split(xh[:, :, cols], xl[:, :, cols], k.bank(b, 2).rearrange("p (c n) -> p c n", c=8), [m, G["f"]])
                trb.free(bi, w)
                G["w"] = [G["w"], w]

            def s2_():
                if t % 2 == 0:
                    return
                g = t // 2
                xh, xl = G["b"]
                hi, b, fr = hb.get()
                o = k.bank(b)[:, 0:256]
                for c in range(8):
                    k.mm(o, win_h[:, c, :], xh[:, c, :], c == 0, False, [G["w"], fr, t_win])
                    k.mm(o, win_h[:, c, :], xl[:, c, :], False, False)
                    m = k.mm(o, win_l[:, c, :], xh[:, c, :], False, c == 7, inc=c == 7)
                xT_ring.free(G["i"], m)
                r = k.af(h[:, 256 * g:256 * g + 256], o, ACT.Identity, [m, t_vec], bias=V("bin"))
                hb.free(hi, r)
                h_tok.append(r)
            return [s0_, s1n, s1_, s2_]

        pipeline_a0 = [a0(t) for t in range(NT)]
        for i in range(NT + 2):
            if 1 <= i <= NT:
                pipeline_a0[i - 1][1]()
            if i < NT:
                pipeline_a0[i][0]()
            if i >= 2:
                pipeline_a0[i - 2][2]()
                pipeline_a0[i - 2][3]()

        t_w1 = p.dma(k.wl, w1[:, :, :], io["w1T"].rearrange("l p n -> p l n"))
        t_w2 = [p.dma(k.wl, w2[:, l, :, :], io["w2T"][l].rearrange("(c p) n -> p c n", p=128)) for l in range(4)]
        t_wo = p.dma(k.wl, wout[:, :], io["woutT"])
        ST = range(4)
        W = [{n: sb(f"{n}{q}", [128, 512]) for n in ("sq", "cs", "y", "a1", "SA", "SB")} for q in ST]
        hid = [sb(f"hid{q}", [128, 4, 512]) for q in ST]
        vs = sb("vs", [128, 4, 8])
        boot = [k.p.last("act"), k.p.last("dve"), k.p.last("pe")]
        T = [{"h": h_tok[2 * q:2 * q + 2], "b0": boot, "b1": boot} for q in ST]
        carry = {}

        def ln_steps(q, wv, bv, func):
            X, w = T[q], W[q]
            B0 = 2 * q
            hc = h[:, 512 * q:512 * q + 512]

            def center():
                X["m"] = k.mm(k.bank(B0), k.cmat, hc, True, True, [X["h"], X["b0"], k.t_c], inc=True)

            def square():
                X["sq"] = k.af(w["sq"][:, :], k.bank(B0), ACT.Square, [X["m"], X.get("sqf")])

            def keep():
                X["cs"] = k.copy(w["cs"][:, :], k.bank(B0), [X["m"], X.get("csf")], e="act")

            def var():
                for t in range(4):
                    m = k.mm(k.PS[:, 512 * B0 + t:512 * B0 + t + 1], w["sq"][:, 128 * t:128 * t + 128], k.onediv,
                             True, True, [X["sq"], X["cs"]], inc=t == 3)
                X["m"] = X["sqf"] = m

            def eps():
                X["v"] = X["b0"] = k.ts(vs[:, q, 0:4], k.PS[:, 512 * B0:512 * B0 + 4], EPS, None, ALU.add, w=[X["m"], X.get("rs")])

            def power():
                X["rs"] = k.tt(vs[:, q, 4:8], vs[:, q, 0:4], k.mhalf[:, 0:4], ALU.pow, [X["v"], k.t_mh, X.get("rsf")], e="pool")

            def spread():
                for t in range(4):
                    o = 512 * (B0 + 1) + 128 * t
                    m = k.mm(k.PS[:, o:o + 128], vs[:, q, 4 + t:5 + t].broadcast_to([128, 128]), k.ident,
                             True, True, [X["rs"], X["b1"]], inc=t == 3)
                X["m"] = X["rsf"] = m

            def scale():
                X["tt"] = X["b1"] = k.tt(w["cs"][:, :], w["cs"][:, :], k.bank(B0 + 1), M, [X["m"], X["cs"]])

            def affine():
                X["y"] = X["csf"] = k.af(w["y"][:, :], w["cs"][:, :], func, [X["tt"], X.get("yf"), t_vec], scale=wv, bias=bv)
            return [("pe", .85, center), ("act", .6, square), ("act", .6, keep), ("pe", .85, var), ("dve", .15, eps),
                    ("pool", .9, power), ("pe", .85, spread), ("dve", .6, scale), ("act", .65, affine)]

        def conv_steps(q, l):
            X, w = T[q], W[q]
            b, half = q // 2, q % 2
            hc = h[:, 512 * q:512 * q + 512]
            ts = slice(512 * half, 512 * half + 512)
            tw = lambda: tabs["half", l] if half else tabs["t"]

            def inputs():
                X["u1"] = k.tt(w["a1"][:, :], w["y"][:, :], cosT[:, l, ts], M, [X["y"], tw(), X.get("a1f")])
                X["u2"] = k.tt(w["cs"][:, :], w["y"][:, :], sinT[:, l, ts], M, [X["y"], tw(), X.get("csf")])
                X["yf"] = [X["u1"], X["u2"]]

            def scans():
                rb = rho[:, l:l + 1].broadcast_to([128, 512])
                if half == 0:
                    n1, n2, t1_, t2_ = i1[:, l:l + 1], i2[:, l:l + 1], t_i1, [t_i2, carry.get(("done", q + 1))]
                else:
                    P = W[q - 1]
                    n1, n2 = P["SA"][:, 511:512], P["SB"][:, 511:512]
                    t1_, t2_ = carry["s", q - 1]
                q1 = k.dve(lambda: nc.vector.tensor_tensor_scan(w["SA"][:, :], rb, w["a1"][:, :], n1, M, A_),
                           [X["u1"], t1_, t2_, t_rho, X.get("Sf")])
                q2 = k.dve(lambda: nc.vector.tensor_tensor_scan(w["SB"][:, :], rb, w["cs"][:, :], n2, M, A_),
                           [X["u2"], t1_, t2_, t_rho, X.get("Sf")])
                carry["s", q] = (q1, q2)
                carry["done", q] = [q1, q2]
                X["csf"] = q2
                X["q"] = (q1, q2)

            def outputs():
                q1, q2 = X["q"]
                u1 = k.tt(w["sq"][:, :], w["SA"][:, :], cosT[:, l, ts], M, [q1, X["sqf"]])
                u2 = k.tt(w["a1"][:, :], w["SB"][:, :], sinT[:, l, ts], M, [q2])
                u3 = k.tt(w["sq"][:, :], w["sq"][:, :], w["a1"][:, :], A_, [u1, u2])
                X["Sf"] = [u1, u2]
                X["a1f"] = u3
                X["h"] = X["sqf"] = k.stt(hc, w["sq"][:, :], V("scl", l), hc, M, A_, [u3, X["h"]])
            need = ("conv", q - 1, l) if half else ("conv", q + 1, l - 1)
            return [("dve", 1.3, inputs, ("table", half * l)), ("dve", 1.4, scans, need, ("conv", q, l)), ("dve", 2.5, outputs)]

        def mlp_steps(q, l):
            X, w = T[q], W[q]
            B0 = 2 * q
            hc = h[:, 512 * q:512 * q + 512]

            def up(m):
                def f():
                    X["m", m] = X["yf"] = k.mm(k.bank(B0 + m % 2), w1[:, l, 128 * m:128 * m + 128], w["y"][:, :], True, True,
                                               [X["y"], X["b%d" % (m % 2)], t_w1], inc=True)
                return f

            def act(m):
                def f():
                    X["b%d" % (m % 2)] = X["g", m] = k.af(hid[q][:, m, :], k.bank(B0 + m % 2), ACT.Silu,
                                                         [X["m", m], X.get("hf"), t_vec], bias=V("b1", 4 * l + m))
                return f

            def down():
                for m in range(4):
                    r = k.mm(k.bank(B0), w2[:, l, m, :], hid[q][:, m, :], m == 0, m == 3,
                             [X["g", m], X["b0"], t_w2], inc=m == 3)
                X["hf"] = r

            def add():
                X["h"] = X["b0"] = k.stt(hc, k.bank(B0), V("b2", l), hc, A_, A_, [X["hf"], X["h"]])
            r = [("pe", .85, up(0)), ("pe", .85, up(1))]
            for m in range(4):
                r.append(("act", .65, act(m)))
                if m < 2:
                    r.append(("pe", .85, up(m + 2)))
            return r + [("pe", 3.4, down), ("dve", .6, add)]

        streams = []
        for q in ST:
            s = []
            for l in range(4):
                s += ln_steps(q, V("ln1w", l), V("ln1b", l), ACT.Silu)
                s += conv_steps(q, l)
                s += ln_steps(q, V("ln2w", l), V("ln2b", l), ACT.Identity)
                if q == 0 and l < 3:
                    s.append(("dve", 2.0, lambda l=l: table(9, range(l + 1, l + 2)), ("table", 0), ("table", l + 1)))
                s += mlp_steps(q, l)
            s += ln_steps(q, V("lnlw"), V("lnlb"), ACT.Identity)
            streams.append(s)
        ready, at, free = [0.0] * 4, [0] * 4, {}
        emitted = {("conv", q, -1) for q in range(4)} | {("table", 0)}
        while any(at[q] < len(streams[q]) for q in ST):
            best = None
            for q in ST:
                if at[q] < len(streams[q]):
                    st = streams[q][at[q]]
                    if len(st) > 3 and st[3] not in emitted:
                        continue
                    start = max(ready[q], free.get(st[0], 0.0))
                    if best is None or (start, -at[q]) < best[:2]:
                        best = (start, -at[q], q, st)
            start, _, q, st = best
            st[2]()
            free[st[0]] = start + st[1]
            ready[q] = start + st[1] + 0.4
            if len(st) > 4:
                emitted.add(st[4])
            at[q] += 1

        yb = Ring([0, 2, 4, 6])
        for q in ST:
            yb.free(q, [T[q]["b0"], T[q]["b1"]])
        xr = xin
        yr = Ring([hid[q][:, 0:2, :].rearrange("p a n -> p (a n)") for q in range(3)])
        for q in range(3):
            yr.free(q, T[q]["hf"])
        t_bo = k.load_bias(bout, one, hid[3][0:64, 0:2, :].rearrange("p a n -> p (a n)"), io["bout"], T[3]["hf"])

        def item(t):
            S = {}

            def mmul():
                S["i"], b, fr = yb.get()
                q, c = t // 4, 128 * (t % 4)
                for s in range(2):
                    cs = slice(512 * s, 512 * s + 512)
                    k.mm(k.bank(b + s), one[:, :], bout[:, cs], True, False, [fr, t_bo])
                    m = k.mm(k.bank(b + s), W[q]["y"][:, c:c + 128], wout[:, cs], False, True,
                             [T[q]["y"], t_wo], inc=s == 1)
                S["steps"] = k.tail_steps(t, k.bank(b, 2), m, lambda toks: yb.free(S["i"], toks), xr, yr, x_src, x_dst, xn_dst,
                                          adder="pool")
            n_ = 4 if xn_dst is not None else 2
            return [mmul] + [(lambda j=j: S["steps"][j]()) for j in range(n_)]
        pipeline([item(t) for t in range(NT)])


def stage_b(k, x_src, xn_src, x_dst, xn_dst):
    nc, p, io = k.nc, k.p, k.io
    with ExitStack() as ctx:
        def sb(name, shape, dt=F32):
            return ctx.enter_context(nc.sbuf_tensor("b_" + name, shape, dt))

        w13h = sb("w13h", [128, 2, 2, FH], F32R)
        w13l = sb("w13l", [128, 2, 2, FH], F32R)
        bx = sb("bx", [96, FH], F32R)
        w2h, w2l = sb("w2h", [128, 6, 1024], F32R), sb("w2l", [128, 6, 1024], F32R)
        a13 = sb("a13", [128, 8, 32])
        a2 = sb("a2", [128, 24, 32])
        sel = sb("sel", [128, 3, 96])
        xnb = [sb(f"xn{i}", [128, 1024]) for i in range(2)]
        xr = Ring([sb(f"x{i}", [128, 1024]) for i in range(2)])
        yr = Ring([sb(f"y{i}", [128, 1024]) for i in range(2)])
        xT = sb("xT", [128, 8, 128])
        xsh, xsl = sb("xsh", [128, 2, 2, 256], F32R), sb("xsl", [128, 2, 2, 256], F32R)
        xs = sb("xs", [128, 2, 128])
        usb = sb("usb", [128, 256])
        ux = sb("ux", [96, 2, 2, 256], F32R)
        ur = sb("ur", [96, 2, 256], F32R)
        gr = Ring([sb(f"g{i}", [128, 2, 256]) for i in range(4)])
        ga = sb("ga", [128, 2, 256])
        gf = sb("gf", [128, 256])
        gfh, gfl = sb("gfh", [128, 6, 256], F32R), sb("gfl", [128, 6, 256], F32R)
        u2 = sb("u2", [128, 256])

        t_a13 = p.dma(k.wl, a13[:, :, :], io["a13T"].rearrange("(c p) n -> p c n", p=128))
        t_sel = p.dma(k.wl, sel[:, :, :], io["sel"])
        t_a2 = []
        for r in range(6):
            n = 128 if r < 5 else 48
            t_a2.append(p.dma(k.wl, a2[0:n, 4 * r:4 * r + 4, :],
                              io["a2T"].rearrange("(j q) n -> q j n", q=688)[128 * r:128 * r + n, :, :]))
        stage = Ring([xr.bufs[0], xr.bufs[1], yr.bufs[0], yr.bufs[1]])
        t_w = {}
        zero = [k.dve(lambda: nc.vector.memset(gfh[:, 5, :].bitcast(F32), 0.0)),
                k.dve(lambda: nc.vector.memset(gfl[:, 5, :].bitcast(F32), 0.0))]
        V4 = lambda a: a.rearrange("p c (j q) -> p c j q", q=688)

        def w13_piece(r, v):
            n = 128 if r < 5 else 48
            i, buf, fr = stage.get()
            b4 = buf[:, 0:8 * n].rearrange("p (c j q) -> p c j q", c=2, j=4)
            t = [p.dma(k.wl, b4[:, c, :, :],
                       io["w13T"][v, 128 * c:128 * c + 128, :].rearrange("p (j q) -> p j q", q=688)[:, :, 128 * r:128 * r + n],
                       fr) for c in range(2)]
            a = k.split(V4(w13h[:, v, :, :])[:, :, :, 128 * r:128 * r + n], V4(w13l[:, v, :, :])[:, :, :, 128 * r:128 * r + n], b4, t)
            stage.free(i, a)
            t_w.setdefault(r, []).append(a)

        def bx_piece(r):
            n = 128 if r < 5 else 48
            i, buf, fr = stage.get()
            view = lambda a: a.rearrange("p (j q) -> p j q", q=688)[:, :, 128 * r:128 * r + n]
            b3 = buf[0:96, 0:4 * n].rearrange("p (j q) -> p j q", j=4)
            t = p.dma(k.wl, b3, view(io["bx"]), fr)
            bx3 = view(bx[:, :])
            a = k.copy(bx3, b3, t, e="act")
            b = k.tt(bx3[32:64], b3[32:64], bx3[32:64].bitcast(F32), ALU.subtract, [a])
            stage.free(i, [a, b])
            t_w.setdefault(r, []).append([a, b])

        t_dn = []
        wpieces = []
        for r in range(6):
            wpieces += [lambda r=r: w13_piece(r, 0), lambda r=r: w13_piece(r, 1), lambda r=r: bx_piece(r)]
        for c in range(6):
            wpieces.append(lambda c=c: t_dn.append(k.load_split(w2h[:, c, :], w2l[:, c, :],
                                                                io["w2x"][128 * c:128 * c + 128, :], stage)))

        def wnext(n):
            for _ in range(min(n, len(wpieces))):
                wpieces.pop(0)()
                if not wpieces:
                    for i in range(2):
                        xr.busy[i], yr.busy[i] = stage.busy[i], stage.busy[2 + i]

        NB = 8
        gbanks = Ring([0, 2])
        misc_free = [None]
        y_free = [None]
        XS = {}

        def prep(n):
            steps = []
            S = {"x": [], "w": []}
            par = n % 2

            def load():
                for i in range(2):
                    t = 2 * n + i
                    S["x"].append(p.dma(k.ld, xnb[i][:, :], xn_src[128 * t:128 * t + 128, :], [XS.get(("f", i)), k.done_xn[t]]))
            steps.append(load)

            def trans(i, hf):
                def f():
                    o = k.bank(5)
                    for c in range(4):
                        cc = 4 * hf + c
                        m = k.tr(o[:, 128 * c:128 * c + 128], xnb[i][:, 128 * cc:128 * cc + 128],
                                 [S["x"][i], misc_free[0]], inc=c == 3)
                    if hf == 1:
                        XS["f", i] = m
                    a = k.copy(xT[:, 4 * hf:4 * hf + 4, :], o.rearrange("p (c n) -> p c n", c=4), [m, XS.get("xTf")], e="act")
                    misc_free[0] = a
                    S["xT", hf] = a
                return f

            def fold(i):
                def f():
                    w = [S["xT", 0], S["xT", 1]]
                    o = k.bank(5)
                    for c in range(8):
                        g = c % 4
                        m = k.mm(o[32 * g:32 * g + 32, 0:128], a13[:, c, :], xT[:, c, :],
                                 c < 4, c >= 4, [w, misc_free[0], t_a13], inc=c == 7, skip=True)
                    a = k.copy(usb[:, 128 * i:128 * i + 128], o[:, 0:128], [m, XS.get("uf")], e="act")
                    misc_free[0] = a
                    S["u", i] = a
                    v = xT[:, :, :].rearrange("p (j c) n -> p j c n", c=2)
                    a = k.tt(xs[:, :, :], v[:, 0], v[:, 1], ALU.add, [w, XS.get("xsf")])
                    a = k.tt(xs[:, :, :], xs[:, :, :], v[:, 2], ALU.add, [a])
                    a = k.tt(xs[:, :, :], xs[:, :, :], v[:, 3], ALU.add, [a])
                    XS["xTf"] = [a, m]
                    cols = slice(128 * i, 128 * i + 128)
                    r = k.split(xsh[:, par, :, cols], xsl[:, par, :, cols], xs[:, :, :], [a, XS.get(("xsf", par))])
                    XS["xsf"] = r
                    S["w"].append(r)
                return f

            def low():
                o = k.bank(5)
                for v in range(2):
                    m = k.mm(o[0:96, 256 * v:256 * v + 256], sel[:, v, :], usb[:, :], True, True,
                             [S["u", 0], S["u", 1], misc_free[0], t_sel], inc=v == 1)
                XS["uf"] = m
                o3 = o.rearrange("p (v n) -> p v n", v=2)
                wf = [m, XS.get(("xsf", par))]
                a = k.copy(ux[0:64, par, :, :], o3[0:64], wf, e="act")
                b = k.copy(ur[64:96, :, :], o3[64:96], [m, XS.get("urf")], e="act")
                c = k.tt(ux[64:96, par, :, :], o3[64:96], ur[64:96, :, :].bitcast(F32), ALU.subtract, [b, wf])
                misc_free[0] = [a, b, c]
                XS["urf"] = c
                S["w"].append([a, c])
                XS["w", n] = S["w"]
            steps += [trans(0, 0), trans(0, 1), fold(0), trans(1, 0), trans(1, 1), fold(1), low]
            return steps

        DN = {}

        def updown(n):
            par = n % 2
            steps = []
            S = {"g": [], "last": None}

            def pair(r, jp):
                rows = 128 if r < 5 else 48

                def f():
                    if n == 0:
                        wnext(2)
                    gi, b, fr = gbanks.get()
                    for v in range(2):
                        for jj in range(2):
                            o = k.PS[0:rows, 512 * (b + v) + 256 * jj:512 * (b + v) + 256 * jj + 256]
                            c0 = 688 * (2 * jp + jj) + 128 * r
                            cs = slice(c0, c0 + rows)
                            w = [XS["w", n], fr, t_w[r] if n == 0 else None]
                            for c in range(2):
                                k.mm(o, w13h[:, v, c, cs], xsh[:, par, c, :], c == 0, False, w)
                                k.mm(o, w13h[:, v, c, cs], xsl[:, par, c, :], False, False)
                                k.mm(o, w13l[:, v, c, cs], xsh[:, par, c, :], False, False)
                            m = k.mm(o, bx[:, cs], ux[:, par, v, :], False, True, inc=True)
                    S["m"] = m
                    i, g, gfr = gr.get()
                    gp = g[0:rows, :, :]
                    P2 = lambda q: k.PS[0:rows, 512 * q:512 * q + 512].rearrange("p (a n) -> p a n", a=2)
                    a = k.af(gp, P2(b), ACT.Silu, [m, gfr])
                    c = k.tt(gp, gp, P2(b + 1), ALU.mult, [a])
                    gbanks.free(gi, [a, c])
                    S["g"].append((i, g, c, r, jp))
                return f

            def folded(r):
                rows = 128 if r < 5 else 48

                def f():
                    if 1:
                        i0, g0, c0_ = S["g"][2 * r][:3]
                        _, g1, c = S["g"][2 * r + 1][:3]
                        a = k.tt(ga[0:rows, :, :], g0[0:rows, :, :], g1[0:rows, :, :], ALU.add, [c0_, c, XS.get("gaf")])
                        d = k.tt(gf[0:rows, :], ga[0:rows, 0, :], ga[0:rows, 1, :], ALU.add, [a, XS.get("gff")])
                        XS["gaf"] = d
                        e = k.split(gfh[0:rows, r, :], gfl[0:rows, r, :], gf[0:rows, :], [d, DN.get("free"), zero])
                        XS["gff"] = e
                        S["gs"] = [S.get("gs"), e]
                        S["fa"] = a
                return f

            def lora2(idx):
                def f():
                    i, g, c, r, jp = S["g"][idx]
                    rows = 128 if r < 5 else 48
                    for jj in range(2):
                        j = 2 * jp + jj
                        m = k.mm(k.PS[32 * j:32 * j + 32, 2048:2048 + 256], a2[0:rows, 4 * r + j, :], g[0:rows, jj, :],
                                 r == 0, r == 5, [c, t_a2, DN.get("u2f")], inc=jj == 1, skip=True)
                    S.setdefault("lm", {})[idx] = m
                    if jp == 1:
                        for q in (idx - 1, idx):
                            gr.free(S["g"][q][0], [S["lm"][q], S["fa"]])
                return f

            for r in range(6):
                for jp in range(2):
                    def both(mid=None, r=r, jp=jp):
                        pair(r, jp)()
                        if mid:
                            mid()
                        idx = 2 * r + jp
                        if idx >= 2 and jp == 0:
                            folded(r - 1)()
                        if idx >= 1:
                            lora2(idx - 1)()
                    steps.append(both)

            def end1():
                folded(5)()
                lora2(11)()
                XS["xsf", par] = S["m"]
                m = S["lm"][11]
                a = k.copy(u2[:, :], k.PS[:, 2048:2048 + 256], [m, DN.get("u2sb")], e="act")
                DN["u2f"] = a

            def end2():
                a = DN["u2f"]
                o = k.bank(5)[0:96, 0:256]
                m = k.mm(o, sel[:, 2, :], u2[:, :], True, True, [a, misc_free[0]], inc=True)
                DN["u2sb"] = m
                o = k.bank(5)[64:96, 0:256]
                e = k.split(gfh[64:96, 5, :], gfl[64:96, 5, :], o, [m, DN.get("free"), zero])
                misc_free[0] = e
                S["gs"] = [S["gs"], e]
            return steps, (end1, end2), S

        def down(n, i, S):
            t = 2 * n + i
            cols = slice(128 * i, 128 * i + 128)

            for s in range(2):
                o = k.bank(6 + s)
                for c in range(6):
                    q = slice(0, 128) if c < 5 else slice(0, 96)
                    a, b = gfh[q, c, cols], gfl[q, c, cols]
                    u, v = w2h[q, c, 512 * s:512 * s + 512], w2l[q, c, 512 * s:512 * s + 512]
                    w = [S["gs"], y_free[0], t_dn if n == 0 else None]
                    k.mm(o, a, u, c == 0, False, w)
                    k.mm(o, a, v, False, False)
                    m = k.mm(o, b, u, False, c == 5, inc=c == 5)
            if i == 1:
                DN["free"] = m

            def free_y(toks):
                y_free[0] = toks
            return k.tail_steps(t, k.bank(6, 2), m, free_y, xr, yr, x_src, x_dst, xn_dst, x_tok=k.done_x[t], early=False)

        wnext(3)
        nx = prep(0)
        for f in nx:
            f()
        wnext(3)
        pend = None
        tails = []

        def tail_some():
            if tails:
                tails.pop(0)()

        for n in range(NB + 1):
            if n < NB:
                steps, end, S = updown(n)
                nx = prep(n + 1) if n + 1 < NB else []
                if nx:
                    nx.pop(0)()
                for q, f in enumerate(steps):
                    mid = None
                    if q == 2 and pend is not None:
                        def mid(n=n, pend=pend):
                            tails.extend(down(n - 1, 1, pend))
                    f(mid)
                    if q == 0 and pend is not None:
                        ends[0]()
                    if q == 1 and pend is not None:
                        ends[1]()
                        tails += down(n - 1, 0, pend)
                        tail_some()
                        tail_some()
                    if q >= 3:
                        tail_some()
                    if q >= 4 and nx:
                        nx.pop(0)()
                while nx:
                    nx.pop(0)()
                while tails:
                    tail_some()
                pend, ends = S, end
            else:
                ends[0]()
                ends[1]()
                a = down(n - 1, 0, pend)
                a[0]()
                a[1]()
                b = down(n - 1, 1, pend)
                for q in range(len(b)):
                    b[q]()
                    if q + 2 < len(a):
                        a[q + 2]()


def proj_pass(k, tiles, in_src, in_tok, weights, x_src, x_dst, xn_dst, rings, bias=None, hook=None,
              transposed=False, extra=None, halved=lambda t: False):
    nc, p = k.nc, k.p
    inr, xth, xr, yr = rings
    trb, yb = Ring([0, 2]), Ring([4, 6])
    if "pp" in k.carry:
        trb, yb = k.carry["pp"]
    k.carry["pp"] = (trb, yb)

    def item(t):
        S = {}

        def load():
            S["ii"], S["in"], fr = inr.get()
            if transposed:
                S["ld"] = p.dma(k.ld, S["in"][:, :].rearrange("p (c n) -> p c n", c=8),
                                in_src.rearrange("(c p) n -> p c n", p=128)[:, :, 128 * t:128 * t + 128], [fr, in_tok(t)])
            else:
                S["ld"] = p.dma(k.ld, S["in"][:, :], in_src[128 * t:128 * t + 128, :], [fr, in_tok(t)])

        def trans():
            if transposed:
                S["xi"], (S["h"], S["l"]), fr = xth.get()
                S["w"] = k.split(S["h"][:, :, :], S["l"][:, :, :], S["in"][:, :].rearrange("p (c n) -> p c n", c=8), [S["ld"], fr])
                inr.free(S["ii"], S["w"])
                return
            bi, b, fr = trb.get()
            for c in range(8):
                m = k.tr(k.PS[:, 512 * b + 128 * c:512 * b + 128 * c + 128], S["in"][:, 128 * c:128 * c + 128],
                         [S["ld"], fr], inc=c == 7)
            inr.free(S["ii"], m)
            S["xi"], (S["h"], S["l"]), fr = xth.get()
            S["w"] = k.split(S["h"][:, :, :], S["l"][:, :, :], k.bank(b, 2).rearrange("p (c n) -> p c n", c=8), [m, fr])
            trb.free(bi, S["w"])

        def half(s):
            b, fr = S["b"], S["fr"]
            wh, wl, t_w = weights(t)
            o = k.bank(b + s)
            if bias:
                k.mm(o, bias[1][:, :], bias[0][:, 512 * s:512 * s + 512], True, False, [fr, bias[2]])
            for c in range(8):
                u, v = wh[:, c, 512 * s:512 * s + 512], wl[:, c, 512 * s:512 * s + 512]
                k.mm(o, S["h"][:, c, :], u, c == 0 and not bias, False, [S["w"], fr, t_w[c]])
                k.mm(o, S["h"][:, c, :], v, False, False)
                m = k.mm(o, S["l"][:, c, :], u, False, c == 7, inc=c == 7)
            return m

        def first():
            if extra:
                extra.pop(0)()
            S["i"], S["b"], S["fr"] = yb.get()
            half(0)

        def second():
            m = half(1)
            xth.free(S["xi"], m)
            S["steps"] = k.tail_steps(t, k.bank(S["b"], 2), m, lambda toks: yb.free(S["i"], toks), xr, yr, x_src, x_dst, xn_dst,
                                      hook=hook, x_tok=k.done_x[t])

        def both():
            first()
            second()
        n_ = (4 + bool(hook)) if xn_dst is not None else 2
        return [load, trans] + ([first, second] if halved(t) else [both]) + [(lambda j=j: S["steps"][j]()) for j in range(n_)]
    pipeline([item(t) for t in tiles])


def stage_c(k, x_src, xn_src, ctx_d, x_dst, xn_dst):
    nc, p, io = k.nc, k.p, k.io
    SC = float(1.0 / 32 ** 0.5)
    LOOK = 2
    NDVE = 3
    DV7, DVC = (0, 2, 4, 6), (0, 1, 2)
    with ExitStack() as ctx:
        def sb(name, shape, dt=F32):
            return ctx.enter_context(nc.sbuf_tensor("c_" + name, shape, dt))

        xth, xtl = sb("xth", [128, 8, 1024], F32R), sb("xtl", [128, 8, 1024], F32R)
        K4 = sb("K4", [128, 8, 1024], F32R)
        Q4 = sb("Q4", [128, 8, 1024], F32R)
        V = sb("V", [128, 8, 8, 65], F32R)
        qh, ql = sb("qh", [128, 1024], F32R), sb("ql", [128, 1024], F32R)
        wqr = Ring([(sb(f"wqh{i}", [128, 8, 128], F32R), sb(f"wql{i}", [128, 8, 128], F32R)) for i in range(2)])
        mc = sb("mc", [128, 4, 8])
        mTr = Ring([sb(f"mT{i}", [8, 128], F32R) for i in range(2)])
        maskw = sb("maskw", [128, 512])
        t_mask = [k.dve(lambda: nc.vector.memset(maskw[:, 0:384], 0.0)),
                  k.copy(maskw[:, 384:512], k.mask, k.t_c)]
        cE = sb("cE", [65, 1024])
        cH, cL, cS = sb("cH", [128, 1024]), sb("cL", [128, 1024]), sb("cS", [128, 1024])
        PU, PE_ = 19, 16
        P0 = sb("P0", [128, 128 * PE_])
        Ph, Pl = sb("Ph", [128, 128 * PU], F32R), sb("Pl", [128, 128 * PU], F32R)
        Pt, Pe = Banks(0, PU), Banks(0, PE_)
        raws = Ring([sb(f"raw{i}", [128, 1024]) for i in range(1)])
        xin = Ring([P0[:, 0:1024], cH[:, :], cL[:, :], cS[:, :]])

        t_one = [k.dve(lambda: nc.vector.memset(V[:, :, :, 64:65].bitcast(F32), 1.0)),
                 k.dve(lambda: nc.vector.memset(K4[96:97, :, :].bitcast(F32), -1.0))]
        k4_free, q4_free = [None] * 8, [None] * 8
        stg_free = [None]
        v_free = [None]
        xt_free = [None]
        mc_free = [None] * 4
        cE_free, cH_free, rs_free, cS_free = [None], [None], [None], [None]
        rs = sb("rs", [128, 32])

        pieces = []
        for b in range(2):
            for _ in range(2):
                pieces += [io["wk"][:, 128 * b:128 * b + 128], io["wv"][:, 128 * b:128 * b + 128]]
            pieces += [io["wq"][:, 128 * j:128 * j + 128] for j in range(8)]
        ahead = []

        def wprep():
            if pieces:
                src = pieces.pop(0)
                ri, raw, rf = raws.get()
                i, (wh, wl), fr = wqr.get()
                t = p.dma(k.wl, raw[:, :].rearrange("p (c n) -> p c n", c=8), src.rearrange("(c p) n -> p c n", p=128), rf)
                w = k.split(wh[:, :, :], wl[:, :, :], raw[:, :].rearrange("p (c n) -> p c n", c=8), [t, fr])
                raws.free(ri, w)
                ahead.append((i, wh, wl, w))

        def wdone(w, m):
            wqr.free(w[0], m)
            wprep()

        def load_x(src):
            tb = Ring([0, 2, 4])
            bar = [k.p.last(e) for e in ("pe", "act", "dve", "pool")]
            t_x = []

            def lt(t):
                S = {}

                def f0():
                    S["i"], S["x"], fr = xin.get()
                    S["ld"] = p.dma(k.ld, S["x"], xn_src[128 * t:128 * t + 128, :], [fr, k.done_xn[t], bar, cH_free[0]])

                def f1():
                    bi, bk, fr = tb.get()
                    for c in range(8):
                        m = k.tr(k.PS[:, 512 * bk + 128 * c:512 * bk + 128 * c + 128], S["x"][:, 128 * c:128 * c + 128],
                                 [S["ld"], fr, bar], inc=c == 7)
                    xin.free(S["i"], m)
                    cols = slice(128 * (t % 8), 128 * (t % 8) + 128)
                    w = k.split(xth[:, :, cols], xtl[:, :, cols], k.bank(bk, 2).rearrange("p (c n) -> p c n", c=8), [m, xt_free[0]])
                    tb.free(bi, w)
                    t_x.append(w)
                return [f0, lambda: None, lambda: None, f1]
            pipeline([lt(t) for t in range(8 * src, 8 * src + 8)])
            Pe.busy = [[k.p.last("pe")] for _ in range(PE_)]
            xin.busy, xin.i = [[], [], [], []], 0
            return t_x

        mb = Ring([6, 7])
        t_k4 = [None] * 8
        t_v = []

        def chunk_T(w, waits, half, bank, fr):
            o = k.bank(bank)
            for c in range(8):
                xc, xd = xth[:, c, 512 * half:512 * half + 512], xtl[:, c, 512 * half:512 * half + 512]
                k.mm(o, w[1][:, c, :], xc, c == 0, False, [w[3], waits, fr])
                k.mm(o, w[1][:, c, :], xd, False, False)
                m = k.mm(o, w[2][:, c, :], xc, False, c == 7, inc=c == 7)
            return m

        def kv(b, src, t_x):
            w = ahead.pop(0)
            r = []
            for half in range(2):
                i, bk, fr = mb.get()
                m = chunk_T(w, t_x, half, bk, fr)
                cs = slice(512 * half, 512 * half + 512)
                r.append(k.split(qh[:, cs], ql[:, cs], k.bank(bk), [m, stg_free[0]]))
                mb.free(i, r[-1])
            wdone(w, m)
            ds = []
            for g in range(4):
                j = 2 * g + src
                s = slice(32 * g, 32 * g + 32)
                t_k4[j] = [p.dma(k.ld, K4[0:32, j, :].bitcast(F32), qh[s, :].bitcast(F32), [r, k4_free[j]]),
                           p.dma(k.ld, K4[32:64, j, :].bitcast(F32), qh[s, :].bitcast(F32), [r]),
                           p.dma(k.ld, K4[64:96, j, :].bitcast(F32), ql[s, :].bitcast(F32), [r])]
                ds.append(t_k4[j])
            stg_free[0] = ds
            w = ahead.pop(0)
            cp = []
            for half in range(2):
                i, bk, fr = mb.get()
                m = chunk_T(w, t_x, half, bk, fr)
                cp.append(k.copy(cL[:, 512 * half:512 * half + 512], k.bank(bk), [m], e="act"))
                mb.free(i, cp[-1])
            wdone(w, m)
            xt_free[0] = m
            for t4 in range(2):
                i, bk, fr = mb.get()
                for q in range(4):
                    n0 = 512 * t4 + 128 * q
                    m = k.tr(k.bank(bk)[:, 128 * q:128 * q + 128], cL[:, n0:n0 + 128], [cp[t4], fr], inc=q == 3)
                hi = []
                src4 = [k.bank(bk)[:, 128 * q:128 * q + 128].rearrange("p (g d) -> p g d", g=4) for q in range(4)]
                vs = [V[:, 4 * t4 + q, src:8:2, :] for q in range(4)]
                for q in range(4):
                    hi.append(k.copy(vs[q][:, :, 0:32], src4[q], [m, v_free[0], t_one], e="act"))
                for q in range(4):
                    a = k.tt(vs[q][:, :, 32:64], src4[q], vs[q][:, :, 0:32].bitcast(F32), ALU.subtract, hi)
                t_v.append([hi, a])
                mb.free(i, a)

        wprep()
        wprep()
        t_x = None
        for b in range(2):
            if b == 0:
                t_x = load_x(1)
            mb.i, mb.busy = 0, [[k.p.last("dve"), k.p.last("act")] for _ in range(2)]
            kv(b, 1 - b, t_x)
            t_x = load_x(b)
            kv(b, b, t_x)

            cH_free[0] = cS_free[0] = k.p.last("pe")

            sr = Banks(0, 5)
            sr.busy = [[t_x] for _ in range(5)]
            ctxf = [[mb.busy, t_x], [mb.busy, t_x]]
            qf = [mb.busy]
            t_q4 = {}
            t_m = {}

            def qproj_steps(j):
                S = {}

                def step(part, c):
                    def f():
                        if part == 0 and c == 0:
                            S["w"] = ahead.pop(0)
                        w = S["w"]
                        o = k.bank(7)
                        xc, xd = xth[:, c, 512 * part:512 * part + 512], xtl[:, c, 512 * part:512 * part + 512]
                        k.mm(o, w[1][:, c, :], xc, c == 0, False, [w[3], t_x, qf[0]])
                        k.mm(o, w[1][:, c, :], xd, False, False)
                        m = k.mm(o, w[2][:, c, :], xc, False, c == 7, inc=c == 7)
                        if c == 7:
                            cs = slice(512 * part, 512 * part + 512)
                            e = k.split(qh[:, cs], ql[:, cs], o, [m, stg_free[0] if part == 0 else None])
                            qf[0] = e
                            S["r"] = [S.get("r"), e]
                            if part == 1:
                                wdone(w, m)
                                stg_free[0] = []
                                if j == 7:
                                    xt_free[0] = m
                    return f

                def place(g):
                    s = slice(32 * g, 32 * g + 32)
                    q = (4 * j + g) % 8
                    d = [p.dma(k.ld, Q4[0:32, q, :].bitcast(F32), qh[s, :].bitcast(F32), [S["r"], q4_free[q]]),
                         p.dma(k.ld, Q4[32:64, q, :].bitcast(F32), ql[s, :].bitcast(F32), [S["r"]]),
                         p.dma(k.ld, Q4[64:96, q, :].bitcast(F32), qh[s, :].bitcast(F32), [S["r"]])]
                    t_q4[4 * j + g] = d
                    stg_free[0].append(d)
                return [step(part, c) for part in range(2) for c in range(8)], place

            def amax(h, t):
                g, q, n = h // 4, h % 8, 128 * (t + 1)
                o = mc[:, h % 4, t:t + 1]
                a = None
                for s in range(0, n, 512):
                    e = min(n, s + 512)
                    i, bk, fr = sr.get(1)
                    r = k.bank(bk)[:, 0:e - s]
                    m = k.mm(r, Q4[0:96, q, 128 * t:128 * t + 128], K4[0:96, g, s:e],
                             True, True, [t_q4[h], t_k4[g], fr], inc=True)
                    w = [m, mc_free[h % 4]]
                    if e < n:
                        a = b_ = k.dve(lambda r=r: nc.vector.tensor_reduce(o, r, AX, ALU.max), w)
                    else:
                        b_ = k.dve(lambda r=r, init=o if a else -3.0e38, c0=512 - (e - s): nc.vector.tensor_tensor_reduce(
                            out=r, in0=r, in1=maskw[:, c0:512], scale=1.0, scalar=init,
                            op0=ALU.add, op1=ALU.max, accum_out=o), [w, a, t_mask])
                    sr.free(i, [b_])
                t_m.setdefault(h, []).append(b_)

            def mrow(h):
                si, bk, sf = sr.get(1)
                o = k.bank(bk)[0:8, 0:128]
                m = k.tr(o, mc[:, h % 4, :], [t_m[h], sf], inc=True)
                mc_free[h % 4] = m
                i, mT, fr = mTr.get()
                a = k.copy(mT[:, :], o, [m, fr], e="act")
                sr.free(si, a)
                d = p.dma(k.ld, Q4[96:97, h % 8, :].bitcast(F32).rearrange("a (t n) -> a t n", t=8), mT[:, :].bitcast(F32), [a, q4_free[h % 8]])
                mTr.free(i, d)
                t_q4[h] = [t_q4[h], d]

            pend = []

            def score(h, kt):
                g, q, n = h // 4, h % 8, 1024 - 128 * kt
                i, bk, fr = sr.get(1 if n <= 512 else 2)
                for s in range(0, n, 512):
                    e = min(n, s + 512)
                    m = k.mm(k.PS[:, 512 * bk + s:512 * bk + e], K4[0:97, g, 128 * kt:128 * kt + 128],
                             Q4[0:97, q, 128 * kt + s:128 * kt + e], True, True, [t_q4[h], t_k4[g], fr, t_one], inc=True)
                v0, P, ef = Pe.get(8 - kt)
                P = P0[:, 128 * P:128 * P + n]
                a = k.af(P, k.PS[:, 512 * bk:512 * bk + n], ACT.Exp, [m, ef], scale=SC)
                sr.free(i, [a])
                c = k.pool(lambda: nc.gpsimd.affine_select(out=P[:, 0:128], in_=P[:, 0:128], compare_op=ALU.is_ge, fill=0.0,
                                                           base=0, pattern=[[1, 128]], channel_multiplier=-1), [a])
                late.append((h, kt, v0, P, [a, c]))
                if kt == 7:
                    q4_free[q] = m
                    if h % 4 == 3:
                        k4_free[g] = m

            finish = []

            def finish_steps(g, w):
                S = {}
                r0 = 32 * b + 4 * g
                rows = lambda d_: d_[r0:r0 + 4, :].rearrange("a (x y) -> (a x) y", y=32)

                def load():
                    S["l"] = p.dma(k.st, rs[:, :], rows(k.sum_d), [w, rs_free[0]])

                def recip():
                    S["r"] = k.dve(lambda: nc.vector.reciprocal(rs[:, :], rs[:, :]), [S["l"]])

                def store():
                    S["s"] = rs_free[0] = p.dma(k.st, rows(k.rec_d), rs[:, :], S["r"])

                def spread():
                    S["c"] = [p.dma(k.st, cS[32 * q:32 * q + 32, :], k.rec_d[r0 + q, :].partition_broadcast(32),
                                    [S["s"], cS_free[0]]) for q in range(4)]

                def add(q):
                    c = slice(512 * q, 512 * q + 512)
                    S["a", q] = k.tt(cH[:, c], cH[:, c], cL[:, c], ALU.add, w)

                def scale(q):
                    c = slice(512 * q, 512 * q + 512)
                    S["m", q] = k.tt(cH[:, c], cH[:, c], cS[:, c], ALU.mult, [S["a", q], S["c"]])

                def end():
                    scale(1)
                    cS_free[0] = [S["m", 0], S["m", 1]]
                    cH_free[0] = p.dma(k.st, ctx_d[128 * g:128 * g + 128, 1024 * b:1024 * b + 1024], cH[:, :], cS_free[0])
                return [load, lambda: add(0), lambda: (recip(), store()), lambda: add(1), spread, lambda: None,
                        lambda: scale(0), end]

            late = []

            def halves():
                h, kt, v0, P, w = late.pop(0)
                while not Pt.can(8 - kt):
                    pv(*pend.pop(0))
                u0, at, pf = Pt.get(8 - kt)
                w = [w, pf]
                n = 1024 - 128 * kt
                H, L = Ph[:, 128 * at:128 * at + n], Pl[:, 128 * at:128 * at + n]
                d = k.copy(H, P, w, e="dve" if kt in (DV7 if h >= 28 else DVC) else "act")
                e = k.tt(L, P, H.bitcast(F32), ALU.subtract, [d, w], e="dve" if kt < NDVE + 2 * (h >= 28) else "pool")
                Pe.free(v0, [d, e])
                pend.append((h, kt, u0, H, L, d, e))

            def evac(h, half, m):
                a = k.copy(cE[:, 512 * half:512 * half + 512], k.bank(5 + half)[0:65, :], [m, cE_free[0]], e="act")
                ctxf[half] = [a]
                return a

            E = {}

            def pv(h, kt, u0, H, P, th, tl):
                g, c0 = h // 4, 128 * kt
                for X, tok in ((H, th), (P, tl)):
                    for half in range(2):
                        lo, hi = max(c0, 512 * half), 512 * half + 512
                        if lo >= hi:
                            continue
                        m = k.mm(k.bank(5 + half)[0:65, lo - 512 * half:512], V[:, kt, g, :], X[:, lo - c0:hi - c0],
                                 kt == 0 and X is H, kt == 4 * half + 3 and X is P,
                                 [tok, ctxf[half], t_v, t_one], inc=True, skip=True)
                        E[half] = m
                Pt.free(u0, m)
                if kt == 3:
                    E["a"] = evac(h, 0, E[0])
                if kt == 7:
                    b_ = evac(h, 1, E[1])
                    w = [E["a"], b_]
                    s = slice(32 * (h % 4), 32 * (h % 4) + 32)
                    d = [p.dma(k.st, cH[s, :], cE[0:32, :], [w, cH_free[0]]),
                         p.dma(k.st, cL[s, :], cE[32:64, :], [w, cH_free[0]]),
                         p.dma(k.st, k.sum_d[32 * b + h:32 * b + h + 1, :], cE[64:65, :], w)]
                    cE_free[0] = d[:]
                    E["d"] = [E.get("d"), d] if h % 4 else [d]
                    if h == 31:
                        v_free[0] = m
                    if h % 4 == 3:
                        finish.extend(finish_steps(g, E["d"]))

            steps, place = qproj_steps(0)
            for f in steps:
                f()
            for g in range(4):
                place(g)
            steps, place = qproj_steps(1)
            for g in range(4):
                for t in range(8):
                    amax(g, t)
                    if t % 2:
                        steps.pop(0)()
                mrow(g)
            for g in range(4):
                place(g)
            for j in range(8):
                steps, place = qproj_steps(j + 2) if j + 2 < 8 else ([], None)
                for g in range(4):
                    h = 4 * j + g
                    for n in range(8):
                        while not Pe.can(8 - n):
                            halves()
                        if finish:
                            finish.pop(0)()
                        if n == 2 and 1 <= h < 29:
                            mrow(h + 3)
                        score(h, n)
                        if j < 7:
                            amax(h + 4, n)
                        while len(late) > 1:
                            halves()
                        if len(pend) > LOOK:
                            pv(*pend.pop(0))
                        if steps and n % 4 != 0:
                            steps.pop(0)()
                    if place and g == 2:
                        assert not steps
                        for q in range(3):
                            place(q)
                    if place and g == 3:
                        place(3)
            while late:
                halves()
            while pend:
                pv(*pend.pop(0))
            while finish:
                finish.pop(0)()
    p.barrier()
    with ExitStack() as ctx:
        def sb(name, shape, dt=F32):
            return ctx.enter_context(nc.sbuf_tensor("c2_" + name, shape, dt))
        pd = d_operands(k)
        wh, wl = sb("wh", [128, 8, 1024], F32R), sb("wl", [128, 8, 1024], F32R)
        bo, one = sb("bo", [64, 1024], F32R), sb("one", [64, 128], F32R)
        stg = Ring([sb(f"stg{i}", [128, 1024]) for i in range(2)])
        rings = (Ring([sb(f"in{i}", [128, 1024]) for i in range(3)]),
                 Ring([(sb(f"h{i}", [128, 8, 128], F32R), sb(f"l{i}", [128, 8, 128], F32R)) for i in range(2)]),
                 Ring([sb(f"x{i}", [128, 1024]) for i in range(4)]), Ring([sb(f"y{i}", [128, 1024]) for i in range(4)]))
        t_bo = k.load_bias(bo, one, rings[0].bufs[0][0:64, :], io["bo"])
        rings[0].busy[0] = [t_bo]
        stg = Ring(stg.bufs + rings[3].bufs + rings[2].bufs[2:])
        t_w = [k.load_split(wh[:, c, :], wl[:, c, :], io["wo"][128 * c:128 * c + 128, :], stg) for c in range(8)]
        rings[3].busy, rings[2].busy[2:] = stg.busy[2:6], stg.busy[6:8]
        k.carry.pop("pp", None)
        proj_pass(k, range(NT), ctx_d, lambda t: None, lambda t: (wh, wl, t_w), x_src, x_dst, xn_dst, rings,
                  bias=(bo, one, t_bo), transposed=True, hook=lambda t, xn, tok: column_sums(k, t, xn, tok),
                  extra=[lambda: None] * 3 + [lambda: d_loads(k, pd)] + [lambda: None] * 12)


def d_operands(k):
    def sb(name, shape):
        return k.dctx.enter_context(k.nc.sbuf_tensor("d_" + name, shape, F32))
    k.pd = {"dn": sb("dn", [128, 4, 1024]), "up": sb("up", [128, 4, 1024]), "wqT": sb("wqT", [128, 8, 128]),
            "keyT": sb("keyT", [128, 8])}
    return k.pd


def d_loads(k, pd):
    for n, src in (("wqT", "lwqT"), ("up", "up"), ("dn", "dnT")):
        pd["t_" + n] = k.p.dma(k.wl, pd[n][:, :, :], k.io[src].rearrange("(c p) n -> p c n", p=128))
    pd["t_keyT"] = k.p.dma(k.wl, pd["keyT"][:, :], k.io["keyT"])


def column_sums(k, t, xn, tok):
    for c in range(8):
        m = k.mm(k.bank(t // 8)[:, c:c + 1], xn[:, 128 * c:128 * c + 128], k.ones[:, 0:1], t % 8 == 0 and c == 0, t % 8 == 7,
                 [tok, k.t_c], inc=c == 7, skip=True)
    k.t_sum[t // 8] = m
    return m


def stage_d(k, x_src, xn_src, x_dst):
    nc, p, io = k.nc, k.p, k.io
    dn, up, wqT, keyT = (k.pd[n] for n in ("dn", "up", "wqT", "keyT"))
    t_dn, t_up, t_wq, t_ky = (k.pd["t_" + n] for n in ("dn", "up", "wqT", "keyT"))
    with ExitStack() as ctx:
        def sb(name, shape, dt=F32, c=ctx):
            return c.enter_context(nc.sbuf_tensor("d_" + name, shape, dt))
        W = [(sb(f"wh{b}", [128, 8, 1024], F32R), sb(f"wl{b}", [128, 8, 1024], F32R)) for b in range(2)]
        sm = sb("sm", [128, 2, 64])
        inr = Ring([sb(f"in{i}", [128, 1024]) for i in range(2)])
        xth = Ring([(sb("h0", [128, 8, 128], F32R), sb("l0", [128, 8, 128], F32R))])
        xr, yr = Ring([sb(f"x{i}", [128, 1024]) for i in range(2)]), Ring([sb(f"y{i}", [128, 1024]) for i in range(2)])
        top = ctx.enter_context(ExitStack())
        upc = sb("upc", [128, 4, 1024], c=top)
        wob = sb("wo", [128, 1024], c=top)

        isq = float(1.0 / np.sqrt(128.0))
        coef = []
        for b in range(2):
            s_ = sm[:, b, :]
            B0 = 2 + 3 * b
            a = k.ts(s_[:, 0:8], k.bank(b)[:, 0:8], 1.0 / 1024, None, ALU.mult, w=[k.t_sum[b]])
            for c in range(8):
                m = k.mm(k.bank(B0)[:, 0:1], wqT[:, c, :], s_[:, c:c + 1], c == 0, c == 7, [a, t_wq], inc=c == 7)
            a = k.copy(s_[:, 8:9], k.bank(B0)[:, 0:1], m)
            m = k.mm(k.bank(B0 + 1)[0:1, 0:8], s_[:, 8:9], keyT[:, :], True, True, [a, t_ky], inc=True)
            s = s_[0:1, 16:24]
            a = k.copy(s, k.bank(B0 + 1)[0:1, 0:8], m)
            a2 = k.dve(lambda o=s_[0:1, 24:25], s=s: nc.vector.tensor_reduce(o, s, AX, ALU.max), [a])
            a2 = k.ts(s_[0:1, 25:26], s_[0:1, 24:25], -isq, None, ALU.mult, w=a2)
            a = k.af(s_[0:1, 32:40], s, ACT.Exp, [a, a2], scale=isq, bias=s_[0:1, 25:26])
            a2 = k.dve(lambda o=s_[0:1, 26:27], s=s_[0:1, 32:40]: nc.vector.tensor_reduce(o, s, AX, ALU.add), [a])
            a2 = k.dve(lambda o=s_[0:1, 27:28], s=s_[0:1, 26:27]: nc.vector.reciprocal(o, s), [a2])
            a = k.ts(s_[0:1, 40:48], s_[0:1, 32:40], s_[0:1, 27:28], None, ALU.mult, w=[a, a2])
            m = k.mm(k.bank(B0 + 2)[:, 0:8], k.ones[0:1, :], s_[0:1, 40:48], True, True, [a], inc=True)
            ce = k.bank(B0 + 2)[:, 0:8].rearrange("p (c e) -> p c e", e=2)
            coef.append([k.copy(s_[0:64, 48:52], ce[0:64, :, 0], m), k.copy(s_[64:128, 48:52], ce[64:128, :, 1], m)])
            if b == 0:
                u0 = [k.ts(upc[:, c, :], up[:, c, :], s_[:, 48 + c:49 + c], None, ALU.mult, w=[coef[0], t_up]) for c in range(4)]

        def chunk(b, i8, U, tu, wb, wor, out):
            def f():
                wi, wo, fr = wor.get()
                tw = p.dma(k.wl, wo[:, :], io["worgT"][128 * i8:128 * i8 + 128, :], fr)
                bi, bk, bf = wb.get()
                for q in range(2):
                    for c in range(4):
                        m = k.mm(k.bank(bk + q), dn[:, c, 128 * i8:128 * i8 + 128], U[:, c, 512 * q:512 * q + 512],
                                 c == 0, c == 3, [tu, t_dn, bf], inc=c == 3)
                a = k.tt(wo[:, :], wo[:, :], k.bank(bk, 2), ALU.add, [tw, m])
                wb.free(bi, a)
                r = k.split(W[b][0][:, i8, :], W[b][1][:, i8, :], wo[:, :], [a])
                wor.free(wi, r)
                out.append(r)
            return f

        t_w = [[], []]
        wb, wor = Ring([0, 2]), Ring([wob, yr.bufs[0], yr.bufs[1]])
        for q in range(2):
            wb.free(q, [u0, coef])
        for i8 in range(8):
            chunk(0, i8, upc, u0, wb, wor, t_w[0])()
        yr.busy = [wor.busy[1], wor.busy[2]]
        wb1, wor1 = Ring([2]), Ring([wob])
        wb1.free(0, wb.busy[1])
        wor1.free(0, wor.busy[0])
        u1 = [k.ts(up[:, c, :], up[:, c, :], sm[:, 1, 48 + c:49 + c], None, ALU.mult, w=[coef[1], u0]) for c in range(4)]
        trb, yb = Ring([0]), Ring([4, 6])
        trb.free(0, wb.busy[0])
        for q in range(2):
            yb.free(q, coef)
        k.carry["pp"] = (trb, yb)

        def widen():
            top.close()
            bar = [k.p.last(e) for e in ("pe", "dve", "act")]
            xth.bufs.append((sb("h1", [128, 8, 128], F32R), sb("l1", [128, 8, 128], F32R)))
            xth.busy, xth.i = [xth.busy[0], [bar]], 3
            assert yb.i % 2 == 0
            yb.bufs, yb.busy, yb.i = [4, 6, 2], [*yb.busy, [bar]], 3
        proj_pass(k, range(NT), xn_src, lambda t: k.done_xn[t], lambda t: (*W[t // 8], t_w[t // 8]), x_src, x_dst, None,
                  (inr, xth, xr, yr), extra=[chunk(1, i8, up, u1, wb1, wor1, t_w[1]) for i8 in range(8)] + [widen],
                  halved=lambda t: t > 8)


def program(nc, io, out):
    with ExitStack() as ctx:
        k = K(nc, ctx, io, out)
        k.carry = {}
        k.done_x, k.done_xn, k.t_sum = {}, {}, {}
        k.dctx = ctx.enter_context(ExitStack())
        x, xn = io["x"], None
        n = 0
        for s in STAGES:
            last = s == STAGES[-1]
            nx = out if last else k.scr[n]
            nn = None if last else k.scr[n + 1]
            n += 2
            old_x, old_xn = dict(k.done_x), dict(k.done_xn)
            for t in range(NT):
                k.done_x.setdefault(t, None)
                k.done_xn.setdefault(t, None)
            if s == "A":
                stage_a(k, x, nx, nn)
            elif s == "B":
                stage_b(k, x, xn, nx, nn)
            elif s == "C":
                stage_c(k, x, xn, k.ctxT, nx, nn)
            elif s == "D":
                stage_d(k, x, xn, nx)
            elif s == "L":
                prelude(k, x, nn)
                nx = x
            x, xn = nx, nn
            k.p.barrier()
        k.p.run(ctx.enter_context(nc.Block()))


def lay_out(i):
    f = np.float32
    g = {n: np.asarray(a) for n, a in i.items()}
    d = {}
    d["x"] = g["L0_attn_x"].reshape(2048, D)
    cst = np.zeros((128, 520), f)
    cst[:, 0:128] = np.eye(128)
    cst[:, 128:256] = np.eye(128) - 1.0 / 128
    cst[:, 256:384] = np.where(np.arange(128)[None, :] > np.arange(128)[:, None], -1.0e38, 0.0)
    cst[:, 384:512] = 1.0
    cst[:, 512] = 1.0 / 128
    d["cst"] = cst
    cols = [g["L0_attn_bin"][None]] + [g["L0_attn_" + n] for n in ("ln1_w", "ln1_b", "phz_re", "phz_im", "lc_re", "lc_im", "sc_lin", "ln2_w", "ln2_b")]
    cols += [g["L0_attn_b1"].reshape(16, 128), g["L0_attn_b2"], g["L0_attn_lnl_w"][None], g["L0_attn_lnl_b"][None]]
    d["vecs"] = np.concatenate(cols, 0).T
    d["winT"] = g["L0_attn_Win"].T
    d["w1T"] = g["L0_attn_W1"].transpose(0, 2, 1)
    d["w2T"] = g["L0_attn_W2"].transpose(0, 2, 1)
    d["woutT"] = g["L0_attn_Wout"].T
    d["bout"] = g["L0_attn_bout"]
    d["w13T"] = np.stack([g["L0_ffn_w1q"].T, g["L0_ffn_w3q"].T])
    bx = np.zeros((96, FH), f)
    for q in range(3):
        bx[32 * q:32 * q + 2] = g["L0_ffn_b1"].T
        bx[32 * q + 2:32 * q + 4] = g["L0_ffn_b3"].T
    d["bx"] = bx
    a13 = np.zeros((D, 32), f)
    a13[:, 0:2] = g["L0_ffn_a1"].T
    a13[:, 2:4] = g["L0_ffn_a3"].T
    d["a13T"] = a13
    a2 = np.zeros((FH, 32), f)
    a2[:, 0:2] = g["L0_ffn_a2"].T
    d["a2T"] = a2
    w2x = np.zeros((768, D), f)
    w2x[0:688] = g["L0_ffn_w2q"].T
    w2x[704:706] = g["L0_ffn_b2"].T
    d["w2x"] = w2x
    sel = np.zeros((128, 3, 96), f)
    for c in range(4):
        for q in range(3):
            for r in range(2):
                sel[32 * c + r, 0, 32 * q + r] = 0.5
                sel[32 * c + 2 + r, 1, 32 * q + 2 + r] = 0.5
        for r in range(2):
            sel[32 * c + r, 2, 64 + r] = 0.5
    d["sel"] = sel
    d["wq"] = g["L1_attn_Wq"]
    kv = g["L1_attn_Wkv"].reshape(D, 8, 2, 32)
    d["wk"] = kv[:, :, 0].reshape(D, 256)
    d["wv"] = kv[:, :, 1].reshape(D, 256)
    d["wo"] = g["L1_attn_Wo"]
    d["bo"] = g["L1_attn_bo"]
    d["worgT"] = g["L1_ffn_W_org"].T
    d["dnT"] = g["L1_ffn_lora_down"].transpose(0, 2, 1).reshape(512, D)
    d["up"] = g["L1_ffn_lora_up"].reshape(512, D)
    d["keyT"] = g["L1_ffn_lora_keys"].T
    d["lwqT"] = g["L1_ffn_Wq"].T
    return {n: np.ascontiguousarray(a) for n, a in d.items()}


def kernel(**inputs):
    import concourse.bacc as bacc
    from concourse.bass_utils import run_bass_kernel_spmd as run

    nc = bacc.Bacc("TRN2", target_bir_lowering=False, num_devices=1, dynamic_dma_scratch_size=1024)
    arrays = lay_out(inputs)
    io = {n: nc.dram_tensor("in_" + n, a.shape, mybir.dt.from_np(a.dtype), kind="ExternalInput").ap()
          for n, a in arrays.items()}
    out = nc.dram_tensor("out_0", (2048, D), F32, kind="ExternalOutput").ap()
    program(nc, io, out)
    r = run(nc, [{"in_" + n: a for n, a in arrays.items()}], core_ids=[0])
    return r.results[0]["out_0"].reshape(2, 1024, D)
```
